# Optimizing a Trainium2 kernel written in Bass

```python
import numpy as np
import jax
import jax.numpy as jnp

def _softmax(x, axis=-1):
    return jax.nn.softmax(x, axis=axis)

def _gelu(x):
    return jax.nn.gelu(x, approximate=True)

def _silu(x):
    return jax.nn.silu(x)

def _sigmoid(x):
    return jax.nn.sigmoid(x)

def _layernorm(x, axis=-1, eps=1e-05):
    m = jnp.mean(x, axis=axis, keepdims=True)
    v = jnp.var(x, axis=axis, keepdims=True)
    return (x - m) / jnp.sqrt(v + eps)

def _scatter_add(tgt, idx, src, axis=0):
    return tgt.at[idx].add(src)

def _segment_sum(src, seg, n):
    return jax.ops.segment_sum(src, seg, n)
kernel_name = 'mk_gnn_resnorm_d2_gnn_r8_c309c5'

def setup_inputs(seed: int=0):
    np.random.seed(seed)
    _w = jnp.asarray

    def _rec_inputs():
        import jax
        import jax.numpy as jnp
        _gk = jax.random.key(seed)
        x = -0.0002117 + 1 * jax.random.normal(jax.random.fold_in(_gk, 1), (1250, 512), jnp.float32)
        src = jax.random.randint(jax.random.fold_in(_gk, 2), (40000,), 0, 1250, jnp.int32)
        dst = jax.random.randint(jax.random.fold_in(_gk, 3), (40000,), 0, 1250, jnp.int32)
        _o = jnp.argsort(dst, stable=True)
        src = src[_o]
        dst = dst[_o]
        node_vec1 = jax.random.uniform(jax.random.fold_in(_gk, 12), (1250, 1), jnp.float32, 0.0, 0.999957)
        return (x, src, dst, node_vec1)
    x, src, dst, node_vec1 = _rec_inputs()

    def _L0_gnn_setup():
        import jax, jax.numpy as jnp
        import numpy as np
        N_NODES = 6250
        N_EDGES = 18750
        D_IN = 512
        D_OUT = 512
        LN_EPS = 1e-05
        key = jax.random.key(seed)
        k_x, k_e, k_ws, k_wn = jax.random.split(key, 4)
        x = jax.random.normal(k_x, (N_NODES, D_IN), dtype=jnp.float32)
        edge_index = jax.random.randint(k_e, (2, N_EDGES), 0, N_NODES, dtype=jnp.int64)
        scale = 1.0 / np.sqrt(D_IN)
        w_self = jax.random.normal(k_ws, (D_OUT, D_IN), dtype=jnp.float32) * scale
        w_neigh = jax.random.normal(k_wn, (D_OUT, D_IN), dtype=jnp.float32) * scale
        bias = jnp.zeros((D_OUT,), dtype=jnp.float32)
        gamma = jnp.ones((D_OUT,), dtype=jnp.float32)
        beta = jnp.zeros((D_OUT,), dtype=jnp.float32)
        return {'x': x, 'edge_index': edge_index, 'w_self': w_self, 'w_neigh': w_neigh, 'bias': bias, 'gamma': gamma, 'beta': beta}
    _L0_gnn_all = _L0_gnn_setup()
    _L0_gnn_in = {k: v for k, v in _L0_gnn_all.items() if k in ('w_self', 'w_neigh', 'bias', 'gamma', 'beta')}
    del _L0_gnn_all

    def _L1_gnn_setup():
        import jax, jax.numpy as jnp
        import numpy as np
        N_NODES = 40962
        LATENT_DIM = 512
        N_EDGES = 81924
        NUM_BLOCKS = 4
        NUM_HEADS = 4
        NUM_FREQ = 32
        BASE_PERIOD = 16
        NOISE_EMB_DIM = 16
        EPS = 1e-05

        def _cond_layer_norm(x, cond, sw, sb, bw, bb):
            mu = jnp.mean(x, axis=-1, keepdims=True)
            var = jnp.var(x, axis=-1, keepdims=True)
            xn = (x - mu) * jax.lax.rsqrt(var + EPS)
            scale = cond @ sw + sb
            bias = cond @ bw + bb
            return xn * (1.0 + scale) + bias

        def _sparse_attention(x, src, dst, wq, bq, wk, bk, wv, bv, wo, bo):
            N, D = x.shape
            H, Dh = (NUM_HEADS, D // NUM_HEADS)
            q = (x @ wq + bq).reshape(N, H, Dh) * Dh ** (-0.5)
            k = (x @ wk + bk).reshape(N, H, Dh)
            v = (x @ wv + bv).reshape(N, H, Dh)
            scores = jnp.einsum('ehd,ehd->eh', q[src], k[dst])
            smax = jax.ops.segment_max(scores, src, num_segments=N)
            ex = jnp.exp(scores - smax[src])
            denom = jax.ops.segment_sum(ex, src, num_segments=N)
            attn = ex / denom[src]
            out = jax.ops.segment_sum(attn[:, :, None] * v[dst], src, num_segments=N)
            return out.reshape(N, D) @ wo + bo

        def _forward(x, edge_index, noise_levels, f_w1, f_b1, f_w2, f_b2, s1_w, s1_b, b1_w, b1_b, wq, bq, wk, bk, wv, bv, wo, bo, s2_w, s2_b, b2_w, b2_b, m_w1, m_b1, m_w2, m_b2):
            src, dst = (edge_index[0], edge_index[1])
            freqs = jnp.arange(1, NUM_FREQ + 1, dtype=x.dtype) * (2.0 * np.pi / BASE_PERIOD)
            ph = noise_levels * freqs
            emb = jnp.concatenate([jnp.sin(ph), jnp.cos(ph)], axis=-1)
            cond = jax.nn.silu(emb @ f_w1 + f_b1) @ f_w2 + f_b2
            for i in range(NUM_BLOCKS):
                y = _cond_layer_norm(x, cond, s1_w[i], s1_b[i], b1_w[i], b1_b[i])
                y = _sparse_attention(y, src, dst, wq[i], bq[i], wk[i], bk[i], wv[i], bv[i], wo[i], bo[i])
                x = x + y
                y = _cond_layer_norm(x, cond, s2_w[i], s2_b[i], b2_w[i], b2_b[i])
                y = jax.nn.relu(y @ m_w1[i] + m_b1[i]) @ m_w2[i] + m_b2[i]
                x = x + y
            return x
        key = jax.random.key(seed)
        ks = jax.random.split(key, 20)

        def w(k, shape, s=0.02):
            return jax.random.normal(k, shape, dtype=jnp.float32) * s
        D, B, C = (LATENT_DIM, NUM_BLOCKS, NOISE_EMB_DIM)
        z = lambda *s: jnp.zeros(s, jnp.float32)
        return {'latent_mesh_nodes': jax.random.normal(ks[0], (N_NODES, D), dtype=jnp.float32), 'edge_index': jax.random.randint(ks[1], (2, N_EDGES), 0, N_NODES, dtype=jnp.int32), 'noise_levels': jax.random.uniform(ks[2], (N_NODES, 1), dtype=jnp.float32), 'f_w1': w(ks[3], (2 * NUM_FREQ, C)), 'f_b1': z(C), 'f_w2': w(ks[4], (C, C)), 'f_b2': z(C), 's1_w': w(ks[5], (B, C, D)), 's1_b': z(B, D), 'b1_w': w(ks[6], (B, C, D)), 'b1_b': z(B, D), 'wq': w(ks[7], (B, D, D)), 'bq': z(B, D), 'wk': w(ks[8], (B, D, D)), 'bk': z(B, D), 'wv': w(ks[9], (B, D, D)), 'bv': z(B, D), 'wo': w(ks[10], (B, D, D)), 'bo': z(B, D), 's2_w': w(ks[11], (B, C, D)), 's2_b': z(B, D), 'b2_w': w(ks[12], (B, C, D)), 'b2_b': z(B, D), 'm_w1': w(ks[13], (B, D, D)), 'm_b1': z(B, D), 'm_w2': w(ks[14], (B, D, D)), 'm_b2': z(B, D)}
    _L1_gnn_all = _L1_gnn_setup()
    _L1_gnn_in = {k: v for k, v in _L1_gnn_all.items() if k in ('f_w1', 'f_b1', 'f_w2', 'f_b2', 's1_w', 's1_b', 'b1_w', 'b1_b', 'wq', 'bq', 'wk', 'bk', 'wv', 'bv', 'wo', 'bo', 's2_w', 's2_b', 'b2_w', 'b2_b', 'm_w1', 'm_b1', 'm_w2', 'm_b2')}
    del _L1_gnn_all
    return {'x': x, 'src': src, 'dst': dst, 'node_vec1': node_vec1, 'L0_gnn_w_self': _L0_gnn_in['w_self'], 'L0_gnn_w_neigh': _L0_gnn_in['w_neigh'], 'L0_gnn_bias': _L0_gnn_in['bias'], 'L0_gnn_gamma': _L0_gnn_in['gamma'], 'L0_gnn_beta': _L0_gnn_in['beta'], 'L1_gnn_f_w1': _L1_gnn_in['f_w1'], 'L1_gnn_f_b1': _L1_gnn_in['f_b1'], 'L1_gnn_f_w2': _L1_gnn_in['f_w2'], 'L1_gnn_f_b2': _L1_gnn_in['f_b2'], 'L1_gnn_s1_w': _L1_gnn_in['s1_w'], 'L1_gnn_s1_b': _L1_gnn_in['s1_b'], 'L1_gnn_b1_w': _L1_gnn_in['b1_w'], 'L1_gnn_b1_b': _L1_gnn_in['b1_b'], 'L1_gnn_wq': _L1_gnn_in['wq'], 'L1_gnn_bq': _L1_gnn_in['bq'], 'L1_gnn_wk': _L1_gnn_in['wk'], 'L1_gnn_bk': _L1_gnn_in['bk'], 'L1_gnn_wv': _L1_gnn_in['wv'], 'L1_gnn_bv': _L1_gnn_in['bv'], 'L1_gnn_wo': _L1_gnn_in['wo'], 'L1_gnn_bo': _L1_gnn_in['bo'], 'L1_gnn_s2_w': _L1_gnn_in['s2_w'], 'L1_gnn_s2_b': _L1_gnn_in['s2_b'], 'L1_gnn_b2_w': _L1_gnn_in['b2_w'], 'L1_gnn_b2_b': _L1_gnn_in['b2_b'], 'L1_gnn_m_w1': _L1_gnn_in['m_w1'], 'L1_gnn_m_b1': _L1_gnn_in['m_b1'], 'L1_gnn_m_w2': _L1_gnn_in['m_w2'], 'L1_gnn_m_b2': _L1_gnn_in['m_b2']}

def reference(x, src, dst, node_vec1, L0_gnn_w_self, L0_gnn_w_neigh, L0_gnn_bias, L0_gnn_gamma, L0_gnn_beta, L1_gnn_f_w1, L1_gnn_f_b1, L1_gnn_f_w2, L1_gnn_f_b2, L1_gnn_s1_w, L1_gnn_s1_b, L1_gnn_b1_w, L1_gnn_b1_b, L1_gnn_wq, L1_gnn_bq, L1_gnn_wk, L1_gnn_bk, L1_gnn_wv, L1_gnn_bv, L1_gnn_wo, L1_gnn_bo, L1_gnn_s2_w, L1_gnn_s2_b, L1_gnn_b2_w, L1_gnn_b2_b, L1_gnn_m_w1, L1_gnn_m_b1, L1_gnn_m_w2, L1_gnn_m_b2):
    import jax
    import jax.numpy as jnp

    def _L0_gnn_ref(x, edge_index, w_self, w_neigh, bias, gamma, beta):
        import jax, jax.numpy as jnp
        import numpy as np
        N_NODES = 6250
        N_EDGES = 18750
        D_IN = 512
        D_OUT = 512
        LN_EPS = 1e-05
        n = x.shape[0]
        s, d = (edge_index[0], edge_index[1])
        agg = jax.ops.segment_sum(x[s], d, num_segments=n)
        cnt = jax.ops.segment_sum(jnp.ones(s.shape[0], x.dtype), d, num_segments=n)
        agg = agg / jnp.maximum(cnt, 1.0)[:, None]
        h = x @ w_self.T + agg @ w_neigh.T + bias
        mu = jnp.mean(h, axis=-1, keepdims=True)
        var = jnp.mean(jnp.square(h - mu), axis=-1, keepdims=True)
        hn = (h - mu) * jax.lax.rsqrt(var + LN_EPS) * gamma + beta
        return jax.nn.relu(hn)

    def _L1_gnn_ref(latent_mesh_nodes, edge_index, noise_levels, f_w1, f_b1, f_w2, f_b2, s1_w, s1_b, b1_w, b1_b, wq, bq, wk, bk, wv, bv, wo, bo, s2_w, s2_b, b2_w, b2_b, m_w1, m_b1, m_w2, m_b2):
        import jax, jax.numpy as jnp
        import numpy as np
        N_NODES = 40962
        LATENT_DIM = 512
        N_EDGES = 81924
        NUM_BLOCKS = 4
        NUM_HEADS = 4
        NUM_FREQ = 32
        BASE_PERIOD = 16
        NOISE_EMB_DIM = 16
        EPS = 1e-05

        def _cond_layer_norm(x, cond, sw, sb, bw, bb):
            mu = jnp.mean(x, axis=-1, keepdims=True)
            var = jnp.var(x, axis=-1, keepdims=True)
            xn = (x - mu) * jax.lax.rsqrt(var + EPS)
            scale = cond @ sw + sb
            bias = cond @ bw + bb
            return xn * (1.0 + scale) + bias

        def _sparse_attention(x, src, dst, wq, bq, wk, bk, wv, bv, wo, bo):
            N, D = x.shape
            H, Dh = (NUM_HEADS, D // NUM_HEADS)
            q = (x @ wq + bq).reshape(N, H, Dh) * Dh ** (-0.5)
            k = (x @ wk + bk).reshape(N, H, Dh)
            v = (x @ wv + bv).reshape(N, H, Dh)
            scores = jnp.einsum('ehd,ehd->eh', q[src], k[dst])
            smax = jax.ops.segment_max(scores, src, num_segments=N)
            ex = jnp.exp(scores - smax[src])
            denom = jax.ops.segment_sum(ex, src, num_segments=N)
            attn = ex / denom[src]
            out = jax.ops.segment_sum(attn[:, :, None] * v[dst], src, num_segments=N)
            return out.reshape(N, D) @ wo + bo

        def _forward(x, edge_index, noise_levels, f_w1, f_b1, f_w2, f_b2, s1_w, s1_b, b1_w, b1_b, wq, bq, wk, bk, wv, bv, wo, bo, s2_w, s2_b, b2_w, b2_b, m_w1, m_b1, m_w2, m_b2):
            src, dst = (edge_index[0], edge_index[1])
            freqs = jnp.arange(1, NUM_FREQ + 1, dtype=x.dtype) * (2.0 * np.pi / BASE_PERIOD)
            ph = noise_levels * freqs
            emb = jnp.concatenate([jnp.sin(ph), jnp.cos(ph)], axis=-1)
            cond = jax.nn.silu(emb @ f_w1 + f_b1) @ f_w2 + f_b2
            for i in range(NUM_BLOCKS):
                y = _cond_layer_norm(x, cond, s1_w[i], s1_b[i], b1_w[i], b1_b[i])
                y = _sparse_attention(y, src, dst, wq[i], bq[i], wk[i], bk[i], wv[i], bv[i], wo[i], bo[i])
                x = x + y
                y = _cond_layer_norm(x, cond, s2_w[i], s2_b[i], b2_w[i], b2_b[i])
                y = jax.nn.relu(y @ m_w1[i] + m_b1[i]) @ m_w2[i] + m_b2[i]
                x = x + y
            return x
        return _forward(latent_mesh_nodes, edge_index, noise_levels, f_w1, f_b1, f_w2, f_b2, s1_w, s1_b, b1_w, b1_b, wq, bq, wk, bk, wv, bv, wo, bo, s2_w, s2_b, b2_w, b2_b, m_w1, m_b1, m_w2, m_b2)
    edge_index = jnp.stack([src, dst])
    x = _layernorm(x + _L0_gnn_ref(x, edge_index, L0_gnn_w_self, L0_gnn_w_neigh, L0_gnn_bias, L0_gnn_gamma, L0_gnn_beta), axis=-1)
    x = _layernorm(x + _L1_gnn_ref(x, edge_index, node_vec1, L1_gnn_f_w1, L1_gnn_f_b1, L1_gnn_f_w2, L1_gnn_f_b2, L1_gnn_s1_w, L1_gnn_s1_b, L1_gnn_b1_w, L1_gnn_b1_b, L1_gnn_wq, L1_gnn_bq, L1_gnn_wk, L1_gnn_bk, L1_gnn_wv, L1_gnn_bv, L1_gnn_wo, L1_gnn_bo, L1_gnn_s2_w, L1_gnn_s2_b, L1_gnn_b2_w, L1_gnn_b2_b, L1_gnn_m_w1, L1_gnn_m_b1, L1_gnn_m_w2, L1_gnn_m_b2), axis=-1)
    return x

_drawn_inputs = setup_inputs


def setup_inputs(seed=0):
    import zlib

    import numpy as np

    out = dict(_drawn_inputs(seed))
    spreads = {'L0_gnn_bias': (0.0, 0.1),
     'L0_gnn_gamma': (1.0, 0.2),
     'L0_gnn_beta': (0.0, 0.1),
     'L1_gnn_f_b1': (0.0, 0.8),
     'L1_gnn_f_b2': (0.0, 0.8),
     'L1_gnn_s1_b': (0.0, 0.8),
     'L1_gnn_b1_b': (0.0, 0.384),
     'L1_gnn_bq': (0.0, 0.8),
     'L1_gnn_bk': (0.0, 0.8),
     'L1_gnn_bv': (0.0, 0.1),
     'L1_gnn_bo': (0.0, 0.1),
     'L1_gnn_s2_b': (0.0, 0.551),
     'L1_gnn_b2_b': (0.0, 0.561),
     'L1_gnn_m_b1': (0.0, 0.1),
     'L1_gnn_m_b2': (0.0, 0.1)}
    factors = {'node_vec1': 8.0,
     'L1_gnn_f_w1': 8.0,
     'L1_gnn_f_w2': 8.0,
     'L1_gnn_s1_w': 8.0,
     'L1_gnn_b1_w': 8.0,
     'L1_gnn_wq': 7.51,
     'L1_gnn_wk': 7.33,
     'L1_gnn_s2_w': 8.0,
     'L1_gnn_b2_w': 8.0}
    for name, (base, spread) in spreads.items():
        noise = np.random.default_rng([zlib.crc32(name.encode()), seed]).standard_normal(out[name].shape)
        drawn = base * np.exp(spread * noise) if base else spread * noise
        out[name] = jnp.asarray(drawn.astype(out[name].dtype))
    for name, factor in factors.items():
        out[name] = (out[name] * factor).astype(out[name].dtype)
    return out
```

```python
import concourse.bass as bass
from concourse import mybir
from contextlib import ExitStack

F32 = mybir.dt.float32
F16 = mybir.dt.float16
I32 = mybir.dt.int32
ALU = mybir.AluOpType
ACT = mybir.ActivationFunctionType
AX = mybir.AxisListType

P = 128
N = 1250
NT = (N + P - 1) // P
TAIL = N - (NT - 1) * P
NPAD = NT * P
D = 512
KD = D // P
E = 40000
NCH = (E + P - 1) // P
NPAIR = (NCH + 1) // 2
NG = (NCH + P - 1) // P
B = 4
H = 4
FREQ = 32
CE = 16
EPS = 1e-5
WS = 32.0
MAGIC = 1.5 * 2.0 ** 23
NOEDGE = -1e34
KAPPA = WS * WS * float(P) ** 0.5
COLS = [(0, 512), (512, 1024), (1024, N)]
COLS_PAD = [(0, 512), (512, 1024), (1024, NPAD)]

C_FREQ, C_PHASE, C_ONE, C_TLO, C_THI, C_LOWER = 0, 1, 2, 3, 4, 5
N_CONST = C_LOWER + NT


def rows(t):
    return TAIL if t == NT - 1 else P


def split_matmuls(pe, out, stationary, moving, start=True, stop=True):
    n = len(stationary)
    for k in range(n):
        (ah, al), (bh, bl) = stationary[k], moving[k]
        pe.matmul(out, ah, bh, start=start and k == 0, stop=False)
        pe.matmul(out, ah, bl, start=False, stop=False)
        last = pe.matmul(out, al, bh, start=False, stop=stop and k == n - 1)
    return last


def graph_layer(nc, io, keep):
    ctx = ExitStack()
    with ctx:
        def sb(name, shape, dt):
            return ctx.enter_context(nc.sbuf_tensor(name, shape, dt))

        def ps(name, n):
            return ctx.enter_context(nc.psum_tensor(name, [P, n], F32))

        def sem(name):
            return ctx.enter_context(nc.semaphore(name))

        x, edges, cond, ident, mhalf = keep.x, keep.edges, keep.cond, keep.ident, keep.mhalf
        const = keep.const

        iota = sb("iota", [P, N], F16)
        ids_raw = sb("ids_raw", [P, 2, NG, P], I32)
        ids_row = sb("ids_row", [P, 2, NG, P], F32)
        ids = sb("ids", [P, 2, NG * P], F32)
        span = sb("span", [P, 2, NG], F32)
        span10 = sb("span10", [P, 2, NG, NT], F32)
        spanT = sb("spanT", [NT, 2, NPAIR * 2], F32)
        pair_no = sb("pair_no", [NT, NPAIR * 2], F32)
        inside = sb("inside", [NT, NPAIR * 2], F32)
        lohi = sb("lohi", [NT, 8], F32)
        ranges_f = sb("ranges_f", [1, 4, NT], F32)
        ranges = sb("ranges", [1, 4, NT], I32)
        zeros = sb("zeros", [P, 512], F16)
        oh_src = sb("oh_src", [P, 2, N], F16)
        oh_dst = sb("oh_dst", [P, 2, P], F16)
        c_rows = sb("c_rows", [P, NPAD], F32)
        c_hi = sb("c_hi", [P, NT, P], F16)
        c_lo = sb("c_lo", [P, NT, P], F16)
        x_hi = sb("x_hi", [P, NT, D], F16)
        x_lo = sb("x_lo", [P, NT, D], F16)
        xT_hi = sb("xT_hi", [P, KD, NPAD], F16)
        xT_lo = sb("xT_lo", [P, KD, NPAD], F16)
        stage = sb("stage", [P, KD * N], F32)
        w_hi = sb("w_hi", [P, 2, KD, D], F16)
        w_lo = sb("w_lo", [P, 2, KD, D], F16)
        mean = sb("mean", [P, D], F32)
        mT_hi = sb("mT_hi", [P, KD, P], F16)
        mT_lo = sb("mT_lo", [P, KD, P], F16)
        degree = sb("degree", [P, 2], F32)
        vecs = sb("vecs", [P, 3, D], F32)
        h = sb("h", [P, D], F32)
        hn = sb("hn", [P, D], F32)
        bn = sb("bn", [P, 2, 6], F32)
        mv = sb("mv", [P, 2, 2], F32)
        rstd = sb("rstd", [P, 2, 4], F32)
        noise = sb("noise", [2 * FREQ, NPAD], F32)
        turns = sb("turns", [2 * FREQ, NPAD], F32)
        f1 = sb("f1", [2 * FREQ, CE], F32)
        fb1 = sb("fb1", [CE, 1], F32)
        f2 = sb("f2", [CE, P], F32)
        fb2 = sb("fb2", [P, 1], F32)

        bank = [ps(f"a_bank{i}", 512) for i in range(2)]
        p_cnt = ps("p_cnt", 3 * 512)
        p_t = ps("p_t", 3 * 512)

        ld_const, ld_ids, ld_noise, ld_f, ld_x, ld_xT, ld_w, ld_vec = (
            sem(n) for n in ("ld_const", "ld_ids", "ld_noise", "ld_f", "ld_x", "ld_xT", "ld_w", "ld_vec"))
        pad_rows = sem("pad_rows")
        padded = sem("padded")
        dv = sem("a_dv")
        rows_ready, ids_T, ids_ready, span_ready, span_T, lohi_ready, lohi_T, ranges_ready = (
            sem(n) for n in ("rows_ready", "ids_T", "ids_ready", "span_ready", "span_T", "lohi_ready",
                             "lohi_T", "ranges_ready"))
        angle_ready, emb_ready, f1_done, z_ready, e_ready, silu_ready, f2_done = (
            sem(n) for n in ("angle_ready", "emb_ready", "f1_done", "z_ready", "e_ready", "silu_ready", "f2_done"))
        ac = sem("a_ac")
        split_done = sem("split_done")
        stage_free = sem("stage_free")
        onehots, counted = sem("onehots"), sem("counted")
        cnt_done, rows_copied = sem("cnt_done"), sem("rows_copied")
        c_T, c_hi_done, c_lo_done = sem("c_T"), sem("c_hi_done"), sem("c_lo_done")
        agg_done, mean_done, m_T, mT_hi_done, mT_lo_done = (
            sem(n) for n in ("agg_done", "mean_done", "m_T", "mT_hi_done", "mT_lo_done"))
        h_done, h_free = sem("h_done"), sem("h_free")
        deg_done, bn0_done, bn1_done, sum_done = (sem(n) for n in ("deg_done", "bn0_done", "bn1_done", "sum_done"))
        stat0, rstd0, norm0, affine0, stat1, rstd1, x1_done = (
            sem(n) for n in ("stat0", "rstd0", "norm0", "affine0", "stat1", "rstd1", "x1_done"))
        gp = sem("a_gp")

        block = ctx.enter_context(nc.Block())

        @block.sync
        def _(sp):
            sp.wait_ge(padded, 5)
            for i, ids_in in enumerate((io["src"], io["dst"])):
                whole = (NG - 1) * P * P
                sp.dma_start(ids_raw[:, i, 0:NG - 1, :],
                             ids_in[0:whole].rearrange("(g c e) -> c g e", g=NG - 1, e=P)).then_inc(ld_ids, 16)
                full = (E - whole) // P
                sp.dma_start(ids_raw[0:full, i, NG - 1, :],
                             ids_in[whole:whole + full * P].rearrange("(c e) -> c e", e=P)).then_inc(ld_ids, 16)
                rest = E - whole - full * P
                sp.dma_start(ids_raw[full:full + 1, i, NG - 1, 0:rest],
                             ids_in[E - rest:E].rearrange("(c e) -> c e", c=1)).then_inc(ld_ids, 16)
                if i == 1:
                    sp.dma_start(ids_raw[full:full + 1, i, NG - 1, rest:P],
                                 ids_in[E - (P - rest):E].rearrange("(c e) -> c e", c=1)).then_inc(ld_ids, 16)
            sp.dma_start(f1[:], io["f_w1"]).then_inc(ld_f, 16)
            sp.dma_start(fb1[:], io["f_b1"].rearrange("(p a) -> p a", a=1)).then_inc(ld_f, 16)
            for q in range(4):
                sp.dma_start(f2[:, 32 * q:32 * q + CE], io["f_w2"]).then_inc(ld_f, 16)
                sp.dma_start(fb2[32 * q:32 * q + CE, :], io["f_b2"].rearrange("(p a) -> p a", a=1)).then_inc(ld_f, 16)
            sp.dma_start(x[:, 0:NT - 1, :], io["x"][0:(NT - 1) * P, :].rearrange("(t p) d -> p t d", p=P)).then_inc(ld_x, 16)
            sp.dma_start(x[0:TAIL, NT - 1, :], io["x"][(NT - 1) * P:N, :]).then_inc(ld_x, 16)
            for i, w in enumerate((io["w_self_T"], io["w_neigh_T"])):
                sp.wait_ge(stage_free, i + 1)
                sp.dma_start(stage[:, 0:KD * D].rearrange("p (k d) -> p k d", k=KD),
                             w.rearrange("(k p) d -> p k d", p=P)).then_inc(ld_w, 16)

        @block.gpsimd
        def _(pool):
            pool.memset(ids_raw[:], -1).then_inc(padded, 1)
            pool.memset(noise[:, N:NPAD], 0.0).then_inc(padded, 1)
            pool.memset(f2[:], 0.0).then_inc(padded, 1)
            pool.memset(fb2[:], 0.0).then_inc(padded, 1)
            pool.memset(x[:, NT - 1, :], 0.0).then_inc(padded, 1)
            pool.memset(zeros[:], 0.0).then_inc(padded, 1)
            pool.memset(xT_hi[:, :, N:NPAD], 0.0).then_inc(padded, 1)
            pool.memset(xT_lo[:, :, N:NPAD], 0.0).then_inc(padded, 1)
            pool.memset(mhalf[:], -0.5).then_inc(gp, 1)

            pool.wait_ge(gp, 1)
            pool.wait_ge(ld_vec, 48)
            for t in range(NT):
                for i, (stat, done) in enumerate(((stat0, rstd0), (stat1, rstd1))):
                    pool.wait_ge(stat, t + 1)
                    pool.tensor_scalar(rstd[:, i, 0:1], mv[:, i, 1:2], EPS, None, ALU.add).then_inc(gp, 1)
                    pool.wait_ge(gp, 2 + 5 * t + 2 * i + (i == 1))
                    pool.tensor_tensor(rstd[:, i, 1:2], rstd[:, i, 0:1], mhalf[:, 0:1], ALU.pow).then_inc(gp, 1)
                    pool.wait_ge(gp, 3 + 5 * t + 2 * i + (i == 1))
                    pool.tensor_scalar(rstd[:, i, 2:3], mv[:, i, 0:1], rstd[:, i, 1:2], -1.0, ALU.mult,
                                       ALU.mult).then_inc(done, 1)
                    if i == 0:
                        pool.wait_ge(norm0, t + 1)
                        pool.tensor_tensor(hn[:], hn[:], vecs[:, 1, :], ALU.mult).then_inc(gp, 1)
                        pool.wait_ge(gp, 4 + 5 * t)
                        pool.tensor_tensor(hn[:], hn[:], vecs[:, 2, :], ALU.add).then_inc(affine0, 1)

        @block.scalar
        def _(act):
            act.dma_start(const[:], io["const"]).then_inc(ld_const, 16)
            act.dma_start(ident[:], io["ident"]).then_inc(ld_const, 16)
            act.dma_start(iota[:], io["iota"].partition_broadcast(P)).then_inc(ld_const, 16)
            act.dma_start(pair_no[:], io["pair_no"].partition_broadcast(NT)).then_inc(ld_const, 16)
            act.wait_ge(padded, 2)
            act.dma_start(noise[:, 0:N], io["noise"].partition_broadcast(2 * FREQ)).then_inc(ld_noise, 16)
            act.dma_start(stage[:].rearrange("p (k n) -> p k n", k=KD),
                          io["xT"].rearrange("(k p) n -> p k n", p=P)).then_inc(ld_xT, 16)
            for i, v in enumerate((io["bias"], io["gamma"], io["beta"])):
                act.dma_start(vecs[:, i, :], v.partition_broadcast(P)).then_inc(ld_vec, 16)

            act.wait_ge(angle_ready, 1)
            act.activation(noise[:], turns[:], ACT.Sin, scale=6.283185307179586).then_inc(emb_ready, 1)
            act.wait_ge(z_ready, 1)
            act.activation(turns[0:CE, :], noise[0:CE, :], ACT.Exp, scale=-1.0).then_inc(e_ready, 1)

            act.wait_ge(ld_xT, 16)
            act.wait_ge(padded, 8)
            act.activation(xT_hi[:, :, 0:N], stage[:].rearrange("p (k n) -> p k n", k=KD), ACT.Copy).then_inc(ac, 1)
            for i in range(2):
                act.wait_ge(ld_w, 16 * (i + 1))
                act.activation(w_hi[:, i], stage[:, 0:KD * D].rearrange("p (k d) -> p k d", k=KD), ACT.Copy,
                               scale=WS).then_inc(ac, 1)
            act.wait_ge(ld_x, 32)
            act.activation(x_hi[:], x[:], ACT.Copy).then_inc(ac, 1)

            act.wait_ge(pad_rows, 1)

            def tile(t):
                act.wait_ge(cnt_done, t + 1)
                act.activation(c_rows[:, 0:N], p_cnt[:, 0:N], ACT.Identity,
                               accum_out=degree[:, 0:1]).then_inc(rows_copied, 1)
                act.wait_ge(c_T, t + 1)
                last = isinstance(t, int) and t == NT - 1
                w = TAIL if last else P
                act.activation(edges[:, :, bass.ds(t * P, w)],
                               p_t[:, 0:NPAD].rearrange("p (s c) -> p s c", c=P)[:, :, 0:w], ACT.Copy)
                act.activation(c_hi[:], p_t[:, 0:NPAD].rearrange("p (s c) -> p s c", c=P), ACT.Copy).then_inc(c_hi_done, 1)
                act.wait_ge(m_T, t + 1)
                act.activation(mT_hi[:], p_t[:, 0:D].rearrange("p (k c) -> p k c", k=KD), ACT.Copy).then_inc(mT_hi_done, 1)
                act.wait_ge(rstd0, t + 1)
                if not isinstance(t, int) or t:
                    act.wait_ge(x1_done, t)
                act.activation(hn[:], h[:], ACT.Identity, bias=rstd[:, 0, 2:3], scale=rstd[:, 0, 1:2]).then_inc(norm0, 1)

            def finish(t):
                act.wait_ge(rstd1, t + 1)
                act.activation(x[:, bass.ds(t, 1), :], hn[:].unsqueeze(1), ACT.Identity, bias=rstd[:, 1, 2:3],
                               scale=rstd[:, 1, 1:2]).then_inc(x1_done, 1)

            tile(0)
            with act.Fori(1, NT - 1) as t:
                finish(t - 1)
                tile(t)
            finish(NT - 2)
            tile(NT - 1)
            finish(NT - 1)

        @block.vector
        def _(dve):
            chain = [0]

            def link(ins):
                chain[0] += 1
                ins.then_inc(dv, 1)
                dve.wait_ge(dv, chain[0])

            dve.wait_ge(ld_ids, 16 * 7)
            dve.tensor_copy(ids_row[:], ids_raw[:]).then_inc(rows_ready, 1)
            dve.wait_ge(rows_ready, 1)
            link(dve.tensor_reduce(span[:, 0, :], ids_row[:, 1], AX.X, ALU.min))
            link(dve.tensor_reduce(span[:, 1, :], ids_row[:, 1], AX.X, ALU.max))
            for i in range(2):
                for g in range(NG):
                    last = dve.tensor_copy(span10[:, i, g, :], span[:, i, g:g + 1].to_broadcast([P, NT]))
            last.then_inc(span_ready, 1)
            for i in range(2):
                dve.wait_ge(ids_T, i + 1)
                last = dve.tensor_copy(ids[:, i, :], bank[i][:, 0:NG * P])
                last.then_inc(ids_ready, 1)
            dve.wait_ge(ld_const, 64)
            dve.wait_ge(span_T, 2)
            for i in range(2):
                link(dve.tensor_copy(spanT[:, i, :], bank[i][0:NT, 0:NPAIR * 2]))
            link(dve.tensor_scalar(inside[:], spanT[:, 1, :], const[0:NT, C_TLO:C_TLO + 1], None, ALU.is_ge))
            link(dve.scalar_tensor_tensor(spanT[:, 0, :], spanT[:, 0, :], const[0:NT, C_THI:C_THI + 1], inside[:],
                                          ALU.is_lt, ALU.mult))
            link(dve.scalar_tensor_tensor(spanT[:, 1, :], pair_no[:], 1.0, spanT[:, 0, :], ALU.add, ALU.mult))
            link(dve.tensor_scalar(inside[:], pair_no[:], 1000.0, None, ALU.add))
            link(dve.scalar_tensor_tensor(inside[:], spanT[:, 0, :], -1000.0, inside[:], ALU.mult, ALU.add))
            link(dve.tensor_reduce(lohi[:, 0:1], inside[:], AX.X, ALU.min))
            link(dve.tensor_reduce(lohi[:, 1:2], spanT[:, 1, :], AX.X, ALU.max))
            link(dve.tensor_scalar(lohi[:, 1:2], lohi[:, 1:2], 1.0, None, ALU.max))
            link(dve.tensor_scalar(lohi[:, 3:4], lohi[:, 1:2], -1.0, None, ALU.add))
            link(dve.tensor_tensor(lohi[:, 0:1], lohi[:, 0:1], lohi[:, 3:4], ALU.min))
            dve.tensor_tensor(lohi[:, 2:3], lohi[:, 1:2], lohi[:, 0:1], ALU.subtract).then_inc(lohi_ready, 1)
            dve.wait_ge(lohi_T, 1)
            link(dve.tensor_copy(ranges_f[:, 0:3, :], bank[0][0:1, 0:3 * NT].rearrange("p (a t) -> p a t", a=3)))
            link(dve.tensor_tensor(ranges_f[:, 3, :], ranges_f[:, 2, :], ranges_f[:, 0, :], ALU.subtract))
            dve.tensor_copy(ranges[:], ranges_f[:]).then_inc(ranges_ready, 1)

            nf = 2 * FREQ
            dve.wait_ge(ld_noise, 16)
            link(dve.tensor_scalar(turns[:], noise[:], const[0:nf, C_FREQ:C_FREQ + 1], None, ALU.mult))
            link(dve.tensor_scalar(noise[:], turns[:], MAGIC, MAGIC, ALU.add, ALU.subtract))
            link(dve.tensor_tensor(turns[:], turns[:], noise[:], ALU.subtract))
            link(dve.tensor_scalar(turns[:], turns[:], const[0:nf, C_PHASE:C_PHASE + 1], None, ALU.add))
            link(dve.tensor_scalar(noise[:], turns[:], MAGIC, MAGIC, ALU.add, ALU.subtract))
            link(dve.tensor_tensor(turns[:], turns[:], noise[:], ALU.subtract))
            half = 0.49999994
            dve.tensor_scalar(turns[:], turns[:], half, -half, ALU.min, ALU.max).then_inc(angle_ready, 1)
            dve.wait_ge(ld_f, 160)
            dve.wait_ge(f1_done, 1)
            dve.tensor_scalar(noise[0:CE, :], p_t[0:CE, 0:NPAD], fb1[:, 0:1], None, ALU.add).then_inc(z_ready, 1)
            dve.wait_ge(e_ready, 1)
            link(dve.tensor_scalar(turns[0:CE, :], turns[0:CE, :], 1.0, None, ALU.add))
            link(dve.reciprocal(turns[0:CE, :], turns[0:CE, :]))
            dve.tensor_tensor(turns[0:CE, :], turns[0:CE, :], noise[0:CE, :], ALU.mult).then_inc(silu_ready, 1)
            link(dve.tensor_tensor(fb2[:], fb2[:], const[:, C_ONE:C_ONE + 1], ALU.add))
            dve.wait_ge(f2_done, 1)
            link(dve.tensor_scalar(c_rows[:, 0:NPAD], p_cnt[:, 0:NPAD], fb2[:, 0:1], None, ALU.add))
            link(dve.tensor_copy(cond[:], c_rows[:, 0:NPAD]))
            for q in (1, 3):
                r = slice(32 * q, 32 * q + 32)
                link(dve.tensor_tensor(cond[r, :], c_rows[r, 0:NPAD], cond[r, :], ALU.subtract))
            dve.memset(c_rows[:, N:NPAD], 0.0).then_inc(pad_rows, 1)

            dve.wait_ge(ac, 1)
            dve.tensor_tensor(xT_lo[:, :, 0:N], stage[:].rearrange("p (k n) -> p k n", k=KD), xT_hi[:, :, 0:N],
                              ALU.subtract).then_inc(stage_free, 1)
            for i in range(2):
                dve.wait_ge(ac, 2 + i)
                dve.scalar_tensor_tensor(w_lo[:, i], stage[:, 0:KD * D].rearrange("p (k d) -> p k d", k=KD), WS,
                                         w_hi[:, i], ALU.mult, ALU.subtract).then_inc(stage_free, 1)
            dve.wait_ge(ac, 4)
            dve.tensor_tensor(x_lo[:], x[:], x_hi[:], ALU.subtract).then_inc(split_done, 1)
            dve.wait_ge(ranges_ready, 1)

            def build_onehots(t):
                first = dve.value_load(ranges[0:1, 0, bass.ds(t, 1)], min_val=0, max_val=NPAIR - 1)
                end = dve.value_load(ranges[0:1, 1, bass.ds(t, 1)], min_val=1, max_val=NPAIR)
                before = dve.value_load(ranges[0:1, 3, bass.ds(t, 1)], min_val=0, max_val=NPAIR * NT)
                with dve.Fori(first, end) as i:
                    for slot in range(2):
                        dve.wait_ge(counted, (i + before) * 2 + (slot + 1))
                        dve.tensor_scalar(oh_src[:, slot, :], iota[:], ids[:, 0, bass.ds(i * 2 + slot, 1)], None,
                                          ALU.is_equal)
                        dve.tensor_scalar(oh_dst[:, slot, :], iota[:, 0:P], ids[:, 1, bass.ds(i * 2 + slot, 1)], None,
                                          ALU.is_equal).then_inc(onehots, 1)
                dve.wait_ge(onehots, (end + before) * 2)
                dve.tensor_scalar(ids[:, 1, :], ids[:, 1, :], float(P), None, ALU.subtract).then_inc(ids_ready, 1)

            def tile(t):
                dve.wait_ge(rows_copied, t + 1)
                dve.tensor_scalar(degree[:, 1:2], degree[:, 0:1], 1.0, None, ALU.max).then_inc(deg_done, 1)
                dve.wait_ge(deg_done, t * 2 + 1)
                dve.reciprocal(degree[:, 1:2], degree[:, 1:2]).then_inc(deg_done, 1)
                dve.wait_ge(c_hi_done, t + 1)
                dve.tensor_tensor(c_lo[:], p_t[:, 0:NPAD].rearrange("p (s c) -> p s c", c=P), c_hi[:],
                                  ALU.subtract).then_inc(c_lo_done, 1)
                dve.wait_ge(deg_done, t * 2 + 2)
                dve.wait_ge(agg_done, t + 1)
                dve.tensor_scalar(mean[:], bank[0][:], degree[:, 1:2], None, ALU.mult).then_inc(mean_done, 1)
                dve.wait_ge(mT_hi_done, t + 1)
                dve.tensor_tensor(mT_lo[:], p_t[:, 0:D].rearrange("p (k c) -> p k c", k=KD), mT_hi[:],
                                  ALU.subtract).then_inc(mT_lo_done, 1)
                dve.wait_ge(h_done, t + 1)
                dve.scalar_tensor_tensor(h[:], bank[1][:], 1.0 / WS, vecs[:, 0, :], ALU.mult, ALU.add).then_inc(h_free, 1)
                dve.wait_ge(h_free, t + 2)
                dve.bn_stats(bn[:, 0, :], h[:]).then_inc(bn0_done, 1)
                dve.wait_ge(ld_vec, 48)
                dve.wait_ge(bn0_done, t + 1)
                dve.bn_aggr(mv[:, 0, :], bn[:, 0, :]).then_inc(stat0, 1)

            def finish(t):
                dve.wait_ge(affine0, t + 1)
                dve.scalar_tensor_tensor(hn[:].unsqueeze(1), hn[:].unsqueeze(1), 0.0, x[:, bass.ds(t, 1), :], ALU.max,
                                         ALU.add).then_inc(sum_done, 1)
                dve.wait_ge(sum_done, t + 1)
                dve.bn_stats(bn[:, 1, :], hn[:]).then_inc(bn1_done, 1)
                dve.wait_ge(ld_vec, 48)
                dve.wait_ge(bn1_done, t + 1)
                dve.bn_aggr(mv[:, 1, :], bn[:, 1, :]).then_inc(stat1, 1)

            dve.wait_ge(ld_vec, 48)
            dve.wait_ge(padded, 8)
            dve.memset(degree[:], 0.0).then_inc(h_free, 1)
            dve.wait_ge(ids_ready, 2)
            build_onehots(0)
            dve.wait_ge(ids_ready, 3)
            tile(0)
            with dve.Fori(1, NT - 1) as t:
                build_onehots(t)
                finish(t - 1)
                dve.wait_ge(ids_ready, t + 3)
                dve.wait_ge(x1_done, t)
                tile(t)
            build_onehots(NT - 1)
            finish(NT - 2)
            dve.wait_ge(x1_done, NT - 1)
            tile(NT - 1)
            finish(NT - 1)

        @block.tensor
        def _(pe):
            pe.wait_ge(rows_ready, 1)
            pe.wait_ge(ld_const, 64)
            for i in range(2):
                for g in range(NG):
                    last = pe.transpose(bank[i][:, g * P:(g + 1) * P], ids_row[:, i, g, :], ident[:])
                last.then_inc(ids_T, 1)
            pe.wait_ge(span_ready, 1)
            pe.wait_ge(ids_ready, 2)
            for i in range(2):
                for g in range(NG):
                    last = pe.matmul(bank[i][0:NT, g * P:(g + 1) * P], span10[:, i, g, :], ident[:], start=True, stop=True)
                last.then_inc(span_T, 1)
            pe.wait_ge(lohi_ready, 1)
            for i in range(2):
                pe.matmul(bank[0][0:1, i * NT:(i + 1) * NT], lohi[:, i:i + 1], ident[0:NT, 0:NT], start=True, stop=True)
            pe.matmul(bank[0][0:1, 2 * NT:3 * NT], lohi[:, 2:3], const[0:NT, C_LOWER:C_LOWER + NT], start=True,
                      stop=True).then_inc(lohi_T, 1)
            pe.wait_ge(ld_f, 160)
            pe.wait_ge(emb_ready, 1)
            for a, b in COLS_PAD:
                last = pe.matmul(p_t[0:CE, a:b], f1[:], noise[:, a:b], start=True, stop=True)
            last.then_inc(f1_done, 1)
            pe.wait_ge(silu_ready, 1)
            for a, b in COLS_PAD:
                last = pe.matmul(p_cnt[:, a:b], f2[:], turns[0:CE, a:b], start=True, stop=True)
            last.then_inc(f2_done, 1)

            pe.wait_ge(ranges_ready, 1)
            pe.wait_ge(stage_free, 3)
            pe.wait_ge(split_done, 1)
            pe.wait_ge(padded, 8)
            pe.wait_ge(pad_rows, 1)

            def clear_counts(last=False):
                for j, (a, b) in enumerate(COLS):
                    m = pe.matmul(p_cnt[:, a:b], zeros[:, 0:P], zeros[:, 0:b - a], start=not last, stop=last)
                return m

            def tile(t):
                clear_counts()
                first = pe.value_load(ranges[0:1, 0, bass.ds(t, 1)], min_val=0, max_val=NPAIR - 1)
                end = pe.value_load(ranges[0:1, 1, bass.ds(t, 1)], min_val=1, max_val=NPAIR)
                before = pe.value_load(ranges[0:1, 3, bass.ds(t, 1)], min_val=0, max_val=NPAIR * NT)
                with pe.Fori(first, end) as i:
                    for slot in range(2):
                        pe.wait_ge(onehots, (i + before) * 2 + (slot + 1))
                        for a, b in COLS:
                            last = pe.matmul(p_cnt[:, a:b], oh_dst[:, slot, :], oh_src[:, slot, a:b], start=False, stop=False)
                        last.then_inc(counted, 1)
                clear_counts(last=True).then_inc(cnt_done, 1)
                pe.wait_ge(h_free, t + 1)
                for k in range(KD):
                    for j, (a, b) in enumerate(((xT_hi, w_hi), (xT_hi, w_lo), (xT_lo, w_hi))):
                        pe.matmul(bank[1][:], a[:, k, bass.ds(t * P, P)], b[:, 0, k, :], start=k == 0 and j == 0, stop=False)
                pe.wait_ge(rows_copied, t + 1)
                for s in range(NT):
                    last = pe.transpose(p_t[:, s * P:(s + 1) * P], c_rows[:, s * P:(s + 1) * P], ident[:])
                last.then_inc(c_T, 1)
                pe.wait_ge(c_lo_done, t + 1)
                split_matmuls(pe, bank[0][:], [(c_hi[0:rows(s), s, :], c_lo[0:rows(s), s, :]) for s in range(NT)],
                              [(x_hi[0:rows(s), s, :], x_lo[0:rows(s), s, :]) for s in range(NT)]).then_inc(agg_done, 1)
                pe.wait_ge(mean_done, t + 1)
                for k in range(KD):
                    last = pe.transpose(p_t[:, k * P:(k + 1) * P], mean[:, k * P:(k + 1) * P], ident[:])
                last.then_inc(m_T, 1)
                pe.wait_ge(mT_lo_done, t + 1)
                split_matmuls(pe, bank[1][:], [(mT_hi[:, k, :], mT_lo[:, k, :]) for k in range(KD)],
                              [(w_hi[:, 1, k, :], w_lo[:, 1, k, :]) for k in range(KD)], start=False).then_inc(h_done, 1)

            clear_counts().then_inc(counted, 1)
            clear_counts(last=True).then_inc(counted, 1)
            tile(0)
            with pe.Fori(1, NT - 1) as t:
                tile(t)
            tile(NT - 1)


def in_register(eng, count):
    return count if isinstance(count, int) else eng.compute_val(count)


STEPS = H * NT
GROUPS = (NT + 1) // 2
JOBS = H * 6 + NT
WIDTH = 2 * P
OS = 4.0
LOADS_FIRST = ["cond1", "q0", "q1", "k0", "k1", "bv", "o0", "o1", "v0", "v1"]
LOADS_STEP = {2: "m20", 4: "m21", 6: "m10", 8: "m11", 10: "cond2"}
LOADS_NEXT = {12: "cond1", 14: "bv", 32: "q0", 34: "q1", 36: "k0", 38: "k1"}
LOADS_MLP = ["o0", "o1", "v0", "v1"]


def block_loads(last):
    steps = dict(LOADS_STEP) if last else {**LOADS_STEP, **LOADS_NEXT}
    return [steps[n] for n in sorted(steps)] + ([] if last else LOADS_MLP)


LOADS = len(block_loads(False))


def mlp_sequence(last):
    norms = NT if last else 2 * NT
    seq = []

    def tick(k):
        for stage, i in (("stats", k), ("norm", k - 1), ("turn", k - 2)):
            if 0 <= i < norms:
                seq.append((stage, i))

    for k in range(6):
        tick(k)
    for j in range(KD):
        seq.append(("up", j))
        tick(6 + j)
    for t in range(4):
        seq.append(("down", t))
        tick(10 + t)
        if last:
            seq.append(("final", t))
    if not last:
        seq += [("load", "o0"), ("load", "o1")]
    seq += [("up", KD + j) for j in range(KD)]
    for t in range(4, 8):
        seq.append(("down", t))
        if last:
            seq.append(("final", t))
        else:
            tick(10 + t)
    seq += [("up", 2 * KD + j) for j in range(KD)]
    for t in range(8, NT):
        seq.append(("down", t))
        if last:
            seq.append(("final", t))
        else:
            tick(10 + t)
    if not last:
        tick(20)
        tick(21)
        seq += [("load", "v0"), ("load", "v1")]
    return seq


def values_at(n):
    if n < 3:
        return None
    h, r = divmod(n - 3, NT)
    g, part = divmod(r, 2)
    return (h * GROUPS + g, part) if h < H else None


def output_at(n):
    if n < 5 or n >= 5 + 2 * H * GROUPS:
        return None
    return divmod(n - 5, 2)


DRAIN = 5 + 2 * H * GROUPS


def job_list(h):
    jobs = [("k", c) for c in range(3)] + [("q", c) for c in range(3)]
    return jobs + ([("v", t) for t in range(NT)] if h == 0 else [])


def job_start(h):
    return 6 * h + (NT if h else 0)


def transformer(nc, io, keep):
    ctx = ExitStack()
    with ctx:
        def sb(name, shape, dt):
            return ctx.enter_context(nc.sbuf_tensor(name, shape, dt))

        def ps(name, n):
            return ctx.enter_context(nc.psum_tensor(name, [P, n], F32))

        def sem(name):
            return ctx.enter_context(nc.semaphore(name))

        x, edges, cond, ident, mhalf = keep.x, keep.edges, keep.cond, keep.ident, keep.mhalf

        w_q, w_k, w_v, w_o, w_2 = (sb(n, [P, 2, KD, D], F16) for n in ("w_q", "w_k", "w_v", "w_o", "w_2"))
        w_1 = w_v
        stage = sb("wstage", [P, 2 * D], F32)
        wc1 = sb("wc1", [P, 2, D], F16)
        wc2 = sb("wc2", [P, 2, D], F16)
        bv = sb("bv", [64, D], F16)
        ones = sb("ones", [64, P], F16)
        brow = sb("brow", [P, D], F32)
        bcols = sb("bcols", [P, B, 3 * KD], F32)
        bcol = sb("bcol", [P, 3 * KD], F32)
        yT = sb("yT", [P, 2, KD, N], F16)
        v = sb("v", [P, 2, NT, D], F16)
        qk = sb("qk", [P, 2, 2, N], F16)
        pr = sb("pr", [P, 2, NPAD], F32)
        pT = sb("pT", [P, 2, 2, NT * WIDTH], F16)
        oT = sb("oT", [P, 2, WIDTH], F16)
        small = sb("small", [P, 8, 4], F32)
        bn = sb("bn_b", [P, 2, 6], F32)
        mv = sb("mv_b", [P, 2, 2], F32)
        rstd = sb("rstd_b", [P, 2, 4], F32)
        xn = [pr[:, i, 0:D] for i in range(2)]
        yn = [pr[:, i, D:2 * D] for i in range(2)]
        pTv = [pT[:, :, i, :].rearrange("p a (t c) -> p a t c", t=NT) for i in range(2)]
        wide = pT[:].rearrange("p a b c -> p (a b c)").bitcast(F32)
        x_in = wide.rearrange("p (t d) -> p t d", t=NT)
        hid = qk[:].rearrange("p a b c -> p (a b c)").bitcast(F32)[:, 0:2 * 512].rearrange("p (a c) -> p a c", a=2)

        psA, psB, ps6, ps7 = ps("psA", 3 * 512), ps("psB", 3 * 512), ps("ps6", 512), ps("ps7", 512)
        norm_bank = [psA[:, 0:512], psA[:, 512:1024]]
        turn_bank = [psA[:, 1024:1536], psB[:, 0:512]]
        up_bank = [psB[:, 512:1024], psB[:, 1024:1536]]
        down_bank = [ps6[:], ps7[:]]

        setup = sem("setup")
        stage_in, stage_scaled, stage_hi, stage_lo = (sem(n) for n in ("stage_in", "stage_scaled", "stage_hi", "stage_lo"))
        brow_in, bcols_in, bcols_scaled, bcol_set = (sem(n) for n in ("brow_in", "bcols_in", "bcols_scaled", "bcol_set"))
        x_saved, x_back, stored = sem("x_saved"), sem("x_back"), sem("stored")
        mask_part, max_part, log_part, edge_scores = (sem(n) for n in ("mask_part", "max_part", "log_part", "edge_scores"))
        bn_done, stats_done, rstd_done, xn_done, scale_done, yn_done, turned, yT_hi, yT_lo = (
            sem(n) for n in ("bn_done", "stats_done", "rstd_done", "xn_done", "scale_done", "yn_done", "turned",
                             "yT_hi", "yT_lo"))
        job_done, job_hi, job_lo = sem("job_done"), sem("job_hi"), sem("job_lo")
        scores_done, masked, exp_done, inv_done, out_scaled = (
            sem(n) for n in ("scores_done", "masked", "exp_done", "inv_done", "out_scaled"))
        pT_done, pT_hi, pT_lo = sem("pT_done"), sem("pT_hi"), sem("pT_lo")
        values_done, oT_hi, oT_lo, out_done, out_added, bo_added = (
            sem(n) for n in ("values_done", "oT_hi", "oT_lo", "out_done", "out_added", "bo_added"))
        up_done, relu_done, hid_hi, hid_lo, down_done, down_added, b2_added = (
            sem(n) for n in ("up_done", "relu_done", "hid_hi", "hid_lo", "down_done", "down_added", "b2_added"))
        final_sum, final_bn, final_stats, final_rstd, final_done = (
            sem(n) for n in ("final_sum", "final_bn", "final_stats", "final_rstd", "final_done"))
        pool_step = sem("pool_step")

        def halves_of(name):
            if name in ("cond1", "cond2"):
                w = (wc1 if name == "cond1" else wc2)[:].rearrange("p a d -> p (a d)")
                return stage[:], w, stage[64:P, :], w[64:P, :], w[64:P, :]
            if name == "bv":
                return stage[0:64, 0:D], bv[:], stage[32:64, 0:D], bv[32:64, :], bv[32:64, :]
            w = {"q": w_q, "k": w_k, "v": w_v, "o": w_o, "m1": w_1, "m2": w_2}[name[:-1]]
            c = 2 * int(name[-1])
            raw = stage[:].rearrange("p (k d) -> p k d", k=2)
            return raw, w[:, 0, c:c + 2, :], raw, w[:, 0, c:c + 2, :], w[:, 1, c:c + 2, :]

        def loads_before(b):
            return b * LOADS + len(LOADS_FIRST)

        def norms_before(b):
            return b * (2 * NT) + NT

        block = ctx.enter_context(nc.Block())

        @block.sync
        def _(sp):
            def load(name, b, seq):
                if not isinstance(seq, int) or seq > 0:
                    sp.wait_ge(stage_lo, seq)
                if name in ("cond1", "cond2"):
                    w = (io["w_cond1"] if name == "cond1" else io["w_cond2"])[bass.ds(b, 1)].rearrange("b r n -> (b r) n")
                    for q in range(4):
                        sp.dma_start(stage[32 * q:32 * q + CE + 1, :], w).then_inc(stage_in, 16)
                elif name == "bv":
                    for q in range(4):
                        r, c = 32 * (q % 2), (q // 2) * 256
                        sp.dma_start(stage[r:r + 1, c:c + 256], io["bv"][bass.ds(b, 1), c:c + 256]).then_inc(stage_in, 16)
                else:
                    w = {"q": io["wq"], "k": io["wk"], "v": io["wv"], "o": io["wo"], "m1": io["m_w1"], "m2": io["m_w2"]}[name[:-1]]
                    src = w[bass.ds(b, 1)].rearrange("b (k p) d -> p (b k) d", p=P)
                    for q in range(4):
                        k, c = 2 * int(name[-1]) + q // 2, (q % 2) * 256
                        sp.dma_start(stage[:, q * 256:(q + 1) * 256].unsqueeze(1), src[:, k:k + 1, c:c + 256]).then_inc(stage_in, 16)

            def load_row(w, b):
                sp.dma_start(brow[:], w[bass.ds(b, 1), :].rearrange("b d -> (b d)").partition_broadcast(P)).then_inc(brow_in, 16)

            sp.dma_start(io["x_scratch"].rearrange("(t p) d -> p t d", p=P), x[:]).then_inc(x_saved, 16)
            sp.dma_start(bcols[:], io["bias_cols"].rearrange("b p j -> p b j")).then_inc(bcols_in, 16)
            load_row(io["bo"], 0)
            sp.wait_ge(setup, 1)
            for i, name in enumerate(LOADS_FIRST):
                load(name, 0, i)

            def body(b, last):
                sp.wait_ge(bo_added, (b + 1) * NT)
                load_row(io["b2"], b)
                names = block_loads(last)
                for i, name in enumerate(names):
                    if not last and i == LOADS - len(LOADS_MLP):
                        sp.wait_ge(b2_added, (b + 1) * NT)
                        load_row(io["bo"], b + 1)
                    load(name, b if name in LOADS_STEP.values() else b + 1, loads_before(b) + i)

            with sp.Fori(0, B - 1) as b:
                body(b, False)
            body(B - 1, True)
            sp.wait_ge(values_done, B * H * GROUPS)
            sp.wait_ge(x_saved, 16)
            sp.dma_start(x_in, io["x_scratch"].rearrange("(t p) d -> p t d", p=P)).then_inc(x_back, 16)
            for t in range(NT):
                sp.wait_ge(final_done, t + 1)
                sp.dma_start(io["out"][t * P:t * P + rows(t), :], x_in[0:rows(t), t, :]).then_inc(stored, 16)
            sp.wait_ge(stored, 16 * NT)

        @block.gpsimd
        def _(pool):
            pool.memset(ones[:], 0.0).then_inc(pool_step, 1)
            pool.memset(stage[:], 0.0).then_inc(pool_step, 1)
            pool.memset(pr[:], 0.0).then_inc(pool_step, 1)
            pool.memset(small[:], 0.0).then_inc(pool_step, 1)
            pool.wait_ge(pool_step, 4)
            pool.memset(ones[0:1, :], WS).then_inc(pool_step, 1)
            pool.memset(ones[32:33, :], WS).then_inc(pool_step, 1)
            pool.wait_ge(pool_step, 6)
            pool.memset(rstd[:], 0.0).then_inc(setup, 1)

            def split(name, seq):
                raw, _, low_of, high, low = halves_of(name)
                scale = 1.0 if name[0:2] in ("co", "bv") else WS
                count = in_register(pool, seq * 64 + 64)
                pool.wait_ge(pool_step, 6)
                pool.wait_ge(stage_in, count)
                pool.tensor_scalar(raw, raw, scale, None, ALU.mult).then_inc(stage_scaled, 1)
                pool.wait_ge(stage_hi, seq + 1)
                pool.tensor_tensor(low, low_of, high, ALU.subtract).then_inc(stage_lo, 1)
                pool.wait_ge(stage_lo, seq + 1)

            def inverse(i, before, aggregated, count, done):
                count = in_register(pool, count)
                pool.wait_ge(pool_step, 6)
                pool.wait_ge(aggregated, count)
                pool.tensor_scalar(rstd[:, i, 0:1], mv[:, i, 1:2], EPS, None, ALU.add).then_inc(pool_step, 1)
                pool.wait_ge(pool_step, before * 2 + 7)
                pool.tensor_tensor(rstd[:, i, 1:2], rstd[:, i, 0:1], mhalf[:, 0:1], ALU.pow).then_inc(pool_step, 1)
                count = in_register(pool, before * 2 + 8)
                pool.wait_ge(pool_step, 6)
                pool.wait_ge(pool_step, count)
                pool.tensor_scalar(rstd[:, i, 2:3], mv[:, i, 0:1], rstd[:, i, 1:2], -1.0, ALU.mult, ALU.mult).then_inc(done, 1)

            split(LOADS_FIRST[0], 0)
            for i in range(NT):
                inverse(i % 2, i, stats_done, i + 1, rstd_done)
            for i in range(1, 5):
                split(LOADS_FIRST[i], i)
            for s in range(NT):
                if s >= 2:
                    pool.wait_ge(edge_scores, s - 1)
                pool.tensor_scalar(wide[:, (s % 2) * N:(s % 2) * N + N], edges[:, s, :], 0.5, NOEDGE, ALU.is_lt,
                                   ALU.mult).then_inc(mask_part, 1)
            for i in range(5, len(LOADS_FIRST)):
                split(LOADS_FIRST[i], i)
            pool.wait_ge(x_saved, 16)

            def body(b, last):
                pool.wait_ge(brow_in, b * 32 + 16)
                for t in range(NT):
                    pool.tensor_tensor(x[:, t, :], x[:, t, :], brow[:], ALU.add).then_inc(bo_added, 1)
                names = block_loads(last)
                i = len(names) - (0 if last else len(LOADS_MLP))
                for j in range(i):
                    split(names[j], loads_before(b) + j)
                pool.wait_ge(brow_in, b * 32 + 32)
                for kind, k in mlp_sequence(last):
                    if kind == "stats":
                        inverse(k % 2, norms_before(b) + k, stats_done, norms_before(b) + k + 1, rstd_done)
                    elif kind == "turn" and k < NT:
                        pool.wait_ge(xn_done, norms_before(b) + k + 1)
                        pool.tensor_tensor(x[:, k, :], x[:, k, :], brow[:], ALU.add).then_inc(b2_added, 1)
                    elif kind == "up":
                        c, j = divmod(k, KD)
                        w = COLS[c][1] - COLS[c][0]
                        pool.wait_ge(hid_hi, b * 3 * KD + k + 1)
                        slot = (c % 2) * KD + j
                        pool.tensor_tensor(v[:, 1, slot, 0:w], hid[:, k % 2, 0:w], v[:, 0, slot, 0:w],
                                           ALU.subtract).then_inc(hid_lo, 1)
                    elif kind == "load":
                        split(k, loads_before(b) + i)
                        i += 1
                    elif kind == "final":
                        if k >= 2:
                            pool.wait_ge(final_done, k - 1)
                        inverse(k % 2, norms_before(b) + NT + k, final_stats, k + 1, final_rstd)

            with pool.Fori(0, B - 1) as b:
                body(b, False)
            body(B - 1, True)

        @block.scalar
        def _(act):
            def split(name, seq):
                raw, high = halves_of(name)[0:2]
                act.wait_ge(stage_scaled, seq + 1)
                act.activation(high, raw, ACT.Copy).then_inc(stage_hi, 1)

            def norm(i, before):
                t = i % NT
                act.wait_ge(rstd_done, before + i + 1)
                act.activation(xn[i % 2], x[:, t, :], ACT.Identity, bias=rstd[:, i % 2, 2:3],
                               scale=rstd[:, i % 2, 1:2]).then_inc(xn_done, 1)

            def turn(i, before):
                t = i % NT
                r = rows(t)
                act.wait_ge(turned, before + i + 1)
                act.activation(yT[:, 0, :, t * P:t * P + r],
                               turn_bank[i % 2].rearrange("p (k c) -> p k c", k=KD)[:, :, 0:r], ACT.Copy).then_inc(yT_hi, 1)

            split(LOADS_FIRST[0], 0)
            for k in range(NT + 1):
                if k < NT:
                    norm(k, 0)
                if k >= 1:
                    turn(k - 1, 0)
            for i in range(1, 5):
                split(LOADS_FIRST[i], i)
            for s in range(NT):
                act.wait_ge(max_part, s + 1)
                act.activation(edges[:, s, :], edges[:, s, :], ACT.Ln).then_inc(log_part, 1)
            for i in range(5, len(LOADS_FIRST)):
                split(LOADS_FIRST[i], i)

            def project(b, h):
                for i, (kind, c) in enumerate(job_list(h)):
                    act.wait_ge(job_done, b * JOBS + job_start(h) + i + 1)
                    slot = psA[:, (i % 3) * 512:(i % 3 + 1) * 512]
                    if kind == "v":
                        r = rows(c)
                        act.activation(v[0:r, 0, c, :], slot[0:r, :], ACT.Copy).then_inc(job_hi, 1)
                    else:
                        which = int(kind == "k")
                        lo, hi = COLS[c]
                        act.wait_ge(bcol_set, b + 1)
                        act.activation(qk[:, which, 0, lo:hi], slot[:, 0:hi - lo], ACT.Identity,
                                       bias=bcol[:, which * KD + h:which * KD + h + 1]).then_inc(job_hi, 1)

            def exponential(b, n):
                r = rows(n % NT)
                act.wait_ge(masked, b * STEPS + n + 1)
                act.activation(pr[0:r, n % 2, 0:N], pr[0:r, n % 2, 0:N], ACT.Exp, bias=small[0:r, n % 8, 0:1], scale=-1.0,
                               accum_out=small[0:r, n % 8, 1:2]).then_inc(exp_done, 1)

            def transposed(b, n):
                s = n % NT
                G, r = n // 2, rows(s)
                if G >= 2:
                    act.wait_ge(values_done, b * H * GROUPS + G - 1)
                act.wait_ge(pT_done, b * STEPS + n + 1)
                act.activation(pTv[G % 2][:, 0, :, (s % 2) * P:(s % 2) * P + r],
                               psB[:, 0:NPAD].rearrange("p (t c) -> p t c", c=P)[:, :, 0:r], ACT.Copy).then_inc(pT_hi, 1)

            def values(b, n):
                G, part = values_at(n) or (0, 0)
                if part:
                    w = sum(rows(2 * (G % GROUPS) + i) for i in range(2))
                    if G:
                        act.wait_ge(out_done, b * STEPS + 2 * G)
                    act.wait_ge(values_done, b * H * GROUPS + G + 1)
                    act.activation(oT[:, 0, 0:w], ps6[:, 0:w], ACT.Copy, scale=1.0 / (WS * OS)).then_inc(oT_hi, 1)

            def body(b, last):
                names = block_loads(last)
                steps = LOADS_STEP if last else {**LOADS_STEP, **LOADS_NEXT}
                i = 0
                for n in range(DRAIN):
                    boundary = n % NT == 0 and n < STEPS
                    if boundary:
                        project(b, n // NT)
                    if 1 <= n <= STEPS:
                        transposed(b, n - 1)
                    if n < STEPS:
                        exponential(b, n)
                    values(b, n)
                    if n in steps:
                        split(names[i], loads_before(b) + i)
                        i += 1
                for kind, k in mlp_sequence(last):
                    if kind == "norm":
                        norm(k, norms_before(b))
                    elif kind == "turn":
                        turn(k, norms_before(b))
                    elif kind == "up":
                        c, j = divmod(k, KD)
                        w = COLS[c][1] - COLS[c][0]
                        if c == 2:
                            act.wait_ge(down_done, b * NT + 4)
                        act.wait_ge(relu_done, b * 3 * KD + k + 1)
                        act.activation(v[:, 0, (c % 2) * KD + j, 0:w], hid[:, k % 2, 0:w], ACT.Copy).then_inc(hid_hi, 1)
                    elif kind == "load":
                        split(k, loads_before(b) + i)
                        i += 1
                    elif kind == "final":
                        act.wait_ge(final_rstd, k + 1)
                        act.activation(x_in[:, k, :], x[:, k, :], ACT.Identity, bias=rstd[:, k % 2, 2:3],
                                       scale=rstd[:, k % 2, 1:2]).then_inc(final_done, 1)

            with act.Fori(0, B - 1) as b:
                body(b, False)
            body(B - 1, True)

        @block.vector
        def _(dve):
            def stats(i, before):
                dve.bn_stats(bn[:, i % 2, :], x[:, i % NT, :]).then_inc(bn_done, 1)
                count = in_register(dve, before + i + 1)
                dve.wait_ge(setup, 1)
                dve.wait_ge(bn_done, count)
                dve.bn_aggr(mv[:, i % 2, :], bn[:, i % 2, :]).then_inc(stats_done, 1)

            def norm(i, before):
                dve.wait_ge(xn_done, before + i + 1)
                dve.wait_ge(scale_done, before + i + 1)
                dve.scalar_tensor_tensor(yn[i % 2], norm_bank[i % 2], 1.0, xn[i % 2], ALU.add, ALU.mult).then_inc(yn_done, 1)

            def turn(i, before):
                t = i % NT
                r = rows(t)
                dve.wait_ge(yT_hi, before + i + 1)
                dve.tensor_tensor(yT[:, 1, :, t * P:t * P + r], turn_bank[i % 2].rearrange("p (k c) -> p k c", k=KD)[:, :, 0:r],
                                  yT[:, 0, :, t * P:t * P + r], ALU.subtract).then_inc(yT_lo, 1)

            dve.wait_ge(setup, 1)
            dve.wait_ge(bcols_in, 16)
            dve.tensor_scalar(bcols[:], bcols[:], WS, None, ALU.mult).then_inc(bcols_scaled, 1)
            dve.wait_ge(bcols_scaled, 1)
            dve.tensor_copy(bcol[:], bcols[:, 0, :]).then_inc(bcol_set, 1)
            for k in range(NT + 2):
                if k < NT:
                    stats(k, 0)
                if 1 <= k <= NT:
                    norm(k - 1, 0)
                if k >= 2:
                    turn(k - 2, 0)
            for s in range(NT + 1):
                if s < NT:
                    dve.wait_ge(mask_part, s + 1)
                    dve.tensor_scalar(edges[:, s, :], edges[:, s, :], 1.0, None, ALU.max).then_inc(max_part, 1)
                if s:
                    dve.wait_ge(log_part, s)
                    u = s - 1
                    dve.scalar_tensor_tensor(edges[:, u, :], edges[:, u, :], KAPPA, wide[:, (u % 2) * N:(u % 2) * N + N],
                                             ALU.mult, ALU.add).then_inc(edge_scores, 1)
            dve.wait_ge(edge_scores, NT)

            def project(b, h):
                for i, (kind, c) in enumerate(job_list(h)):
                    dve.wait_ge(job_hi, b * JOBS + job_start(h) + i + 1)
                    slot = psA[:, (i % 3) * 512:(i % 3 + 1) * 512]
                    if kind == "v":
                        r = rows(c)
                        dve.tensor_tensor(v[0:r, 1, c, :], slot[0:r, :], v[0:r, 0, c, :], ALU.subtract).then_inc(job_lo, 1)
                    else:
                        which = int(kind == "k")
                        lo, hi = COLS[c]
                        dve.scalar_tensor_tensor(qk[:, which, 1, lo:hi], slot[:, 0:hi - lo],
                                                 bcol[:, which * KD + h:which * KD + h + 1], qk[:, which, 0, lo:hi],
                                                 ALU.add, ALU.subtract).then_inc(job_lo, 1)

            def mask(b, n):
                s = n % NT
                r = rows(s)
                count = in_register(dve, b * STEPS + n + 1)
                dve.wait_ge(setup, 1)
                dve.wait_ge(scores_done, count)
                dve.tensor_tensor_reduce(out=pr[0:r, n % 2, 0:N], in0=psA[0:r, 0:N], in1=edges[0:r, s, :],
                                         scale=-1.0 / KAPPA, scalar=3e38, op0=ALU.add, op1=ALU.min,
                                         accum_out=small[0:r, n % 8, 0:1]).then_inc(masked, 1)

            def inverse(b, n):
                m = small[0:rows(n % NT), n % 8, :]
                dve.wait_ge(exp_done, b * STEPS + n + 1)
                dve.reciprocal(m[:, 2:3], m[:, 1:2])
                dve.tensor_scalar(m[:, 3:4], m[:, 0:1], -NOEDGE / KAPPA / 8, OS / WS, ALU.is_lt, ALU.mult).then_inc(inv_done, 1)

            def scale(b, n):
                m = small[0:rows(n % NT), n % 8, :]
                dve.wait_ge(inv_done, b * STEPS + n + 1)
                dve.tensor_tensor(m[:, 3:4], m[:, 3:4], m[:, 2:3], ALU.mult).then_inc(out_scaled, 1)

            def transposed(b, n):
                s = n % NT
                G, r = n // 2, rows(s)
                out = pTv[G % 2][:, :, :, (s % 2) * P:(s % 2) * P + r]
                dve.wait_ge(pT_hi, b * STEPS + n + 1)
                dve.tensor_tensor(out[:, 1], psB[:, 0:NPAD].rearrange("p (t c) -> p t c", c=P)[:, :, 0:r], out[:, 0],
                                  ALU.subtract).then_inc(pT_lo, 1)

            def values(b, n):
                G, part = values_at(n) or (0, 0)
                if part:
                    w = sum(rows(2 * (G % GROUPS) + i) for i in range(2))
                    dve.wait_ge(oT_hi, b * H * GROUPS + G + 1)
                    dve.scalar_tensor_tensor(oT[:, 1, 0:w], ps6[:, 0:w], 1.0 / (WS * OS), oT[:, 0, 0:w], ALU.mult, ALU.subtract).then_inc(oT_lo, 1)

            def output(b, n):
                if output_at(n) is None:
                    return
                G, i = output_at(n)
                t = 2 * (G % GROUPS) + i
                r = rows(t)
                if G < GROUPS:
                    dve.wait_ge(bo_added, b * NT + t + 1)
                dve.wait_ge(out_scaled, b * STEPS + 2 * G + i + 1)
                dve.wait_ge(out_done, b * STEPS + 2 * G + i + 1)
                dve.scalar_tensor_tensor(x[0:r, t, :], ps7[0:r, :], small[0:r, (2 * G + i) % 8, 3:4], x[0:r, t, :], ALU.mult,
                                         ALU.add).then_inc(out_added, 1)

            def body(b, last):
                for n in range(DRAIN):
                    boundary = n % NT == 0 and n < STEPS
                    if boundary:
                        project(b, n // NT)
                    elif n < STEPS:
                        mask(b, n)
                    if 2 <= n < STEPS + 2:
                        scale(b, n - 2)
                    if 1 <= n <= STEPS:
                        transposed(b, n - 1)
                        inverse(b, n - 1)
                    if boundary:
                        mask(b, n)
                    values(b, n)
                    output(b, n)
                for kind, k in mlp_sequence(last):
                    if kind == "load":
                        continue
                    t = k % NT
                    if kind == "stats":
                        if k < NT:
                            dve.wait_ge(out_added, b * STEPS + (H - 1) * NT + t + 1)
                        else:
                            dve.wait_ge(down_added, b * NT + t + 1)
                        stats(k, norms_before(b))
                    elif kind == "norm":
                        norm(k, norms_before(b))
                    elif kind == "turn":
                        turn(k, norms_before(b))
                    elif kind == "up":
                        c, j = divmod(k, KD)
                        w = COLS[c][1] - COLS[c][0]
                        if k >= 2:
                            dve.wait_ge(hid_lo, b * 3 * KD + k - 1)
                        dve.wait_ge(up_done, b * 3 * KD + k + 1)
                        dve.tensor_scalar(hid[:, k % 2, 0:w], up_bank[k % 2][:, 0:w], bcol[:, 2 * KD + j:2 * KD + j + 1], 0.0,
                                          ALU.add, ALU.max).then_inc(relu_done, 1)
                    elif kind == "down":
                        r = rows(t)
                        dve.wait_ge(b2_added, b * NT + t + 1)
                        dve.wait_ge(down_done, b * NT + t + 1)
                        dve.scalar_tensor_tensor(x[0:r, t, :], down_bank[t % 2][0:r, :], 1.0 / (WS * WS), x[0:r, t, :],
                                                 ALU.mult, ALU.add).then_inc(down_added, 1)
                    elif kind == "final":
                        if t == 0:
                            dve.wait_ge(x_back, 16)
                        if t >= 2:
                            dve.wait_ge(final_rstd, t - 1)
                        dve.wait_ge(down_added, b * NT + t + 1)
                        dve.tensor_tensor(x[:, t, :], x[:, t, :], x_in[:, t, :], ALU.add).then_inc(final_sum, 1)
                        dve.wait_ge(final_sum, t + 1)
                        dve.bn_stats(bn[:, t % 2, :], x[:, t, :]).then_inc(final_bn, 1)
                        dve.wait_ge(final_bn, t + 1)
                        dve.bn_aggr(mv[:, t % 2, :], bn[:, t % 2, :]).then_inc(final_stats, 1)
                if not last:
                    dve.wait_ge(setup, 1)
                    dve.wait_ge(relu_done, (b + 1) * 3 * KD)
                    dve.tensor_copy(bcol[:].unsqueeze(1), bcols[:, bass.ds(b + 1, 1), :]).then_inc(bcol_set, 1)

            with dve.Fori(0, B - 1) as b:
                body(b, False)
            body(B - 1, True)

        @block.tensor
        def _(pe):
            def norm(i, before, wc, wait=None):
                t = i % NT
                pe.matmul(norm_bank[i % 2], cond[:, t * P:(t + 1) * P], wc[:, 0, :], start=True, stop=True).then_inc(scale_done, 1)

            def turn(i, before, wc):
                t = i % NT
                r = rows(t)
                if not isinstance(before, int) or before + i >= 2:
                    pe.wait_ge(yT_lo, before + i - 1)
                pe.wait_ge(yn_done, before + i + 1)
                for k in range(KD):
                    out = turn_bank[i % 2][:, k * P:k * P + r]
                    pe.matmul(out, wc[:, 1, k * P:(k + 1) * P], cond[:, t * P:t * P + r], start=True, stop=False)
                    last = pe.matmul(out, yn[i % 2][0:r, k * P:(k + 1) * P], ident[0:r, 0:r], start=False, stop=True,
                                     is_transpose=True)
                last.then_inc(turned, 1)

            pe.wait_ge(stage_lo, 1)
            for k in range(NT + 1):
                if k < NT:
                    norm(k, 0, wc1)
                if k >= 1:
                    turn(k - 1, 0, wc1)

            def project(b, h):
                if h:
                    pe.wait_ge(masked, b * STEPS + h * NT)
                else:
                    pe.wait_ge(yT_lo, norms_before(b))
                    pe.wait_ge(stage_lo, loads_before(b) - 4)
                for i, (kind, c) in enumerate(job_list(h)):
                    if i >= 3:
                        pe.wait_ge(job_lo, b * JOBS + job_start(h) + i - 2)
                    slot = psA[:, (i % 3) * 512:(i % 3 + 1) * 512]
                    if kind == "v":
                        if c == 0:
                            pe.wait_ge(stage_lo, loads_before(b))
                        r = rows(c)
                        pe.matmul(slot[0:r, :], ones[:, 0:r], bv[:], start=True, stop=False)
                        last = split_matmuls(pe, slot[0:r, :],
                                             [(yT[:, 0, k, c * P:c * P + r], yT[:, 1, k, c * P:c * P + r]) for k in range(KD)],
                                             [(w_v[:, 0, k, :], w_v[:, 1, k, :]) for k in range(KD)], start=False)
                    else:
                        w = w_k if kind == "k" else w_q
                        lo, hi = COLS[c]
                        last = split_matmuls(pe, slot[:, 0:hi - lo],
                                             [(w[:, 0, k, h * P:(h + 1) * P], w[:, 1, k, h * P:(h + 1) * P]) for k in range(KD)],
                                             [(yT[:, 0, k, lo:hi], yT[:, 1, k, lo:hi]) for k in range(KD)])
                    last.then_inc(job_done, 1)

            def scores(b, n):
                s = n % NT
                r = rows(s)
                if s == 0:
                    pe.wait_ge(job_lo, b * JOBS + job_start(n // NT + 1))
                else:
                    pe.wait_ge(masked, b * STEPS + n)
                for part, (i, j) in enumerate(((0, 0), (0, 1), (1, 0))):
                    for lo, hi in COLS:
                        last = pe.matmul(psA[0:r, lo:hi], qk[:, 0, i, s * P:s * P + r], qk[:, 1, j, lo:hi],
                                         start=part == 0, stop=part == 2)
                last.then_inc(scores_done, 1)

            def values(b, n):
                if values_at(n) is None:
                    return
                G, part = values_at(n)
                h, g = divmod(G, GROUPS)
                w = sum(rows(2 * g + i) for i in range(2))
                if part == 0:
                    if G:
                        pe.wait_ge(oT_lo, b * H * GROUPS + G)
                    pe.wait_ge(pT_lo, b * STEPS + 2 * G + 2)
                half = NT // 2
                tiles = range(part * half, part * half + half)
                last = split_matmuls(pe, ps6[:, 0:w],
                                     [(v[0:rows(d), 0, d, h * P:(h + 1) * P], v[0:rows(d), 1, d, h * P:(h + 1) * P]) for d in tiles],
                                     [(pTv[G % 2][0:rows(d), 0, d, 0:w], pTv[G % 2][0:rows(d), 1, d, 0:w]) for d in tiles],
                                     start=part == 0, stop=part == 1)
                if part:
                    last.then_inc(values_done, 1)

            def transpose(b, n):
                r = rows(n % NT)
                if n:
                    pe.wait_ge(pT_lo, b * STEPS + n)
                pe.wait_ge(exp_done, b * STEPS + n + 1)
                for d in range(NT):
                    last = pe.transpose(psB[:, d * P:d * P + r], pr[0:r, n % 2, d * P:(d + 1) * P], ident[0:r, 0:r])
                last.then_inc(pT_done, 1)

            def output(b, n):
                if output_at(n) is None:
                    return
                G, i = output_at(n)
                h, g = divmod(G, GROUPS)
                r = rows(2 * g + i)
                if n > 5:
                    pe.wait_ge(out_added, b * STEPS + 2 * G + i)
                if i == 0:
                    pe.wait_ge(oT_lo, b * H * GROUPS + G + 1)
                split_matmuls(pe, ps7[0:r, :], [(oT[:, 0, i * P:i * P + r], oT[:, 1, i * P:i * P + r])],
                              [(w_o[:, 0, h, :], w_o[:, 1, h, :])]).then_inc(out_done, 1)

            def body(b, last):
                names = block_loads(last)
                for n in range(DRAIN):
                    boundary = n % NT == 0 and n < STEPS
                    if boundary:
                        project(b, n // NT)
                    elif n < STEPS:
                        scores(b, n)
                    if 1 <= n <= STEPS:
                        transpose(b, n - 1)
                    values(b, n)
                    if boundary:
                        scores(b, n)
                    output(b, n)
                pe.wait_ge(stage_lo, loads_before(b) + names.index("cond2") + 1)
                for kind, k in mlp_sequence(last):
                    if kind == "load":
                        continue
                    wc = wc2 if k < NT else wc1
                    if kind == "norm":
                        if k == NT:
                            pe.wait_ge(stage_lo, loads_before(b) + names.index("cond1") + 1)
                        norm(k, norms_before(b), wc)
                    elif kind == "turn":
                        turn(k, norms_before(b), wc)
                    elif kind == "up":
                        c, j = divmod(k, KD)
                        lo, hi = COLS[c]
                        if j == 0:
                            pe.wait_ge(yT_lo, norms_before(b) + min(4 * c + 4, NT))
                        if k >= 2:
                            pe.wait_ge(relu_done, b * 3 * KD + k - 1)
                        split_matmuls(pe, up_bank[k % 2][:, 0:hi - lo],
                                      [(w_1[:, 0, i, j * P:(j + 1) * P], w_1[:, 1, i, j * P:(j + 1) * P]) for i in range(KD)],
                                      [(yT[:, 0, i, lo:hi], yT[:, 1, i, lo:hi]) for i in range(KD)]).then_inc(up_done, 1)
                    elif kind == "down":
                        c, r = k // KD, rows(k)
                        if k >= 2:
                            pe.wait_ge(down_added, b * NT + k - 1)
                        if k % KD == 0:
                            pe.wait_ge(hid_lo, b * 3 * KD + (c + 1) * KD)
                        at = (k % KD) * P
                        split_matmuls(pe, down_bank[k % 2][0:r, :],
                                      [(v[:, 0, (c % 2) * KD + i, at:at + r], v[:, 1, (c % 2) * KD + i, at:at + r]) for i in range(KD)],
                                      [(w_2[:, 0, i, :], w_2[:, 1, i, :]) for i in range(KD)]).then_inc(down_done, 1)

            with pe.Fori(0, B - 1) as b:
                body(b, False)
            body(B - 1, True)


class Kept:
    pass


def kept(nc, ctx):
    k = Kept()

    def sb(name, shape, dt):
        return ctx.enter_context(nc.sbuf_tensor(name, shape, dt))

    k.x = sb("x", [P, NT, D], F32)
    k.edges = sb("edges", [P, NT, N], F32)
    k.cond = sb("cond", [P, NPAD], F16)
    k.ident = sb("ident", [P, P], F32)
    k.const = sb("const", [P, N_CONST], F32)
    k.mhalf = sb("mhalf", [P, 1], F32)
    return k


def build(nc, io):
    io["x_scratch"] = nc.dram_tensor("x_scratch", (NPAD, D), F32).ap()
    ctx = ExitStack()
    with ctx:
        keep = kept(nc, ctx)
        graph_layer(nc, io, keep)
        transformer(nc, io, keep)


def arrays(inputs):
    import numpy as np
    a = {k: np.ascontiguousarray(v) for k, v in inputs.items()}
    g, b = "L0_gnn_", "L1_gnn_"
    const = np.zeros((P, N_CONST), np.float32)
    const[0:2 * FREQ, C_FREQ] = np.tile(np.arange(1, FREQ + 1) / 16.0, 2)
    const[FREQ:2 * FREQ, C_PHASE] = 0.25
    const[CE::32, C_ONE] = 1.0
    const[:, C_TLO] = P * np.arange(P)
    const[:, C_THI] = P * np.arange(1, P + 1)
    const[0:NT, C_LOWER:C_LOWER + NT] = np.triu(np.ones((NT, NT)), 1)
    t = lambda v: np.ascontiguousarray(v.T)
    cols = lambda v: v.reshape(B, KD, P).transpose(0, 2, 1)

    def norm_weights(n):
        parts = [np.concatenate([a[b + f"{m}{n}_w"], a[b + f"{m}{n}_b"][:, None, :]], axis=1) for m in "sb"]
        return np.ascontiguousarray(np.concatenate(parts, axis=2))

    return {
        "x": a["x"], "xT": t(a["x"]), "src": a["src"], "dst": a["dst"], "noise": a["node_vec1"].reshape(N),
        "w_self_T": t(a[g + "w_self"]), "w_neigh_T": t(a[g + "w_neigh"]),
        "bias": a[g + "bias"], "gamma": a[g + "gamma"], "beta": a[g + "beta"],
        "f_w1": a[b + "f_w1"], "f_b1": a[b + "f_b1"], "f_w2": a[b + "f_w2"], "f_b2": a[b + "f_b2"],
        "const": const, "ident": np.eye(P, dtype=np.float32), "iota": np.arange(N).astype(np.float16),
        "pair_no": (np.arange(2 * NPAIR) // 2).astype(np.float32),
        "w_cond1": norm_weights("1"), "w_cond2": norm_weights("2"),
        "wq": a[b + "wq"], "wk": a[b + "wk"], "wv": a[b + "wv"], "wo": a[b + "wo"],
        "m_w1": a[b + "m_w1"], "m_w2": a[b + "m_w2"],
        "bias_cols": np.ascontiguousarray(np.concatenate([cols(a[b + n]) for n in ("bq", "bk", "m_b1")], axis=2)),
        "bv": a[b + "bv"], "bo": a[b + "bo"], "b2": a[b + "m_b2"],
    }


def kernel(**inputs):
    import numpy as np
    import concourse.bacc as bacc
    from concourse.bass_utils import run_bass_kernel_spmd

    nc = bacc.Bacc("TRN2", target_bir_lowering=False, num_devices=1)
    given = arrays({k: np.asarray(v) for k, v in inputs.items()})
    io = {
        k: nc.dram_tensor(f"in_{k}", v.shape, mybir.dt.from_np(v.dtype), kind="ExternalInput").ap()
        for k, v in given.items()}
    io["out"] = nc.dram_tensor("out", (N, D), F32, kind="ExternalOutput").ap()
    build(nc, io)
    r = run_bass_kernel_spmd(nc, [{f"in_{k}": v for k, v in given.items()}], core_ids=[0])
    return r.results[0]["out"]
```

```python
import concourse.bass as bass
from concourse import mybir
from contextlib import ExitStack

F32 = mybir.dt.float32
F16 = mybir.dt.float16
I32 = mybir.dt.int32
ALU = mybir.AluOpType
ACT = mybir.ActivationFunctionType
AX = mybir.AxisListType

P = 128
N = 1250
NT = (N + P - 1) // P
TAIL = N - (NT - 1) * P
NPAD = NT * P
D = 512
KD = D // P
E = 40000
NCH = (E + P - 1) // P
SLOTS = 4
NQUAD = (NCH + SLOTS - 1) // SLOTS
NSEG = 4
NG = (NCH + P - 1) // P
B = 4
H = 4
FREQ = 32
CE = 16
EPS = 1e-5
WS = 32.0
TINY = 1e-20
MAGIC = 1.5 * 2.0 ** 23
NOEDGE = -1e34
KAPPA = WS * WS * float(P) ** 0.5
COLS = [(0, 512), (512, 1024), (1024, N)]
COLS_PAD = [(0, 512), (512, 1024), (1024, NPAD)]

C_FREQ, C_PHASE, C_ONE, C_TLO, C_THI, C_LOWER = 0, 1, 2, 3, 4, 5
N_CONST = C_LOWER + NT


def rows(t):
    return TAIL if t == NT - 1 else P


def split_matmuls(pe, out, stationary, moving, start=True, stop=True):
    n = len(stationary)
    for k in range(n):
        (ah, al), (bh, bl) = stationary[k], moving[k]
        pe.matmul(out, ah, bh, start=start and k == 0, stop=False)
        pe.matmul(out, ah, bl, start=False, stop=False)
        last = pe.matmul(out, al, bh, start=False, stop=stop and k == n - 1)
    return last


def in_register(eng, count):
    return count if isinstance(count, int) else eng.compute_val(count)


def bounds_of(eng, ranges, t):
    def load(row, low, high):
        return eng.value_load(ranges[0:1, row, bass.ds(t, 1)], min_val=low, max_val=high)

    ends = [load(4 + k, k, NQUAD - NSEG + k) for k in range(1, NSEG)]
    return [load(0, 0, NQUAD - NSEG)] + ends + [load(1, NSEG, NQUAD)], load(4, 0, NQUAD * NT)


def graph_layer(nc, io, keep):
    ctx = ExitStack()
    with ctx:
        def sb(name, shape, dt):
            return ctx.enter_context(nc.sbuf_tensor(name, shape, dt))

        def ps(name, n):
            return ctx.enter_context(nc.psum_tensor(name, [P, n], F32))

        def sem(name):
            return ctx.enter_context(nc.semaphore(name))

        x, edges, cond, ident, mhalf = keep.x, keep.edges, keep.cond, keep.ident, keep.mhalf
        const = keep.const

        iota = sb("iota", [P, N], F16)
        ids_raw = sb("ids_raw", [P, 2, NG, P], I32)
        ids_row = sb("ids_row", [P, 2, NG, P], F32)
        ids = sb("ids", [P, 2, NG * P], F32)
        span = sb("span", [P, 2, NG], F32)
        span10 = sb("span10", [P, 2, NG, NT], F32)
        spanT = sb("spanT", [NT, 2, NQUAD * SLOTS], F32)
        quad_no = sb("quad_no", [NT, NQUAD * SLOTS], F32)
        inside = sb("inside", [NT, NQUAD * SLOTS], F32)
        lohi = sb("lohi", [NT, 8], F32)
        ranges_f = sb("ranges_f", [1, 4 + NSEG, NT], F32)
        ranges = sb("ranges", [1, 4 + NSEG, NT], I32)
        zeros = sb("zeros", [P, 512], F16)
        oh_src = sb("oh_src", [P, SLOTS, N], F16)
        oh_dst = sb("oh_dst", [P, SLOTS, P], F16)
        c_rows = sb("c_rows", [P, NPAD], F32)
        c_hi = sb("c_hi", [P, NT, P], F16)
        c_lo = sb("c_lo", [P, NT, P], F16)
        x_hi = sb("x_hi", [P, NT, D], F16)
        x_lo = sb("x_lo", [P, NT, D], F16)
        xT_hi = sb("xT_hi", [P, KD, NPAD], F16)
        xT_lo = sb("xT_lo", [P, KD, NPAD], F16)
        stage = sb("stage", [P, KD * N], F32)
        w_hi = sb("w_hi", [P, 2, KD, D], F16)
        w_lo = sb("w_lo", [P, 2, KD, D], F16)
        mean = sb("mean", [P, D], F32)
        mT_hi = sb("mT_hi", [P, KD, P], F16)
        mT_lo = sb("mT_lo", [P, KD, P], F16)
        degree = sb("degree", [P, 2], F32)
        vecs = sb("vecs", [P, 3, D], F32)
        h = sb("h", [P, D], F32)
        hn = sb("hn", [P, D], F32)
        bn = sb("bn", [P, 2, 6], F32)
        mv = sb("mv", [P, 2, 2], F32)
        rstd = sb("rstd", [P, 2, 4], F32)
        noise = sb("noise", [2 * FREQ, NPAD], F32)
        turns = c_rows[0:2 * FREQ, :]
        f1 = sb("f1", [2 * FREQ, CE], F32)
        fb1 = sb("fb1", [CE, 1], F32)
        f2 = sb("f2", [CE, P], F32)
        fb2 = sb("fb2", [P, 1], F32)

        tiny = sb("tiny", [P, 1], F32)
        no_edge = stage[:, 0:NT * P].rearrange("p (s c) -> p s c", c=P)

        bank = [ps(f"a_bank{i}", 512) for i in range(2)]
        p_cnt = ps("p_cnt", 3 * 512)
        p_t = ps("p_t", 3 * 512)

        ld_const, ld_ids, ld_noise, ld_f, ld_x, ld_xT, ld_w, ld_vec = (
            sem(n) for n in ("ld_const", "ld_ids", "ld_noise", "ld_f", "ld_x", "ld_xT", "ld_w", "ld_vec"))
        pad_rows = sem("pad_rows")
        padded = sem("padded")
        dv = sem("a_dv")
        rows_ready, ids_T, ids_ready, span_ready, span_T, lohi_ready, lohi_T, ranges_ready = (
            sem(n) for n in ("rows_ready", "ids_T", "ids_ready", "span_ready", "span_T", "lohi_ready",
                             "lohi_T", "ranges_ready"))
        angle_ready, emb_ready, f1_done, z_ready, e_ready, silu_ready, f2_done = (
            sem(n) for n in ("angle_ready", "emb_ready", "f1_done", "z_ready", "e_ready", "silu_ready", "f2_done"))
        ac = sem("a_ac")
        split_done = sem("split_done")
        stage_free = sem("stage_free")
        onehots, counted = sem("onehots"), sem("counted")
        cnt_done, rows_copied = sem("cnt_done"), sem("rows_copied")
        logs_done, no_edge_done, scores_set = sem("logs_done"), sem("no_edge_done"), sem("scores_set")
        c_T, c_hi_done, c_lo_done = sem("c_T"), sem("c_hi_done"), sem("c_lo_done")
        agg_done, mean_done, m_T, mT_hi_done, mT_lo_done = (
            sem(n) for n in ("agg_done", "mean_done", "m_T", "mT_hi_done", "mT_lo_done"))
        h_done, h_free = sem("h_done"), sem("h_free")
        deg_done, bn0_done, bn1_done, sum_done = (sem(n) for n in ("deg_done", "bn0_done", "bn1_done", "sum_done"))
        stat0, rstd0, norm0, affine0, stat1, rstd1, x1_done = (
            sem(n) for n in ("stat0", "rstd0", "norm0", "affine0", "stat1", "rstd1", "x1_done"))
        gp = sem("a_gp")

        block = ctx.enter_context(nc.Block())

        @block.sync
        def _(sp):
            sp.wait_ge(padded, 5)
            for i, ids_in in enumerate((io["src"], io["dst"])):
                whole = (NG - 1) * P * P
                sp.dma_start(ids_raw[:, i, 0:NG - 1, :],
                             ids_in[0:whole].rearrange("(g c e) -> c g e", g=NG - 1, e=P)).then_inc(ld_ids, 16)
                full = (E - whole) // P
                sp.dma_start(ids_raw[0:full, i, NG - 1, :],
                             ids_in[whole:whole + full * P].rearrange("(c e) -> c e", e=P)).then_inc(ld_ids, 16)
                rest = E - whole - full * P
                sp.dma_start(ids_raw[full:full + 1, i, NG - 1, 0:rest],
                             ids_in[E - rest:E].rearrange("(c e) -> c e", c=1)).then_inc(ld_ids, 16)
                if i == 1:
                    sp.dma_start(ids_raw[full:full + 1, i, NG - 1, rest:P],
                                 ids_in[E - (P - rest):E].rearrange("(c e) -> c e", c=1)).then_inc(ld_ids, 16)
            sp.dma_start(f1[:], io["f_w1"]).then_inc(ld_f, 16)
            sp.dma_start(fb1[:], io["f_b1"].rearrange("(p a) -> p a", a=1)).then_inc(ld_f, 16)
            for q in range(4):
                sp.dma_start(f2[:, 32 * q:32 * q + CE], io["f_w2"]).then_inc(ld_f, 16)
                sp.dma_start(fb2[32 * q:32 * q + CE, :], io["f_b2"].rearrange("(p a) -> p a", a=1)).then_inc(ld_f, 16)
            sp.dma_start(x[:, 0:NT - 1, :], io["x"][0:(NT - 1) * P, :].rearrange("(t p) d -> p t d", p=P)).then_inc(ld_x, 16)
            sp.dma_start(x[0:TAIL, NT - 1, :], io["x"][(NT - 1) * P:N, :]).then_inc(ld_x, 16)
            for i, w in enumerate((io["w_self_T"], io["w_neigh_T"])):
                sp.wait_ge(stage_free, i + 1)
                sp.dma_start(stage[:, 0:KD * D].rearrange("p (k d) -> p k d", k=KD),
                             w.rearrange("(k p) d -> p k d", p=P)).then_inc(ld_w, 16)

        @block.gpsimd
        def _(pool):
            pool.memset(ids_raw[:], -1).then_inc(padded, 1)
            pool.memset(noise[:, N:NPAD], 0.0).then_inc(padded, 1)
            pool.memset(f2[:], 0.0).then_inc(padded, 1)
            pool.memset(fb2[:], 0.0).then_inc(padded, 1)
            pool.memset(x[:, NT - 1, :], 0.0).then_inc(padded, 1)
            pool.memset(zeros[:], 0.0).then_inc(padded, 1)
            pool.memset(xT_hi[:, :, N:NPAD], 0.0).then_inc(padded, 1)
            pool.memset(xT_lo[:, :, N:NPAD], 0.0).then_inc(padded, 1)
            pool.memset(tiny[:], TINY).then_inc(padded, 1)
            pool.memset(mhalf[:], -0.5).then_inc(gp, 1)

            pool.wait_ge(ac, 1)
            pool.tensor_tensor(xT_lo[:, :, 0:N], stage[:].rearrange("p (k n) -> p k n", k=KD), xT_hi[:, :, 0:N],
                               ALU.subtract).then_inc(stage_free, 1)
            pool.wait_ge(ac, 2)
            pool.tensor_tensor(x_lo[:], x[:], x_hi[:], ALU.subtract).then_inc(split_done, 1)

            pool.wait_ge(gp, 1)
            pool.wait_ge(ld_vec, 48)
            for t in range(NT):
                for i, (stat, done) in enumerate(((stat0, rstd0), (stat1, rstd1))):
                    pool.wait_ge(stat, t + 1)
                    pool.tensor_scalar(rstd[:, i, 0:1], mv[:, i, 1:2], EPS, None, ALU.add).then_inc(gp, 1)
                    pool.wait_ge(gp, 2 + 5 * t + 2 * i + (i == 1))
                    pool.tensor_tensor(rstd[:, i, 1:2], rstd[:, i, 0:1], mhalf[:, 0:1], ALU.pow).then_inc(gp, 1)
                    pool.wait_ge(gp, 3 + 5 * t + 2 * i + (i == 1))
                    pool.tensor_scalar(rstd[:, i, 2:3], mv[:, i, 0:1], rstd[:, i, 1:2], -1.0, ALU.mult,
                                       ALU.mult).then_inc(done, 1)
                    if i == 0:
                        pool.wait_ge(norm0, t + 1)
                        pool.tensor_tensor(hn[:], hn[:], vecs[:, 1, :], ALU.mult).then_inc(gp, 1)
                        pool.wait_ge(gp, 4 + 5 * t)
                        pool.tensor_tensor(hn[:], hn[:], vecs[:, 2, :], ALU.add).then_inc(affine0, 1)

        @block.scalar
        def _(act):
            act.dma_start(const[:], io["const"]).then_inc(ld_const, 16)
            act.dma_start(ident[:], io["ident"]).then_inc(ld_const, 16)
            act.dma_start(iota[:], io["iota"].partition_broadcast(P)).then_inc(ld_const, 16)
            act.dma_start(quad_no[:], io["quad_no"].partition_broadcast(NT)).then_inc(ld_const, 16)
            act.wait_ge(padded, 2)
            act.dma_start(noise[:, 0:N], io["noise"].partition_broadcast(2 * FREQ)).then_inc(ld_noise, 16)
            act.dma_start(stage[:].rearrange("p (k n) -> p k n", k=KD),
                          io["xT"].rearrange("(k p) n -> p k n", p=P)).then_inc(ld_xT, 16)
            for i, v in enumerate((io["bias"], io["gamma"], io["beta"])):
                act.dma_start(vecs[:, i, :], v.partition_broadcast(P)).then_inc(ld_vec, 16)

            act.wait_ge(angle_ready, 1)
            act.activation(noise[:], turns[:], ACT.Sin, scale=6.283185307179586).then_inc(emb_ready, 1)
            act.wait_ge(ld_xT, 16)
            act.wait_ge(padded, 9)
            act.activation(xT_hi[:, :, 0:N], stage[:].rearrange("p (k n) -> p k n", k=KD), ACT.Copy).then_inc(ac, 1)
            act.wait_ge(ld_x, 32)
            act.activation(x_hi[:], x[:], ACT.Copy).then_inc(ac, 1)
            act.wait_ge(z_ready, 1)
            act.activation(turns[0:CE, :], noise[0:CE, :], ACT.Exp, scale=-1.0).then_inc(e_ready, 1)
            for i in range(2):
                act.wait_ge(ld_w, 16 * (i + 1))
                act.activation(w_hi[:, i], stage[:, 0:KD * D].rearrange("p (k d) -> p k d", k=KD), ACT.Copy,
                               scale=WS).then_inc(ac, 1)
            act.wait_ge(pad_rows, 1)

            def iteration(t, counts=True, mid=True, old=True):
                u = t - 1
                if mid:
                    act.wait_ge(c_T, t)
                    w = TAIL if isinstance(u, int) and u == NT - 1 else P
                    by_src = p_t[:, 0:NPAD].rearrange("p (s c) -> p s c", c=P)
                    act.activation(edges[:, :, bass.ds(u * P, w)], by_src[:, :, 0:w], ACT.Ln,
                                   bias=tiny[:, 0:1]).then_inc(logs_done, 1)
                    act.activation(c_hi[:], by_src, ACT.Copy).then_inc(c_hi_done, 1)
                if old:
                    act.wait_ge(rstd0, t - 1)
                    act.activation(hn[:], h[:], ACT.Identity, bias=rstd[:, 0, 2:3], scale=rstd[:, 0, 1:2]).then_inc(norm0, 1)
                    act.wait_ge(rstd1, t - 1)
                    act.activation(x[:, bass.ds(t - 2, 1), :], hn[:].unsqueeze(1), ACT.Identity, bias=rstd[:, 1, 2:3],
                                   scale=rstd[:, 1, 1:2]).then_inc(x1_done, 1)
                if mid:
                    act.wait_ge(m_T, t)
                    act.activation(mT_hi[:], p_t[:, 0:D].rearrange("p (k c) -> p k c", k=KD), ACT.Copy).then_inc(mT_hi_done, 1)
                if counts:
                    act.wait_ge(cnt_done, t + 1)
                    act.activation(c_rows[:, 0:N], p_cnt[:, 0:N], ACT.Identity,
                                   accum_out=degree[:, 0:1]).then_inc(rows_copied, 1)

            iteration(0, mid=False, old=False)
            iteration(1, old=False)
            with act.Fori(2, NT) as t:
                iteration(t)
            iteration(NT, counts=False)
            iteration(NT + 1, counts=False, mid=False)

        @block.vector
        def _(dve):
            chain = [0]

            def link(ins):
                chain[0] += 1
                ins.then_inc(dv, 1)
                dve.wait_ge(dv, chain[0])

            dve.wait_ge(ld_ids, 16 * 7)
            dve.tensor_copy(ids_row[:], ids_raw[:]).then_inc(rows_ready, 1)
            dve.wait_ge(rows_ready, 1)
            link(dve.tensor_reduce(span[:, 0, :], ids_row[:, 1], AX.X, ALU.min))
            link(dve.tensor_reduce(span[:, 1, :], ids_row[:, 1], AX.X, ALU.max))
            for i in range(2):
                for g in range(NG):
                    last = dve.tensor_copy(span10[:, i, g, :], span[:, i, g:g + 1].to_broadcast([P, NT]))
            last.then_inc(span_ready, 1)
            dve.wait_ge(ld_const, 64)
            nf = 2 * FREQ
            dve.wait_ge(ld_noise, 16)
            link(dve.tensor_scalar(turns[:], noise[:], const[0:nf, C_FREQ:C_FREQ + 1], None, ALU.mult))
            link(dve.tensor_scalar(noise[:], turns[:], MAGIC, MAGIC, ALU.add, ALU.subtract))
            link(dve.tensor_tensor(turns[:], turns[:], noise[:], ALU.subtract))
            link(dve.tensor_scalar(turns[:], turns[:], const[0:nf, C_PHASE:C_PHASE + 1], None, ALU.add))
            link(dve.tensor_scalar(noise[:], turns[:], MAGIC, MAGIC, ALU.add, ALU.subtract))
            link(dve.tensor_tensor(turns[:], turns[:], noise[:], ALU.subtract))
            half = 0.49999994
            dve.tensor_scalar(turns[:], turns[:], half, -half, ALU.min, ALU.max).then_inc(angle_ready, 1)
            for i in range(2):
                dve.wait_ge(ids_T, i + 1)
                last = dve.tensor_copy(ids[:, i, :], bank[i][:, 0:NG * P])
                last.then_inc(ids_ready, 1)
            dve.wait_ge(ld_const, 64)
            dve.wait_ge(span_T, 2)
            for i in range(2):
                link(dve.tensor_copy(spanT[:, i, :], bank[i][0:NT, 0:NQUAD * SLOTS]))
            link(dve.tensor_scalar(inside[:], spanT[:, 1, :], const[0:NT, C_TLO:C_TLO + 1], None, ALU.is_ge))
            link(dve.scalar_tensor_tensor(spanT[:, 0, :], spanT[:, 0, :], const[0:NT, C_THI:C_THI + 1], inside[:],
                                          ALU.is_lt, ALU.mult))
            link(dve.scalar_tensor_tensor(spanT[:, 1, :], quad_no[:], 1.0, spanT[:, 0, :], ALU.add, ALU.mult))
            link(dve.tensor_scalar(inside[:], quad_no[:], 1000.0, None, ALU.add))
            link(dve.scalar_tensor_tensor(inside[:], spanT[:, 0, :], -1000.0, inside[:], ALU.mult, ALU.add))
            link(dve.tensor_reduce(lohi[:, 0:1], inside[:], AX.X, ALU.min))
            link(dve.tensor_reduce(lohi[:, 1:2], spanT[:, 1, :], AX.X, ALU.max))
            link(dve.tensor_scalar(lohi[:, 1:2], lohi[:, 1:2], float(NSEG), None, ALU.max))
            link(dve.tensor_scalar(lohi[:, 3:4], lohi[:, 1:2], -float(NSEG), None, ALU.add))
            link(dve.tensor_tensor(lohi[:, 0:1], lohi[:, 0:1], lohi[:, 3:4], ALU.min))
            link(dve.tensor_tensor(lohi[:, 2:3], lohi[:, 1:2], lohi[:, 0:1], ALU.subtract))
            link(dve.tensor_scalar(lohi[:, 3:4], lohi[:, 2:3], 1.0 / NSEG, 0.5 / NSEG - 0.5, ALU.mult, ALU.add))
            dve.tensor_scalar(lohi[:, 3:4], lohi[:, 3:4], MAGIC, MAGIC, ALU.add, ALU.subtract).then_inc(lohi_ready, 1)
            dve.wait_ge(lohi_T, 1)
            link(dve.tensor_copy(ranges_f[:, 0:4, :], bank[0][0:1, 0:4 * NT].rearrange("p (a t) -> p a t", a=4)))
            link(dve.tensor_tensor(ranges_f[:, 4, :], ranges_f[:, 2, :], ranges_f[:, 0, :], ALU.subtract))
            for k in range(1, NSEG):
                link(dve.scalar_tensor_tensor(ranges_f[:, 4 + k, :], ranges_f[:, 3, :], float(k), ranges_f[:, 0, :],
                                              ALU.mult, ALU.add))
            dve.tensor_copy(ranges[:], ranges_f[:]).then_inc(ranges_ready, 1)

            def segment(bounds, before, k):
                with dve.Fori(bounds[k], bounds[k + 1]) as i:
                    for slot in range(SLOTS):
                        dve.wait_ge(counted, (i + before) * SLOTS + (slot + 1))
                        dve.tensor_scalar(oh_src[:, slot, :], iota[:], ids[:, 0, bass.ds(i * SLOTS + slot, 1)], None,
                                          ALU.is_equal)
                        dve.tensor_scalar(oh_dst[:, slot, :], iota[:, 0:P], ids[:, 1, bass.ds(i * SLOTS + slot, 1)], None,
                                          ALU.is_equal).then_inc(onehots, 1)

            def next_ids(bounds, before):
                dve.wait_ge(onehots, (bounds[NSEG] + before) * SLOTS)
                dve.tensor_scalar(ids[:, 1, :], ids[:, 1, :], float(P), None, ALU.subtract).then_inc(ids_ready, 1)

            def counts_split(u):
                dve.wait_ge(rows_copied, u + 1)
                dve.tensor_scalar(degree[:, 1:2], degree[:, 0:1], 1.0, None, ALU.max).then_inc(deg_done, 1)
                dve.wait_ge(deg_done, u * 2 + 1)
                dve.reciprocal(degree[:, 1:2], degree[:, 1:2]).then_inc(deg_done, 1)
                dve.wait_ge(c_hi_done, u + 1)
                dve.tensor_tensor(c_lo[:], p_t[:, 0:NPAD].rearrange("p (s c) -> p s c", c=P), c_hi[:],
                                  ALU.subtract).then_inc(c_lo_done, 1)
                w = TAIL if isinstance(u, int) and u == NT - 1 else P
                e = edges[:, :, bass.ds(u * P, w)]
                dve.wait_ge(logs_done, u + 1)
                dve.tensor_scalar(no_edge[:, :, 0:w], e, 0.0, -NOEDGE / 40, ALU.min, ALU.mult).then_inc(no_edge_done, 1)
                dve.wait_ge(no_edge_done, u + 1)
                dve.scalar_tensor_tensor(e, e, KAPPA, no_edge[:, :, 0:w], ALU.mult, ALU.add).then_inc(scores_set, 1)

            def mean_of(u):
                dve.wait_ge(deg_done, u * 2 + 2)
                dve.wait_ge(agg_done, u + 1)
                dve.tensor_scalar(mean[:], bank[0][:], degree[:, 1:2], None, ALU.mult).then_inc(mean_done, 1)

            def mean_split(u):
                dve.wait_ge(mT_hi_done, u + 1)
                dve.tensor_tensor(mT_lo[:], p_t[:, 0:D].rearrange("p (k c) -> p k c", k=KD), mT_hi[:],
                                  ALU.subtract).then_inc(mT_lo_done, 1)

            def layer(u):
                dve.wait_ge(h_done, u + 1)
                dve.scalar_tensor_tensor(h[:], bank[1][:], 1.0 / WS, vecs[:, 0, :], ALU.mult, ALU.add).then_inc(h_free, 1)
                dve.wait_ge(h_free, u + 2)
                dve.bn_stats(bn[:, 0, :], h[:]).then_inc(bn0_done, 1)
                dve.wait_ge(ld_vec, 48)
                dve.wait_ge(bn0_done, u + 1)
                dve.bn_aggr(mv[:, 0, :], bn[:, 0, :]).then_inc(stat0, 1)

            def finish(u):
                dve.wait_ge(affine0, u + 1)
                dve.scalar_tensor_tensor(hn[:].unsqueeze(1), hn[:].unsqueeze(1), 0.0, x[:, bass.ds(u, 1), :], ALU.max,
                                         ALU.add).then_inc(sum_done, 1)
                dve.wait_ge(sum_done, u + 1)
                dve.bn_stats(bn[:, 1, :], hn[:]).then_inc(bn1_done, 1)
                dve.wait_ge(ld_vec, 48)
                dve.wait_ge(bn1_done, u + 1)
                dve.bn_aggr(mv[:, 1, :], bn[:, 1, :]).then_inc(stat1, 1)

            def silu_input():
                dve.wait_ge(ld_f, 160)
                dve.wait_ge(f1_done, 1)
                dve.tensor_scalar(noise[0:CE, :], p_t[0:CE, 0:NPAD], fb1[:, 0:1], None, ALU.add).then_inc(z_ready, 1)

            def silu():
                dve.wait_ge(e_ready, 1)
                link(dve.tensor_scalar(turns[0:CE, :], turns[0:CE, :], 1.0, None, ALU.add))
                link(dve.reciprocal(turns[0:CE, :], turns[0:CE, :]))
                dve.tensor_tensor(turns[0:CE, :], turns[0:CE, :], noise[0:CE, :], ALU.mult).then_inc(silu_ready, 1)

            def weights_low(i):
                dve.wait_ge(ac, 3 + i)
                dve.scalar_tensor_tensor(w_lo[:, i], stage[:, 0:KD * D].rearrange("p (k d) -> p k d", k=KD), WS,
                                         w_hi[:, i], ALU.mult, ALU.subtract).then_inc(stage_free, 1)

            def conditioning():
                link(dve.tensor_tensor(fb2[:], fb2[:], const[:, C_ONE:C_ONE + 1], ALU.add))
                dve.wait_ge(f2_done, 1)
                link(dve.tensor_scalar(c_rows[:, 0:NPAD], p_t[:, 0:NPAD], fb2[:, 0:1], None, ALU.add))
                link(dve.tensor_copy(cond[:], c_rows[:, 0:NPAD]))
                for q in (1, 3):
                    r = slice(32 * q, 32 * q + 32)
                    link(dve.tensor_tensor(cond[r, :], c_rows[r, 0:NPAD], cond[r, :], ALU.subtract))
                dve.memset(c_rows[:, N:NPAD], 0.0).then_inc(pad_rows, 1)

            def iteration(t, counts=True, mid=True, old=True):
                first = isinstance(t, int) and t == 0
                if counts:
                    bounds, before = bounds_of(dve, ranges, t)
                    count = in_register(dve, t + 2)
                    dve.wait_ge(ld_const, 64)
                    dve.wait_ge(ids_ready, count)
                    segment(bounds, before, 0)
                if first:
                    silu_input()
                if mid:
                    counts_split(t - 1)
                if old:
                    layer(t - 2)
                if counts:
                    segment(bounds, before, 1)
                if first:
                    silu()
                if old:
                    finish(t - 2)
                if counts:
                    segment(bounds, before, 2)
                if first:
                    weights_low(0)
                if mid:
                    mean_of(t - 1)
                if counts:
                    segment(bounds, before, 3)
                    next_ids(bounds, before)
                if first:
                    conditioning()
                    weights_low(1)
                if mid:
                    mean_split(t - 1)

            dve.wait_ge(ld_vec, 48)
            dve.wait_ge(padded, 9)
            dve.memset(degree[:], 0.0).then_inc(h_free, 1)
            dve.wait_ge(ranges_ready, 1)
            iteration(0, mid=False, old=False)
            iteration(1, old=False)
            with dve.Fori(2, NT) as t:
                iteration(t)
            iteration(NT, counts=False)
            iteration(NT + 1, counts=False, mid=False)

        @block.tensor
        def _(pe):
            pe.wait_ge(rows_ready, 1)
            pe.wait_ge(ld_const, 64)
            for i in range(2):
                for g in range(NG):
                    last = pe.transpose(bank[i][:, g * P:(g + 1) * P], ids_row[:, i, g, :], ident[:])
                last.then_inc(ids_T, 1)
            pe.wait_ge(span_ready, 1)
            pe.wait_ge(ids_ready, 2)
            for i in range(2):
                for g in range(NG):
                    last = pe.matmul(bank[i][0:NT, g * P:(g + 1) * P], span10[:, i, g, :], ident[:], start=True, stop=True)
                last.then_inc(span_T, 1)
            pe.wait_ge(lohi_ready, 1)
            for i in (0, 1, 3):
                pe.matmul(bank[0][0:1, i * NT:(i + 1) * NT], lohi[:, i:i + 1], ident[0:NT, 0:NT], start=True, stop=True)
            pe.matmul(bank[0][0:1, 2 * NT:3 * NT], lohi[:, 2:3], const[0:NT, C_LOWER:C_LOWER + NT], start=True,
                      stop=True).then_inc(lohi_T, 1)
            pe.wait_ge(ld_f, 160)
            pe.wait_ge(emb_ready, 1)
            for a, b in COLS_PAD:
                last = pe.matmul(p_t[0:CE, a:b], f1[:], noise[:, a:b], start=True, stop=True)
            last.then_inc(f1_done, 1)
            pe.wait_ge(ranges_ready, 1)
            pe.wait_ge(padded, 9)

            def clear_counts(last=False):
                for j, (a, b) in enumerate(COLS):
                    m = pe.matmul(p_cnt[:, a:b], zeros[:, 0:P], zeros[:, 0:b - a], start=not last, stop=last)
                return m

            def segment(bounds, before, k):
                with pe.Fori(bounds[k], bounds[k + 1]) as i:
                    for slot in range(SLOTS):
                        pe.wait_ge(onehots, (i + before) * SLOTS + (slot + 1))
                        for a, b in COLS:
                            last = pe.matmul(p_cnt[:, a:b], oh_dst[:, slot, :], oh_src[:, slot, a:b], start=False, stop=False)
                        last.then_inc(counted, 1)

            def neighbours(u):
                pe.wait_ge(c_lo_done, u + 1)
                split_matmuls(pe, bank[0][:], [(c_hi[0:rows(s), s, :], c_lo[0:rows(s), s, :]) for s in range(NT)],
                              [(x_hi[0:rows(s), s, :], x_lo[0:rows(s), s, :]) for s in range(NT)]).then_inc(agg_done, 1)

            def turn_mean(u):
                pe.wait_ge(logs_done, u + 1)
                pe.wait_ge(mean_done, u + 1)
                for k in range(KD):
                    last = pe.transpose(p_t[:, k * P:(k + 1) * P], mean[:, k * P:(k + 1) * P], ident[:])
                last.then_inc(m_T, 1)

            def layer(u):
                pe.wait_ge(h_free, u + 1)
                for k in range(KD):
                    for j, (a, b) in enumerate(((xT_hi, w_hi), (xT_hi, w_lo), (xT_lo, w_hi))):
                        pe.matmul(bank[1][:], a[:, k, bass.ds(u * P, P)], b[:, 0, k, :], start=k == 0 and j == 0, stop=False)
                pe.wait_ge(mT_lo_done, u + 1)
                split_matmuls(pe, bank[1][:], [(mT_hi[:, k, :], mT_lo[:, k, :]) for k in range(KD)],
                              [(w_hi[:, 1, k, :], w_lo[:, 1, k, :]) for k in range(KD)], start=False).then_inc(h_done, 1)

            def turn_counts(t):
                pe.wait_ge(rows_copied, t + 1)
                for s in range(NT):
                    last = pe.transpose(p_t[:, s * P:(s + 1) * P], c_rows[:, s * P:(s + 1) * P], ident[:])
                last.then_inc(c_T, 1)

            def iteration(t, counts=True, mid=True):
                first, second = (isinstance(t, int) and t == n for n in (0, 1))
                if counts:
                    bounds, before = bounds_of(pe, ranges, t)
                    clear_counts()
                    segment(bounds, before, 0)
                    segment(bounds, before, 1)
                if second:
                    pe.wait_ge(split_done, 1)
                if mid:
                    neighbours(t - 1)
                if counts:
                    segment(bounds, before, 2)
                if first:
                    pe.wait_ge(silu_ready, 1)
                    for a, b in COLS_PAD:
                        last = pe.matmul(p_t[:, a:b], f2[:], turns[0:CE, a:b], start=True, stop=True)
                    last.then_inc(f2_done, 1)
                if mid:
                    turn_mean(t - 1)
                if counts:
                    segment(bounds, before, 3)
                    clear_counts(last=True).then_inc(cnt_done, 1)
                if second:
                    pe.wait_ge(stage_free, 3)
                if mid:
                    layer(t - 1)
                if counts:
                    turn_counts(t)

            clear_counts()
            clear_counts(last=True).then_inc(counted, SLOTS)
            iteration(0, mid=False)
            iteration(1)
            with pe.Fori(2, NT) as t:
                iteration(t)
            iteration(NT, counts=False)


STEPS = H * NT
GROUPS = (NT + 1) // 2
JOBS = H * 6 + NT
WIDTH = 2 * P
OS = 4.0
LOADS_FIRST = ["cond1", "q0", "q1", "k0", "k1", "bv"]
LOADS_STEP = {2: "m20", 4: "m21", 6: "m10", 8: "m11", 10: "cond2"}
LOADS_NEXT = {12: "cond1", 14: "bv", 32: "q0", 34: "q1", 36: "k0", 38: "k1"}
LATE = ["o0", "o1", "v0", "v1"]
TICKS_EARLY = 4


def block_loads(last):
    steps = dict(LOADS_STEP) if last else {**LOADS_STEP, **LOADS_NEXT}
    return [steps[n] for n in sorted(steps)]


LOADS = len(block_loads(False))


def tick(k, norms):
    return [(stage, i) for stage, i in (("stats", k), ("norm", k - 1), ("turn", k - 2)) if 0 <= i < norms]


def early_ticks():
    return [item for k in range(TICKS_EARLY) for item in tick(k, NT)]


def first_sequence():
    seq = [("load", 0)]
    for k in range(NT + 2):
        seq += tick(k, NT)
        if k % 2 and k // 2 + 1 < len(LOADS_FIRST):
            seq.append(("load", k // 2 + 1))
        if k >= NT - 2:
            seq.append(("late", k - (NT - 2)))
    return seq


def mlp_sequence(last):
    norms = NT if last else 2 * NT
    seq = []
    for k in range(TICKS_EARLY, 6):
        seq += tick(k, norms)
    for j in range(KD):
        seq.append(("up", j))
        seq += tick(6 + j, norms)
    for c in range(3):
        if c:
            seq += [("up", c * KD + j) for j in range(KD)]
        for t in range(4 * c, min(4 * c + 4, NT)):
            seq.append(("down", t))
            if last:
                seq.append(("final", t))
            if not last or t < 2:
                seq += tick(10 + t, norms)
            if t in (3, 4) and not last:
                seq.append(("late", t - 3))
    if not last:
        seq += tick(20, norms) + [("late", 2)] + tick(21, norms) + [("late", 3)]
    return seq


def values_at(n):
    if n < 3:
        return None
    h, r = divmod(n - 3, NT)
    g, part = divmod(r, 2)
    return (h * GROUPS + g, part) if h < H else None


def output_at(n):
    if n < 5 or n >= 5 + 2 * H * GROUPS:
        return None
    return divmod(n - 5, 2)


DRAIN = 5 + 2 * H * GROUPS


def job_list(h):
    jobs = [("k", c) for c in range(3)] + [("q", c) for c in range(3)]
    return jobs + ([("v", t) for t in range(NT)] if h == 0 else [])


def job_start(h):
    return 6 * h + (NT if h else 0)


def transformer(nc, io, keep):
    ctx = ExitStack()
    with ctx:
        def sb(name, shape, dt):
            return ctx.enter_context(nc.sbuf_tensor(name, shape, dt))

        def ps(name, n):
            return ctx.enter_context(nc.psum_tensor(name, [P, n], F32))

        def sem(name):
            return ctx.enter_context(nc.semaphore(name))

        x, edges, cond, ident, mhalf = keep.x, keep.edges, keep.cond, keep.ident, keep.mhalf

        w_q, w_k, w_v, w_o, w_2 = (sb(n, [P, 2, KD, D], F16) for n in ("w_q", "w_k", "w_v", "w_o", "w_2"))
        w_1 = w_v
        stage = sb("wstage", [P, 2 * D], F32)
        wc1 = sb("wc1", [P, 2, D], F16)
        wc2 = sb("wc2", [P, 2, D], F16)
        bv = sb("bv", [64, D], F16)
        ones = sb("ones", [64, P], F16)
        brow = sb("brow", [P, D], F32)
        bcols = sb("bcols", [P, B, 3 * KD], F32)
        bcol = sb("bcol", [P, 3 * KD], F32)
        yT = sb("yT", [P, 2, KD, N], F16)
        v = sb("v", [P, 2, NT, D], F16)
        qk = sb("qk", [P, 2, 2, N], F16)
        pr = sb("pr", [P, 2, NPAD], F32)
        pT = sb("pT", [P, 2, 2, NT * WIDTH], F16)
        oT = sb("oT", [P, 2, WIDTH], F16)
        small = sb("small", [P, 8, 4], F32)
        bn = sb("bn_b", [P, 2, 6], F32)
        mv = sb("mv_b", [P, 2, 2], F32)
        rstd = sb("rstd_b", [P, 2, 4], F32)
        xn = [pr[:, i, 0:D] for i in range(2)]
        yn = [pr[:, i, D:2 * D] for i in range(2)]
        pTv = [pT[:, :, i, :].rearrange("p a (t c) -> p a t c", t=NT) for i in range(2)]
        wide = pT[:].rearrange("p a b c -> p (a b c)").bitcast(F32)
        late_raw = [wide[:, j * 2 * D:(j + 1) * 2 * D] for j in range(len(LATE))]
        x_in = wide.rearrange("p (t d) -> p t d", t=NT)
        hid = qk[:].rearrange("p a b c -> p (a b c)").bitcast(F32)[:, 0:2 * 512].rearrange("p (a c) -> p a c", a=2)

        psA, psB, ps6, ps7 = ps("psA", 3 * 512), ps("psB", 3 * 512), ps("ps6", 512), ps("ps7", 512)
        norm_bank = [psA[:, 0:512], psA[:, 512:1024]]
        turn_bank = [psA[:, 1024:1536], psB[:, 0:512]]
        up_bank = [psB[:, 512:1024], psB[:, 1024:1536]]
        down_bank = [ps6[:], ps7[:]]

        setup = sem("setup")
        stage_in, stage_scaled, stage_hi, stage_lo = (sem(n) for n in ("stage_in", "stage_scaled", "stage_hi", "stage_lo"))
        late_in, late_hi, late_lo = (sem(n) for n in ("late_in", "late_hi", "late_lo"))
        brow_in, bcols_in, bcols_scaled, bcol_set = (sem(n) for n in ("brow_in", "bcols_in", "bcols_scaled", "bcol_set"))
        x_saved, x_back, stored = sem("x_saved"), sem("x_back"), sem("stored")
        bn_done, stats_done, rstd_done, xn_done, scale_done, yn_done, turned, yT_hi, yT_lo = (
            sem(n) for n in ("bn_done", "stats_done", "rstd_done", "xn_done", "scale_done", "yn_done", "turned",
                             "yT_hi", "yT_lo"))
        job_done, job_hi, job_lo = sem("job_done"), sem("job_hi"), sem("job_lo")
        scores_done, masked, exp_done, inv_done, out_scaled = (
            sem(n) for n in ("scores_done", "masked", "exp_done", "inv_done", "out_scaled"))
        pT_done, pT_hi, pT_lo = sem("pT_done"), sem("pT_hi"), sem("pT_lo")
        values_done, oT_hi, oT_lo, out_done, out_added, bo_added = (
            sem(n) for n in ("values_done", "oT_hi", "oT_lo", "out_done", "out_added", "bo_added"))
        up_done, relu_done, hid_hi, hid_lo, down_done, down_added, b2_added = (
            sem(n) for n in ("up_done", "relu_done", "hid_hi", "hid_lo", "down_done", "down_added", "b2_added"))
        final_sum, final_bn, final_stats, final_rstd, final_done = (
            sem(n) for n in ("final_sum", "final_bn", "final_stats", "final_rstd", "final_done"))
        pool_step = sem("pool_step")

        def halves_of(name):
            if name in ("cond1", "cond2"):
                w = (wc1 if name == "cond1" else wc2)[:].rearrange("p a d -> p (a d)")
                return stage[:], w, stage[64:P, :], w[64:P, :], w[64:P, :]
            if name == "bv":
                return stage[0:64, 0:D], bv[:], stage[32:64, 0:D], bv[32:64, :], bv[32:64, :]
            w = {"q": w_q, "k": w_k, "m1": w_1, "m2": w_2}[name[:-1]]
            c = 2 * int(name[-1])
            raw = stage[:].rearrange("p (k d) -> p k d", k=2)
            return raw, w[:, 0, c:c + 2, :], raw, w[:, 0, c:c + 2, :], w[:, 1, c:c + 2, :]

        def scale_of(name):
            return 1.0 if name[0:2] in ("co", "bv") else WS

        def late_halves(j):
            w = w_o if j < 2 else w_v
            c = 2 * (j % 2)
            return late_raw[j].rearrange("p (k d) -> p k d", k=2), w[:, 0, c:c + 2, :], w[:, 1, c:c + 2, :]

        def loads_before(b):
            return b * LOADS + len(LOADS_FIRST)

        def norms_before(b):
            return b * (2 * NT) + NT

        block = ctx.enter_context(nc.Block())

        @block.sync
        def _(sp):
            def load(name, b, seq):
                if not isinstance(seq, int) or seq > 0:
                    sp.wait_ge(stage_lo, seq)
                if name in ("cond1", "cond2"):
                    w = (io["w_cond1"] if name == "cond1" else io["w_cond2"])[bass.ds(b, 1)].rearrange("b r n -> (b r) n")
                    for q in range(4):
                        sp.dma_start(stage[32 * q:32 * q + CE + 1, :], w).then_inc(stage_in, 16)
                elif name == "bv":
                    for q in range(4):
                        r, c = 32 * (q % 2), (q // 2) * 256
                        sp.dma_start(stage[r:r + 1, c:c + 256], io["bv"][bass.ds(b, 1), c:c + 256]).then_inc(stage_in, 16)
                else:
                    w = {"q": io["wq"], "k": io["wk"], "m1": io["m_w1"], "m2": io["m_w2"]}[name[:-1]]
                    src = w[bass.ds(b, 1)].rearrange("b (k p) d -> p (b k) d", p=P)
                    for q in range(4):
                        k, c = 2 * int(name[-1]) + q // 2, (q % 2) * 256
                        sp.dma_start(stage[:, q * 256:(q + 1) * 256].unsqueeze(1), src[:, k:k + 1, c:c + 256]).then_inc(stage_in, 16)

            def load_late(b):
                for j in range(len(LATE)):
                    src = (io["wo"] if j < 2 else io["wv"])[bass.ds(b, 1)].rearrange("b (k p) d -> p (b k) d", p=P)
                    for q in range(4):
                        k, c = 2 * (j % 2) + q // 2, (q % 2) * 256
                        sp.dma_start(late_raw[j][:, q * 256:(q + 1) * 256].unsqueeze(1), src[:, k:k + 1, c:c + 256]).then_inc(late_in, 16)

            def load_row(w, b):
                sp.dma_start(brow[:], w[bass.ds(b, 1), :].rearrange("b d -> (b d)").partition_broadcast(P)).then_inc(brow_in, 16)

            sp.dma_start(io["x_scratch"].rearrange("(t p) d -> p t d", p=P), x[:]).then_inc(x_saved, 16)
            sp.dma_start(bcols[:], io["bias_cols"].rearrange("b p j -> p b j")).then_inc(bcols_in, 16)
            load_row(io["bo"], 0)
            sp.wait_ge(setup, 1)
            for i, name in enumerate(LOADS_FIRST):
                load(name, 0, i)
                if i == 1:
                    load_late(0)

            def body(b, last):
                sp.wait_ge(bo_added, (b + 1) * NT)
                load_row(io["b2"], b)
                names = block_loads(last)
                for i, name in enumerate(names):
                    load(name, b if name in LOADS_STEP.values() else b + 1, loads_before(b) + i)
                if not last:
                    sp.wait_ge(values_done, (b + 1) * H * GROUPS)
                    load_late(b + 1)
                    sp.wait_ge(b2_added, (b + 1) * NT)
                    load_row(io["bo"], b + 1)

            with sp.Fori(0, B - 1) as b:
                body(b, False)
            body(B - 1, True)
            sp.wait_ge(values_done, B * H * GROUPS)
            sp.wait_ge(x_saved, 16)
            sp.dma_start(x_in, io["x_scratch"].rearrange("(t p) d -> p t d", p=P)).then_inc(x_back, 16)
            for t in range(NT):
                sp.wait_ge(final_done, t + 1)
                sp.dma_start(io["out"][t * P:t * P + rows(t), :], x_in[0:rows(t), t, :]).then_inc(stored, 16)
            sp.wait_ge(stored, 16 * NT)

        @block.gpsimd
        def _(pool):
            pool.memset(ones[:], 0.0).then_inc(pool_step, 1)
            pool.memset(stage[:], 0.0).then_inc(pool_step, 1)
            pool.memset(pr[:], 0.0).then_inc(pool_step, 1)
            pool.memset(small[:], 0.0).then_inc(pool_step, 1)
            pool.wait_ge(pool_step, 4)
            pool.memset(ones[0:1, :], WS).then_inc(pool_step, 1)
            pool.memset(ones[32:33, :], WS).then_inc(pool_step, 1)
            pool.wait_ge(pool_step, 6)
            pool.memset(rstd[:], 0.0).then_inc(setup, 1)

            def split(name, seq):
                raw, _, low_of, high, low = halves_of(name)
                count = in_register(pool, seq * 64 + 64)
                pool.wait_ge(pool_step, 6)
                pool.wait_ge(stage_in, count)
                pool.tensor_scalar(raw, raw, scale_of(name), None, ALU.mult).then_inc(stage_scaled, 1)
                pool.wait_ge(stage_hi, seq + 1)
                pool.tensor_tensor(low, low_of, high, ALU.subtract).then_inc(stage_lo, 1)
                pool.wait_ge(stage_lo, seq + 1)

            def inverse(i, before, aggregated, count, done):
                count = in_register(pool, count)
                pool.wait_ge(pool_step, 6)
                pool.wait_ge(aggregated, count)
                pool.tensor_scalar(rstd[:, i, 0:1], mv[:, i, 1:2], EPS, None, ALU.add).then_inc(pool_step, 1)
                pool.wait_ge(pool_step, before * 2 + 7)
                pool.tensor_tensor(rstd[:, i, 1:2], rstd[:, i, 0:1], mhalf[:, 0:1], ALU.pow).then_inc(pool_step, 1)
                count = in_register(pool, before * 2 + 8)
                pool.wait_ge(pool_step, 6)
                pool.wait_ge(pool_step, count)
                pool.tensor_scalar(rstd[:, i, 2:3], mv[:, i, 0:1], rstd[:, i, 1:2], -1.0, ALU.mult, ALU.mult).then_inc(done, 1)

            for k in range(NT):
                inverse(k % 2, k, stats_done, k + 1, rstd_done)
            pool.wait_ge(x_saved, 16)

            def body(b, last):
                pool.wait_ge(xn_done, norms_before(b))
                pool.wait_ge(brow_in, b * 32 + 16)
                for t in range(NT):
                    pool.tensor_tensor(x[:, t, :], x[:, t, :], brow[:], ALU.add).then_inc(bo_added, 1)
                names = block_loads(last)
                for j in range(len(names)):
                    split(names[j], loads_before(b) + j)
                pool.wait_ge(brow_in, b * 32 + 32)
                for kind, k in early_ticks() + mlp_sequence(last):
                    if kind == "stats":
                        inverse(k % 2, norms_before(b) + k, stats_done, norms_before(b) + k + 1, rstd_done)
                    elif kind == "turn" and k < NT:
                        pool.wait_ge(xn_done, norms_before(b) + k + 1)
                        pool.tensor_tensor(x[:, k, :], x[:, k, :], brow[:], ALU.add).then_inc(b2_added, 1)
                    elif kind == "final":
                        if k >= 2:
                            pool.wait_ge(final_done, k - 1)
                        inverse(k % 2, norms_before(b) + NT + k, final_stats, k + 1, final_rstd)

            with pool.Fori(0, B - 1) as b:
                body(b, False)
            body(B - 1, True)

        @block.scalar
        def _(act):
            def split(name, seq):
                raw, high = halves_of(name)[0:2]
                act.wait_ge(stage_scaled, seq + 1 - len(LOADS_FIRST))
                act.activation(high, raw, ACT.Copy).then_inc(stage_hi, 1)

            def norm(i, before):
                t = i % NT
                act.wait_ge(rstd_done, before + i + 1)
                act.activation(xn[i % 2], x[:, t, :], ACT.Identity, bias=rstd[:, i % 2, 2:3],
                               scale=rstd[:, i % 2, 1:2]).then_inc(xn_done, 1)

            def turn(i, before):
                t = i % NT
                r = rows(t)
                act.wait_ge(turned, before + i + 1)
                act.activation(yT[:, 0, :, t * P:t * P + r],
                               turn_bank[i % 2].rearrange("p (k c) -> p k c", k=KD)[:, :, 0:r], ACT.Copy).then_inc(yT_hi, 1)

            def late_high(j, b):
                raw, high, _ = late_halves(j)
                act.wait_ge(late_in, (b + 1) * (len(LATE) * 64))
                act.activation(high, raw, ACT.Copy, scale=WS).then_inc(late_hi, 1)

            for kind, k in first_sequence():
                if kind == "load":
                    raw, high = halves_of(LOADS_FIRST[k])[0:2]
                    act.wait_ge(stage_in, k * 64 + 64)
                    act.activation(high, raw, ACT.Copy, scale=scale_of(LOADS_FIRST[k])).then_inc(stage_hi, 1)
                elif kind == "norm":
                    norm(k, 0)
                elif kind == "turn":
                    turn(k, 0)
                elif kind == "late":
                    late_high(k, 0)

            def project(b, h):
                for i, (kind, c) in enumerate(job_list(h)):
                    act.wait_ge(job_done, b * JOBS + job_start(h) + i + 1)
                    slot = psA[:, (i % 3) * 512:(i % 3 + 1) * 512]
                    if kind == "v":
                        r = rows(c)
                        act.activation(v[0:r, 0, c, :], slot[0:r, :], ACT.Copy).then_inc(job_hi, 1)
                    else:
                        which = int(kind == "k")
                        lo, hi = COLS[c]
                        act.wait_ge(bcol_set, b + 1)
                        act.activation(qk[:, which, 0, lo:hi], slot[:, 0:hi - lo], ACT.Identity,
                                       bias=bcol[:, which * KD + h:which * KD + h + 1]).then_inc(job_hi, 1)

            def exponential(b, n):
                r = rows(n % NT)
                act.wait_ge(masked, b * STEPS + n + 1)
                act.activation(pr[0:r, n % 2, 0:N], pr[0:r, n % 2, 0:N], ACT.Exp, bias=small[0:r, n % 8, 0:1], scale=-1.0,
                               accum_out=small[0:r, n % 8, 1:2]).then_inc(exp_done, 1)

            def transposed(b, n):
                s = n % NT
                G, r = n // 2, rows(s)
                if G >= 2:
                    act.wait_ge(values_done, b * H * GROUPS + G - 1)
                act.wait_ge(pT_done, b * STEPS + n + 1)
                act.activation(pTv[G % 2][:, 0, :, (s % 2) * P:(s % 2) * P + r],
                               psB[:, 0:NPAD].rearrange("p (t c) -> p t c", c=P)[:, :, 0:r], ACT.Copy).then_inc(pT_hi, 1)

            def values(b, n):
                G, part = values_at(n) or (0, 0)
                if part:
                    w = sum(rows(2 * (G % GROUPS) + i) for i in range(2))
                    if G:
                        act.wait_ge(out_done, b * STEPS + 2 * G)
                    act.wait_ge(values_done, b * H * GROUPS + G + 1)
                    act.activation(oT[:, 0, 0:w], ps6[:, 0:w], ACT.Copy, scale=1.0 / (WS * OS)).then_inc(oT_hi, 1)

            def body(b, last):
                names = block_loads(last)
                steps = LOADS_STEP if last else {**LOADS_STEP, **LOADS_NEXT}
                i = 0
                for n in range(DRAIN):
                    boundary = n % NT == 0 and n < STEPS
                    if boundary:
                        project(b, n // NT)
                    if 1 <= n <= STEPS:
                        transposed(b, n - 1)
                    if n < STEPS:
                        exponential(b, n)
                    values(b, n)
                    if n in steps:
                        split(names[i], loads_before(b) + i)
                        i += 1
                    if n >= DRAIN - TICKS_EARLY:
                        second_half(b, tick(n - (DRAIN - TICKS_EARLY), NT))
                second_half(b, mlp_sequence(last))

            def second_half(b, items):
                for kind, k in items:
                    if kind == "norm":
                        norm(k, norms_before(b))
                    elif kind == "turn":
                        turn(k, norms_before(b))
                    elif kind == "up":
                        c, j = divmod(k, KD)
                        w = COLS[c][1] - COLS[c][0]
                        if c == 2:
                            act.wait_ge(down_done, b * NT + 4)
                        if k >= 2:
                            act.wait_ge(hid_lo, b * 3 * KD + k - 1)
                        act.wait_ge(up_done, b * 3 * KD + k + 1)
                        act.activation(hid[:, k % 2, 0:w], up_bank[k % 2][:, 0:w], ACT.Relu,
                                       bias=bcol[:, 2 * KD + j:2 * KD + j + 1]).then_inc(relu_done, 1)
                        act.wait_ge(relu_done, b * 3 * KD + k + 1)
                        act.activation(v[:, 0, (c % 2) * KD + j, 0:w], hid[:, k % 2, 0:w], ACT.Copy).then_inc(hid_hi, 1)
                    elif kind == "late":
                        if k < 2:
                            act.wait_ge(out_done, (b + 1) * STEPS)
                        else:
                            act.wait_ge(up_done, (b + 1) * (3 * KD))
                        late_high(k, b + 1)
                    elif kind == "final":
                        act.wait_ge(final_rstd, k + 1)
                        act.activation(x_in[:, k, :], x[:, k, :], ACT.Identity, bias=rstd[:, k % 2, 2:3],
                                       scale=rstd[:, k % 2, 1:2]).then_inc(final_done, 1)

            with act.Fori(0, B - 1) as b:
                body(b, False)
            body(B - 1, True)

        @block.vector
        def _(dve):
            def stats(i, before):
                dve.bn_stats(bn[:, i % 2, :], x[:, i % NT, :]).then_inc(bn_done, 1)
                count = in_register(dve, before + i + 1)
                dve.wait_ge(setup, 1)
                dve.wait_ge(bn_done, count)
                dve.bn_aggr(mv[:, i % 2, :], bn[:, i % 2, :]).then_inc(stats_done, 1)

            def norm(i, before):
                dve.wait_ge(xn_done, before + i + 1)
                dve.wait_ge(scale_done, before + i + 1)
                dve.scalar_tensor_tensor(yn[i % 2], norm_bank[i % 2], 1.0, xn[i % 2], ALU.add, ALU.mult).then_inc(yn_done, 1)

            def turn(i, before):
                t = i % NT
                r = rows(t)
                dve.wait_ge(yT_hi, before + i + 1)
                dve.tensor_tensor(yT[:, 1, :, t * P:t * P + r], turn_bank[i % 2].rearrange("p (k c) -> p k c", k=KD)[:, :, 0:r],
                                  yT[:, 0, :, t * P:t * P + r], ALU.subtract).then_inc(yT_lo, 1)

            dve.wait_ge(setup, 1)
            dve.wait_ge(bcols_in, 16)
            dve.tensor_scalar(bcols[:], bcols[:], WS, None, ALU.mult).then_inc(bcols_scaled, 1)
            dve.wait_ge(bcols_scaled, 1)
            dve.tensor_copy(bcol[:], bcols[:, 0, :]).then_inc(bcol_set, 1)
            def late_low(j, b):
                raw, high, low = late_halves(j)
                dve.wait_ge(late_hi, b * len(LATE) + (j + 1))
                dve.scalar_tensor_tensor(low, raw, WS, high, ALU.mult, ALU.subtract).then_inc(late_lo, 1)

            for kind, k in first_sequence():
                if kind == "load":
                    _, _, raw, high, low = halves_of(LOADS_FIRST[k])
                    dve.wait_ge(stage_hi, k + 1)
                    dve.scalar_tensor_tensor(low, raw, scale_of(LOADS_FIRST[k]), high, ALU.mult,
                                             ALU.subtract).then_inc(stage_lo, 1)
                elif kind == "stats":
                    stats(k, 0)
                elif kind == "norm":
                    norm(k, 0)
                elif kind == "turn":
                    turn(k, 0)
                elif kind == "late":
                    late_low(k, 0)

            def project(b, h):
                for i, (kind, c) in enumerate(job_list(h)):
                    dve.wait_ge(job_hi, b * JOBS + job_start(h) + i + 1)
                    slot = psA[:, (i % 3) * 512:(i % 3 + 1) * 512]
                    if kind == "v":
                        r = rows(c)
                        dve.tensor_tensor(v[0:r, 1, c, :], slot[0:r, :], v[0:r, 0, c, :], ALU.subtract).then_inc(job_lo, 1)
                    else:
                        which = int(kind == "k")
                        lo, hi = COLS[c]
                        dve.scalar_tensor_tensor(qk[:, which, 1, lo:hi], slot[:, 0:hi - lo],
                                                 bcol[:, which * KD + h:which * KD + h + 1], qk[:, which, 0, lo:hi],
                                                 ALU.add, ALU.subtract).then_inc(job_lo, 1)

            def mask(b, n):
                s = n % NT
                r = rows(s)
                count = in_register(dve, b * STEPS + n + 1)
                dve.wait_ge(setup, 1)
                dve.wait_ge(scores_done, count)
                dve.tensor_tensor_reduce(out=pr[0:r, n % 2, 0:N], in0=psA[0:r, 0:N], in1=edges[0:r, s, :],
                                         scale=-1.0 / KAPPA, scalar=3e38, op0=ALU.add, op1=ALU.min,
                                         accum_out=small[0:r, n % 8, 0:1]).then_inc(masked, 1)

            def inverse(b, n):
                m = small[0:rows(n % NT), n % 8, :]
                dve.wait_ge(exp_done, b * STEPS + n + 1)
                dve.reciprocal(m[:, 2:3], m[:, 1:2])
                dve.tensor_scalar(m[:, 3:4], m[:, 0:1], -NOEDGE / KAPPA / 8, OS / WS, ALU.is_lt, ALU.mult).then_inc(inv_done, 1)

            def scale(b, n):
                m = small[0:rows(n % NT), n % 8, :]
                dve.wait_ge(inv_done, b * STEPS + n + 1)
                dve.tensor_tensor(m[:, 3:4], m[:, 3:4], m[:, 2:3], ALU.mult).then_inc(out_scaled, 1)

            def transposed(b, n):
                s = n % NT
                G, r = n // 2, rows(s)
                out = pTv[G % 2][:, :, :, (s % 2) * P:(s % 2) * P + r]
                dve.wait_ge(pT_hi, b * STEPS + n + 1)
                dve.tensor_tensor(out[:, 1], psB[:, 0:NPAD].rearrange("p (t c) -> p t c", c=P)[:, :, 0:r], out[:, 0],
                                  ALU.subtract).then_inc(pT_lo, 1)

            def values(b, n):
                G, part = values_at(n) or (0, 0)
                if part:
                    w = sum(rows(2 * (G % GROUPS) + i) for i in range(2))
                    dve.wait_ge(oT_hi, b * H * GROUPS + G + 1)
                    dve.scalar_tensor_tensor(oT[:, 1, 0:w], ps6[:, 0:w], 1.0 / (WS * OS), oT[:, 0, 0:w], ALU.mult, ALU.subtract).then_inc(oT_lo, 1)

            def output(b, n):
                if output_at(n) is None:
                    return
                G, i = output_at(n)
                t = 2 * (G % GROUPS) + i
                r = rows(t)
                if G < GROUPS:
                    dve.wait_ge(bo_added, b * NT + t + 1)
                dve.wait_ge(out_scaled, b * STEPS + 2 * G + i + 1)
                dve.wait_ge(out_done, b * STEPS + 2 * G + i + 1)
                dve.scalar_tensor_tensor(x[0:r, t, :], ps7[0:r, :], small[0:r, (2 * G + i) % 8, 3:4], x[0:r, t, :], ALU.mult,
                                         ALU.add).then_inc(out_added, 1)

            def body(b, last):
                for n in range(DRAIN):
                    boundary = n % NT == 0 and n < STEPS
                    if boundary:
                        project(b, n // NT)
                    elif n < STEPS:
                        mask(b, n)
                    if 2 <= n < STEPS + 2:
                        scale(b, n - 2)
                    if 1 <= n <= STEPS:
                        transposed(b, n - 1)
                        inverse(b, n - 1)
                    if boundary:
                        mask(b, n)
                    values(b, n)
                    output(b, n)
                    if n >= DRAIN - TICKS_EARLY:
                        second_half(b, tick(n - (DRAIN - TICKS_EARLY), NT))
                second_half(b, mlp_sequence(last))
                if not last:
                    dve.wait_ge(setup, 1)
                    dve.wait_ge(relu_done, (b + 1) * 3 * KD)
                    dve.tensor_copy(bcol[:].unsqueeze(1), bcols[:, bass.ds(b + 1, 1), :]).then_inc(bcol_set, 1)

            def second_half(b, items):
                for kind, k in items:
                    t = k % NT
                    if kind == "stats":
                        if k < NT:
                            dve.wait_ge(out_added, b * STEPS + (H - 1) * NT + t + 1)
                        else:
                            dve.wait_ge(down_added, b * NT + t + 1)
                        stats(k, norms_before(b))
                    elif kind == "norm":
                        norm(k, norms_before(b))
                    elif kind == "turn":
                        turn(k, norms_before(b))
                    elif kind == "up":
                        c, j = divmod(k, KD)
                        w = COLS[c][1] - COLS[c][0]
                        dve.wait_ge(hid_hi, b * 3 * KD + k + 1)
                        slot = (c % 2) * KD + j
                        dve.tensor_tensor(v[:, 1, slot, 0:w], hid[:, k % 2, 0:w], v[:, 0, slot, 0:w],
                                          ALU.subtract).then_inc(hid_lo, 1)
                    elif kind == "late":
                        late_low(k, b + 1)
                    elif kind == "down":
                        r = rows(t)
                        dve.wait_ge(b2_added, b * NT + t + 1)
                        dve.wait_ge(down_done, b * NT + t + 1)
                        dve.scalar_tensor_tensor(x[0:r, t, :], down_bank[t % 2][0:r, :], 1.0 / (WS * WS), x[0:r, t, :],
                                                 ALU.mult, ALU.add).then_inc(down_added, 1)
                    elif kind == "final":
                        if t == 0:
                            dve.wait_ge(x_back, 16)
                        if t >= 2:
                            dve.wait_ge(final_rstd, t - 1)
                        dve.wait_ge(down_added, b * NT + t + 1)
                        dve.tensor_tensor(x[:, t, :], x[:, t, :], x_in[:, t, :], ALU.add).then_inc(final_sum, 1)
                        dve.wait_ge(final_sum, t + 1)
                        dve.bn_stats(bn[:, t % 2, :], x[:, t, :]).then_inc(final_bn, 1)
                        dve.wait_ge(final_bn, t + 1)
                        dve.bn_aggr(mv[:, t % 2, :], bn[:, t % 2, :]).then_inc(final_stats, 1)

            with dve.Fori(0, B - 1) as b:
                body(b, False)
            body(B - 1, True)

        @block.tensor
        def _(pe):
            def norm(i, before, wc, wait=None):
                t = i % NT
                pe.matmul(norm_bank[i % 2], cond[:, t * P:(t + 1) * P], wc[:, 0, :], start=True, stop=True).then_inc(scale_done, 1)

            def turn(i, before, wc):
                t = i % NT
                r = rows(t)
                if not isinstance(before, int) or before + i >= 2:
                    pe.wait_ge(yT_lo, before + i - 1)
                pe.wait_ge(yn_done, before + i + 1)
                for k in range(KD):
                    out = turn_bank[i % 2][:, k * P:k * P + r]
                    pe.matmul(out, wc[:, 1, k * P:(k + 1) * P], cond[:, t * P:t * P + r], start=True, stop=False)
                    last = pe.matmul(out, yn[i % 2][0:r, k * P:(k + 1) * P], ident[0:r, 0:r], start=False, stop=True,
                                     is_transpose=True)
                last.then_inc(turned, 1)

            pe.wait_ge(stage_lo, 1)
            for kind, k in first_sequence():
                if kind == "norm":
                    norm(k, 0, wc1)
                elif kind == "turn":
                    turn(k, 0, wc1)

            def project(b, h):
                if h:
                    pe.wait_ge(masked, b * STEPS + h * NT)
                else:
                    pe.wait_ge(yT_lo, norms_before(b))
                    pe.wait_ge(stage_lo, loads_before(b))
                for i, (kind, c) in enumerate(job_list(h)):
                    if i >= 3:
                        pe.wait_ge(job_lo, b * JOBS + job_start(h) + i - 2)
                    slot = psA[:, (i % 3) * 512:(i % 3 + 1) * 512]
                    if kind == "v":
                        if c == 0:
                            pe.wait_ge(late_lo, (b + 1) * len(LATE))
                        r = rows(c)
                        pe.matmul(slot[0:r, :], ones[:, 0:r], bv[:], start=True, stop=False)
                        last = split_matmuls(pe, slot[0:r, :],
                                             [(yT[:, 0, k, c * P:c * P + r], yT[:, 1, k, c * P:c * P + r]) for k in range(KD)],
                                             [(w_v[:, 0, k, :], w_v[:, 1, k, :]) for k in range(KD)], start=False)
                    else:
                        w = w_k if kind == "k" else w_q
                        lo, hi = COLS[c]
                        last = split_matmuls(pe, slot[:, 0:hi - lo],
                                             [(w[:, 0, k, h * P:(h + 1) * P], w[:, 1, k, h * P:(h + 1) * P]) for k in range(KD)],
                                             [(yT[:, 0, k, lo:hi], yT[:, 1, k, lo:hi]) for k in range(KD)])
                    last.then_inc(job_done, 1)

            def scores(b, n):
                s = n % NT
                r = rows(s)
                if s == 0:
                    pe.wait_ge(job_lo, b * JOBS + job_start(n // NT + 1))
                else:
                    pe.wait_ge(masked, b * STEPS + n)
                for part, (i, j) in enumerate(((0, 0), (0, 1), (1, 0))):
                    for lo, hi in COLS:
                        last = pe.matmul(psA[0:r, lo:hi], qk[:, 0, i, s * P:s * P + r], qk[:, 1, j, lo:hi],
                                         start=part == 0, stop=part == 2)
                last.then_inc(scores_done, 1)

            def values(b, n):
                if values_at(n) is None:
                    return
                G, part = values_at(n)
                h, g = divmod(G, GROUPS)
                w = sum(rows(2 * g + i) for i in range(2))
                if part == 0:
                    if G:
                        pe.wait_ge(oT_lo, b * H * GROUPS + G)
                    pe.wait_ge(pT_lo, b * STEPS + 2 * G + 2)
                half = NT // 2
                tiles = range(part * half, part * half + half)
                last = split_matmuls(pe, ps6[:, 0:w],
                                     [(v[0:rows(d), 0, d, h * P:(h + 1) * P], v[0:rows(d), 1, d, h * P:(h + 1) * P]) for d in tiles],
                                     [(pTv[G % 2][0:rows(d), 0, d, 0:w], pTv[G % 2][0:rows(d), 1, d, 0:w]) for d in tiles],
                                     start=part == 0, stop=part == 1)
                if part:
                    last.then_inc(values_done, 1)

            def transpose(b, n):
                r = rows(n % NT)
                if n:
                    pe.wait_ge(pT_lo, b * STEPS + n)
                pe.wait_ge(exp_done, b * STEPS + n + 1)
                for d in range(NT):
                    last = pe.transpose(psB[:, d * P:d * P + r], pr[0:r, n % 2, d * P:(d + 1) * P], ident[0:r, 0:r])
                last.then_inc(pT_done, 1)

            def output(b, n):
                if output_at(n) is None:
                    return
                G, i = output_at(n)
                h, g = divmod(G, GROUPS)
                r = rows(2 * g + i)
                if n > 5:
                    pe.wait_ge(out_added, b * STEPS + 2 * G + i)
                if i == 0:
                    pe.wait_ge(oT_lo, b * H * GROUPS + G + 1)
                split_matmuls(pe, ps7[0:r, :], [(oT[:, 0, i * P:i * P + r], oT[:, 1, i * P:i * P + r])],
                              [(w_o[:, 0, h, :], w_o[:, 1, h, :])]).then_inc(out_done, 1)

            def body(b, last):
                names = block_loads(last)
                for n in range(DRAIN):
                    boundary = n % NT == 0 and n < STEPS
                    if boundary:
                        project(b, n // NT)
                    elif n < STEPS:
                        scores(b, n)
                    if 1 <= n <= STEPS:
                        transpose(b, n - 1)
                    values(b, n)
                    if boundary:
                        scores(b, n)
                    output(b, n)
                    if n >= DRAIN - TICKS_EARLY:
                        if n == DRAIN - TICKS_EARLY:
                            pe.wait_ge(stage_lo, loads_before(b) + names.index("cond2") + 1)
                        second_half(b, tick(n - (DRAIN - TICKS_EARLY), NT), last)
                second_half(b, mlp_sequence(last), last)

            def second_half(b, items, last):
                names = block_loads(last)
                for kind, k in items:
                    wc = wc2 if k < NT else wc1
                    if kind == "norm":
                        if k == NT:
                            pe.wait_ge(stage_lo, loads_before(b) + names.index("cond1") + 1)
                        norm(k, norms_before(b), wc)
                    elif kind == "turn":
                        turn(k, norms_before(b), wc)
                    elif kind == "up":
                        c, j = divmod(k, KD)
                        lo, hi = COLS[c]
                        if j == 0:
                            pe.wait_ge(yT_lo, norms_before(b) + min(4 * c + 4, NT))
                        if k >= 2:
                            pe.wait_ge(relu_done, b * 3 * KD + k - 1)
                        split_matmuls(pe, up_bank[k % 2][:, 0:hi - lo],
                                      [(w_1[:, 0, i, j * P:(j + 1) * P], w_1[:, 1, i, j * P:(j + 1) * P]) for i in range(KD)],
                                      [(yT[:, 0, i, lo:hi], yT[:, 1, i, lo:hi]) for i in range(KD)]).then_inc(up_done, 1)
                    elif kind == "down":
                        c, r = k // KD, rows(k)
                        if k >= 2:
                            pe.wait_ge(down_added, b * NT + k - 1)
                        if k % KD == 0:
                            pe.wait_ge(hid_lo, b * 3 * KD + (c + 1) * KD)
                        at = (k % KD) * P
                        split_matmuls(pe, down_bank[k % 2][0:r, :],
                                      [(v[:, 0, (c % 2) * KD + i, at:at + r], v[:, 1, (c % 2) * KD + i, at:at + r]) for i in range(KD)],
                                      [(w_2[:, 0, i, :], w_2[:, 1, i, :]) for i in range(KD)]).then_inc(down_done, 1)

            with pe.Fori(0, B - 1) as b:
                body(b, False)
            body(B - 1, True)


class Kept:
    pass


def kept(nc, ctx):
    k = Kept()

    def sb(name, shape, dt):
        return ctx.enter_context(nc.sbuf_tensor(name, shape, dt))

    k.x = sb("x", [P, NT, D], F32)
    k.edges = sb("edges", [P, NT, N], F32)
    k.cond = sb("cond", [P, NPAD], F16)
    k.ident = sb("ident", [P, P], F32)
    k.const = sb("const", [P, N_CONST], F32)
    k.mhalf = sb("mhalf", [P, 1], F32)
    return k


def build(nc, io):
    io["x_scratch"] = nc.dram_tensor("x_scratch", (NPAD, D), F32).ap()
    ctx = ExitStack()
    with ctx:
        keep = kept(nc, ctx)
        graph_layer(nc, io, keep)
        transformer(nc, io, keep)


def arrays(inputs):
    import numpy as np
    a = {k: np.ascontiguousarray(v) for k, v in inputs.items()}
    g, b = "L0_gnn_", "L1_gnn_"
    const = np.zeros((P, N_CONST), np.float32)
    const[0:2 * FREQ, C_FREQ] = np.tile(np.arange(1, FREQ + 1) / 16.0, 2)
    const[FREQ:2 * FREQ, C_PHASE] = 0.25
    const[CE::32, C_ONE] = 1.0
    const[:, C_TLO] = P * np.arange(P)
    const[:, C_THI] = P * np.arange(1, P + 1)
    const[0:NT, C_LOWER:C_LOWER + NT] = np.triu(np.ones((NT, NT)), 1)
    t = lambda v: np.ascontiguousarray(v.T)
    cols = lambda v: v.reshape(B, KD, P).transpose(0, 2, 1)

    def norm_weights(n):
        parts = [np.concatenate([a[b + f"{m}{n}_w"], a[b + f"{m}{n}_b"][:, None, :]], axis=1) for m in "sb"]
        return np.ascontiguousarray(np.concatenate(parts, axis=2))

    return {
        "x": a["x"], "xT": t(a["x"]), "src": a["src"], "dst": a["dst"], "noise": a["node_vec1"].reshape(N),
        "w_self_T": t(a[g + "w_self"]), "w_neigh_T": t(a[g + "w_neigh"]),
        "bias": a[g + "bias"], "gamma": a[g + "gamma"], "beta": a[g + "beta"],
        "f_w1": a[b + "f_w1"], "f_b1": a[b + "f_b1"], "f_w2": a[b + "f_w2"], "f_b2": a[b + "f_b2"],
        "const": const, "ident": np.eye(P, dtype=np.float32), "iota": np.arange(N).astype(np.float16),
        "quad_no": (np.arange(NQUAD * SLOTS) // SLOTS).astype(np.float32),
        "w_cond1": norm_weights("1"), "w_cond2": norm_weights("2"),
        "wq": a[b + "wq"], "wk": a[b + "wk"], "wv": a[b + "wv"], "wo": a[b + "wo"],
        "m_w1": a[b + "m_w1"], "m_w2": a[b + "m_w2"],
        "bias_cols": np.ascontiguousarray(np.concatenate([cols(a[b + n]) for n in ("bq", "bk", "m_b1")], axis=2)),
        "bv": a[b + "bv"], "bo": a[b + "bo"], "b2": a[b + "m_b2"],
    }


def kernel(**inputs):
    import numpy as np
    import concourse.bacc as bacc
    from concourse.bass_utils import run_bass_kernel_spmd

    nc = bacc.Bacc("TRN2", target_bir_lowering=False, num_devices=1)
    given = arrays({k: np.asarray(v) for k, v in inputs.items()})
    io = {
        k: nc.dram_tensor(f"in_{k}", v.shape, mybir.dt.from_np(v.dtype), kind="ExternalInput").ap()
        for k, v in given.items()}
    io["out"] = nc.dram_tensor("out", (N, D), F32, kind="ExternalOutput").ap()
    build(nc, io)
    r = run_bass_kernel_spmd(nc, [{f"in_{k}": v for k, v in given.items()}], core_ids=[0])
    return r.results[0]["out"]
```

```python
import concourse.bass as bass
from concourse import mybir
from contextlib import ExitStack

F32 = mybir.dt.float32
F16 = mybir.dt.float16
I32 = mybir.dt.int32
ALU = mybir.AluOpType
ACT = mybir.ActivationFunctionType
AX = mybir.AxisListType

P = 128
N = 1250
NT = (N + P - 1) // P
TAIL = N - (NT - 1) * P
NPAD = NT * P
D = 512
KD = D // P
E = 40000
NCH = (E + P - 1) // P
SLOTS = 4
NQUAD = (NCH + SLOTS - 1) // SLOTS
NSEG = 4
NG = (NCH + P - 1) // P
B = 4
H = 4
FREQ = 32
CE = 16
EPS = 1e-5
WS = 32.0
TINY = 1e-20
MAGIC = 1.5 * 2.0 ** 23
NOEDGE = -1e34
KAPPA = WS * WS * float(P) ** 0.5
COLS = [(0, 512), (512, 1024), (1024, N)]
COLS_PAD = [(0, 512), (512, 1024), (1024, NPAD)]

C_FREQ, C_PHASE, C_ONE, C_TLO, C_THI, C_LOWER = 0, 1, 2, 3, 4, 5
N_CONST = C_LOWER + NT


def rows(t):
    return TAIL if t == NT - 1 else P


def split_matmuls(pe, out, stationary, moving, start=True, stop=True):
    n = len(stationary)
    for k in range(n):
        (ah, al), (bh, bl) = stationary[k], moving[k]
        pe.matmul(out, ah, bh, start=start and k == 0, stop=False)
        pe.matmul(out, ah, bl, start=False, stop=False)
        last = pe.matmul(out, al, bh, start=False, stop=stop and k == n - 1)
    return last


def in_register(eng, count):
    return count if isinstance(count, int) else eng.compute_val(count)


def segments_of(nc, eng, first, size, end, most):
    bounds = [first + size * k for k in range(1, NSEG)]
    inner = [eng.snap(nc.s_assert_within(v, k, most - NSEG + k, skip_runtime_bounds_check_because="segments fill the span"))
             for k, v in enumerate(bounds, start=1)]
    return [first] + inner + [end]


def graph_layer(nc, io, keep):
    ctx = ExitStack()
    with ctx:
        def sb(name, shape, dt):
            return ctx.enter_context(nc.sbuf_tensor(name, shape, dt))

        def ps(name, n):
            return ctx.enter_context(nc.psum_tensor(name, [P, n], F32))

        def sem(name):
            return ctx.enter_context(nc.semaphore(name))

        x, edges, cond, ident, mhalf = keep.x, keep.edges, keep.cond, keep.ident, keep.mhalf
        const = keep.const

        iota = sb("iota", [P, N], F16)
        ids_raw = sb("ids_raw", [P, 2, NG, P], I32)
        ids_row = sb("ids_row", [P, 2, NG, P], F32)
        ids = sb("ids", [P, 2, NG * P], F32)
        span = sb("span", [P, 2, NG], F32)
        span10 = sb("span10", [P, 2, NG, NT], F32)
        spanT = sb("spanT", [NT, 2, NQUAD * SLOTS], F32)
        quad_no = sb("quad_no", [NT, NQUAD * SLOTS], F32)
        inside = sb("inside", [NT, NQUAD * SLOTS], F32)
        lohi = sb("lohi", [NT, 8], F32)
        ranges_f = sb("ranges_f", [1, 6, NT], F32)
        ranges = sb("ranges", [1, 6, NT], I32)
        zeros = sb("zeros", [P, 512], F16)
        oh_src = sb("oh_src", [P, SLOTS, N], F16)
        oh_dst = sb("oh_dst", [P, SLOTS, P], F16)
        c_rows = sb("c_rows", [P, NPAD], F32)
        c_hi = sb("c_hi", [P, NT, P], F16)
        c_lo = sb("c_lo", [P, NT, P], F16)
        x_hi = sb("x_hi", [P, NT, D], F16)
        x_lo = sb("x_lo", [P, NT, D], F16)
        xT_hi = sb("xT_hi", [P, KD, NPAD], F16)
        xT_lo = sb("xT_lo", [P, KD, NPAD], F16)
        stage = sb("stage", [P, KD * N], F32)
        w_hi = sb("w_hi", [P, 2, KD, D], F16)
        w_lo = sb("w_lo", [P, 2, KD, D], F16)
        mean = sb("mean", [P, D], F32)
        mT_hi = sb("mT_hi", [P, KD, P], F16)
        mT_lo = sb("mT_lo", [P, KD, P], F16)
        degree = sb("degree", [P, 2], F32)
        vecs = sb("vecs", [P, 3, D], F32)
        h = sb("h", [P, D], F32)
        hn = sb("hn", [P, D], F32)
        bn = sb("bn", [P, 2, 6], F32)
        mv = sb("mv", [P, 2, 2], F32)
        rstd = sb("rstd", [P, 2, 4], F32)
        noise = sb("noise", [2 * FREQ, NPAD], F32)
        turns = c_rows[0:2 * FREQ, :]
        f1 = sb("f1", [2 * FREQ, CE], F32)
        fb1 = sb("fb1", [CE, 1], F32)
        f2 = sb("f2", [CE, P], F32)
        fb2 = sb("fb2", [P, 1], F32)

        cond_raw = stage[:, KD * D:KD * D + NPAD]
        tiny = sb("tiny", [P, 2], F32)
        no_edge = stage[:, 0:NT * P].rearrange("p (s c) -> p s c", c=P)

        bank = [ps(f"a_bank{i}", 512) for i in range(2)]
        p_cnt = ps("p_cnt", 3 * 512)
        p_t = ps("p_t", 3 * 512)

        ld_const, ld_ids, ld_noise, ld_f, ld_x, ld_xT, ld_w, ld_vec = (
            sem(n) for n in ("ld_const", "ld_ids", "ld_noise", "ld_f", "ld_x", "ld_xT", "ld_w", "ld_vec"))
        pad_rows = sem("pad_rows")
        padded = sem("padded")
        dv = sem("a_dv")
        rows_ready, ids_T, ids_ready, span_ready, span_T, lohi_ready, lohi_T, ranges_ready = (
            sem(n) for n in ("rows_ready", "ids_T", "ids_ready", "span_ready", "span_T", "lohi_ready",
                             "lohi_T", "ranges_ready"))
        angle_ready, emb_ready, f1_done, z_ready, e_ready, silu_ready, f2_done = (
            sem(n) for n in ("angle_ready", "emb_ready", "f1_done", "z_ready", "e_ready", "silu_ready", "f2_done"))
        ac = sem("a_ac")
        split_done = sem("split_done")
        stage_free = sem("stage_free")
        onehots, counted = sem("onehots"), sem("counted")
        cnt_done, rows_copied = sem("cnt_done"), sem("rows_copied")
        logs_done, no_edge_done, scores_set = sem("logs_done"), sem("no_edge_done"), sem("scores_set")
        c_T, c_hi_done, c_lo_done = sem("c_T"), sem("c_hi_done"), sem("c_lo_done")
        agg_done, mean_done, m_T, mT_hi_done, mT_lo_done = (
            sem(n) for n in ("agg_done", "mean_done", "m_T", "mT_hi_done", "mT_lo_done"))
        h_done, h_free = sem("h_done"), sem("h_free")
        deg_done, bn0_done, bn1_done, sum_done = (sem(n) for n in ("deg_done", "bn0_done", "bn1_done", "sum_done"))
        stat0, rstd0, norm0, affine0, stat1, rstd1, x1_done = (
            sem(n) for n in ("stat0", "rstd0", "norm0", "affine0", "stat1", "rstd1", "x1_done"))
        cond_read = sem("cond_read")
        gp = sem("a_gp")

        block = ctx.enter_context(nc.Block())

        @block.sync
        def _(sp):
            sp.wait_ge(padded, 5)
            for i, ids_in in enumerate((io["src"], io["dst"])):
                whole = (NG - 1) * P * P
                sp.dma_start(ids_raw[:, i, 0:NG - 1, :],
                             ids_in[0:whole].rearrange("(g c e) -> c g e", g=NG - 1, e=P)).then_inc(ld_ids, 16)
                full = (E - whole) // P
                sp.dma_start(ids_raw[0:full, i, NG - 1, :],
                             ids_in[whole:whole + full * P].rearrange("(c e) -> c e", e=P)).then_inc(ld_ids, 16)
                rest = E - whole - full * P
                sp.dma_start(ids_raw[full:full + 1, i, NG - 1, 0:rest],
                             ids_in[E - rest:E].rearrange("(c e) -> c e", c=1)).then_inc(ld_ids, 16)
                if i == 1:
                    sp.dma_start(ids_raw[full:full + 1, i, NG - 1, rest:P],
                                 ids_in[E - (P - rest):E].rearrange("(c e) -> c e", c=1)).then_inc(ld_ids, 16)
            sp.dma_start(f1[:], io["f_w1"]).then_inc(ld_f, 16)
            sp.dma_start(fb1[:], io["f_b1"].rearrange("(p a) -> p a", a=1)).then_inc(ld_f, 16)
            for q in range(4):
                sp.dma_start(f2[:, 32 * q:32 * q + CE], io["f_w2"]).then_inc(ld_f, 16)
                sp.dma_start(fb2[32 * q:32 * q + CE, :], io["f_b2"].rearrange("(p a) -> p a", a=1)).then_inc(ld_f, 16)
            sp.dma_start(stage[:].rearrange("p (k n) -> p k n", k=KD),
                         io["xT"].rearrange("(k p) n -> p k n", p=P)).then_inc(ld_xT, 16)
            sp.dma_start(x[:, 0:NT - 1, :], io["x"][0:(NT - 1) * P, :].rearrange("(t p) d -> p t d", p=P)).then_inc(ld_x, 16)
            sp.dma_start(x[0:TAIL, NT - 1, :], io["x"][(NT - 1) * P:N, :]).then_inc(ld_x, 16)
            for i, w in enumerate((io["w_self_T"], io["w_neigh_T"])):
                sp.wait_ge(stage_free, i + 1)
                sp.dma_start(stage[:, 0:KD * D].rearrange("p (k d) -> p k d", k=KD),
                             w.rearrange("(k p) d -> p k d", p=P)).then_inc(ld_w, 16)

        @block.gpsimd
        def _(pool):
            pool.memset(ids_raw[:], -1).then_inc(padded, 1)
            pool.memset(noise[:, N:NPAD], 0.0).then_inc(padded, 1)
            pool.memset(f2[:], 0.0).then_inc(padded, 1)
            pool.memset(fb2[:], 0.0).then_inc(padded, 1)
            pool.memset(x[:, NT - 1, :], 0.0).then_inc(padded, 1)
            pool.memset(zeros[:], 0.0).then_inc(padded, 1)
            pool.memset(xT_hi[:, :, N:NPAD], 0.0).then_inc(padded, 1)
            pool.memset(xT_lo[:, :, N:NPAD], 0.0).then_inc(padded, 1)
            pool.memset(tiny[:, 0:1], TINY).then_inc(padded, 1)
            pool.memset(tiny[:, 1:2], 1.0).then_inc(padded, 1)
            pool.memset(mhalf[:], -0.5).then_inc(gp, 1)

            pool.wait_ge(ac, 1)
            pool.tensor_tensor(xT_lo[:, :, 0:N], stage[:].rearrange("p (k n) -> p k n", k=KD), xT_hi[:, :, 0:N],
                               ALU.subtract).then_inc(stage_free, 1)
            pool.wait_ge(ac, 2)
            pool.tensor_tensor(x_lo[:], x[:], x_hi[:], ALU.subtract).then_inc(split_done, 1)

            pool.wait_ge(gp, 1)
            pool.wait_ge(ld_vec, 48)
            for t in range(NT):
                for i, (stat, done) in enumerate(((stat0, rstd0), (stat1, rstd1))):
                    pool.wait_ge(stat, t + 1)
                    pool.tensor_scalar(rstd[:, i, 0:1], mv[:, i, 1:2], EPS, None, ALU.add).then_inc(gp, 1)
                    pool.wait_ge(gp, 2 + 5 * t + 2 * i + (i == 1))
                    pool.tensor_tensor(rstd[:, i, 1:2], rstd[:, i, 0:1], mhalf[:, 0:1], ALU.pow).then_inc(gp, 1)
                    pool.wait_ge(gp, 3 + 5 * t + 2 * i + (i == 1))
                    pool.tensor_scalar(rstd[:, i, 2:3], mv[:, i, 0:1], rstd[:, i, 1:2], -1.0, ALU.mult,
                                       ALU.mult).then_inc(done, 1)
                    if i == 0:
                        pool.wait_ge(norm0, t + 1)
                        pool.tensor_tensor(hn[:], hn[:], vecs[:, 1, :], ALU.mult).then_inc(gp, 1)
                        pool.wait_ge(gp, 4 + 5 * t)
                        pool.tensor_tensor(hn[:], hn[:], vecs[:, 2, :], ALU.add).then_inc(affine0, 1)

        @block.scalar
        def _(act):
            act.dma_start(const[:], io["const"]).then_inc(ld_const, 16)
            act.dma_start(ident[:], io["ident"]).then_inc(ld_const, 16)
            act.dma_start(iota[:], io["iota"].partition_broadcast(P)).then_inc(ld_const, 16)
            act.dma_start(quad_no[:], io["quad_no"].partition_broadcast(NT)).then_inc(ld_const, 16)
            act.wait_ge(padded, 2)
            act.dma_start(noise[:, 0:N], io["noise"].partition_broadcast(2 * FREQ)).then_inc(ld_noise, 16)
            for i, v in enumerate((io["bias"], io["gamma"], io["beta"])):
                act.dma_start(vecs[:, i, :], v.partition_broadcast(P)).then_inc(ld_vec, 16)

            act.wait_ge(angle_ready, 1)
            act.activation(noise[:], turns[:], ACT.Sin, scale=6.283185307179586).then_inc(emb_ready, 1)
            act.wait_ge(ld_xT, 16)
            act.wait_ge(padded, 10)
            act.activation(xT_hi[:, :, 0:N], stage[:].rearrange("p (k n) -> p k n", k=KD), ACT.Copy).then_inc(ac, 1)
            act.wait_ge(ld_x, 32)
            act.activation(x_hi[:], x[:], ACT.Copy).then_inc(ac, 1)
            act.wait_ge(z_ready, 1)
            act.activation(turns[0:CE, :], noise[0:CE, :], ACT.Exp, scale=-1.0).then_inc(e_ready, 1)
            act.wait_ge(e_ready, 1)
            act.activation(turns[0:CE, :], turns[0:CE, :], ACT.Ln, bias=tiny[0:CE, 1:2]).then_inc(e_ready, 1)
            act.wait_ge(e_ready, 2)
            act.activation(turns[0:CE, :], turns[0:CE, :], ACT.Exp, scale=-1.0).then_inc(e_ready, 1)
            for i in range(2):
                act.wait_ge(ld_w, 16 * (i + 1))
                act.activation(w_hi[:, i], stage[:, 0:KD * D].rearrange("p (k d) -> p k d", k=KD), ACT.Copy,
                               scale=WS).then_inc(ac, 1)
            act.wait_ge(pad_rows, 1)

            def iteration(t, counts=True, mid=True, old=True):
                u = t - 1
                if mid:
                    act.wait_ge(c_T, t)
                    w = TAIL if isinstance(u, int) and u == NT - 1 else P
                    by_src = p_t[:, 0:NPAD].rearrange("p (s c) -> p s c", c=P)
                    act.activation(edges[:, :, bass.ds(u * P, w)], by_src[:, :, 0:w], ACT.Ln,
                                   bias=tiny[:, 0:1]).then_inc(logs_done, 1)
                    act.activation(c_hi[:], by_src, ACT.Copy).then_inc(c_hi_done, 1)
                if old:
                    act.wait_ge(rstd0, t - 1)
                    act.activation(hn[:], h[:], ACT.Identity, bias=rstd[:, 0, 2:3], scale=rstd[:, 0, 1:2]).then_inc(norm0, 1)
                if mid:
                    act.wait_ge(deg_done, u * 2 + 2)
                    act.wait_ge(agg_done, t)
                    act.activation(mean[:], bank[0][:], ACT.Copy, scale=degree[:, 1:2]).then_inc(mean_done, 1)
                    act.wait_ge(m_T, t)
                    act.activation(mT_hi[:], p_t[:, 0:D].rearrange("p (k c) -> p k c", k=KD), ACT.Copy).then_inc(mT_hi_done, 1)
                if counts:
                    act.wait_ge(cnt_done, t + 1)
                    act.activation(c_rows[:, 0:N], p_cnt[:, 0:N], ACT.Identity,
                                   accum_out=degree[:, 0:1]).then_inc(rows_copied, 1)
                if old:
                    act.wait_ge(rstd1, t - 1)
                    act.activation(x[:, bass.ds(t - 2, 1), :], hn[:].unsqueeze(1), ACT.Identity, bias=rstd[:, 1, 2:3],
                                   scale=rstd[:, 1, 1:2]).then_inc(x1_done, 1)
                    act.wait_ge(x1_done, t - 1)

            iteration(0, mid=False, old=False)
            iteration(1, old=False)
            with act.Fori(2, NT) as t:
                iteration(t)
            iteration(NT, counts=False)
            iteration(NT + 1, counts=False, mid=False)

        @block.vector
        def _(dve):
            chain = [0]

            def link(ins):
                chain[0] += 1
                ins.then_inc(dv, 1)
                dve.wait_ge(dv, chain[0])

            dve.wait_ge(ld_ids, 16 * 7)
            dve.tensor_copy(ids_row[:], ids_raw[:]).then_inc(rows_ready, 1)
            dve.wait_ge(rows_ready, 1)
            link(dve.tensor_reduce(span[:, 0, :], ids_row[:, 1], AX.X, ALU.min))
            link(dve.tensor_reduce(span[:, 1, :], ids_row[:, 1], AX.X, ALU.max))
            for i in range(2):
                for g in range(NG):
                    last = dve.tensor_copy(span10[:, i, g, :], span[:, i, g:g + 1].to_broadcast([P, NT]))
            last.then_inc(span_ready, 1)
            dve.wait_ge(ld_const, 64)
            nf = 2 * FREQ
            dve.wait_ge(ld_noise, 16)
            link(dve.tensor_scalar(turns[:], noise[:], const[0:nf, C_FREQ:C_FREQ + 1], None, ALU.mult))
            link(dve.tensor_scalar(noise[:], turns[:], MAGIC, MAGIC, ALU.add, ALU.subtract))
            link(dve.tensor_tensor(turns[:], turns[:], noise[:], ALU.subtract))
            link(dve.tensor_scalar(turns[:], turns[:], const[0:nf, C_PHASE:C_PHASE + 1], None, ALU.add))
            link(dve.tensor_scalar(noise[:], turns[:], MAGIC, MAGIC, ALU.add, ALU.subtract))
            link(dve.tensor_tensor(turns[:], turns[:], noise[:], ALU.subtract))
            half = 0.49999994
            dve.tensor_scalar(turns[:], turns[:], half, -half, ALU.min, ALU.max).then_inc(angle_ready, 1)
            for i in range(2):
                dve.wait_ge(ids_T, i + 1)
                last = dve.tensor_copy(ids[:, i, :], bank[i][:, 0:NG * P])
                last.then_inc(ids_ready, 1)
            dve.wait_ge(ld_const, 64)
            dve.wait_ge(span_T, 2)
            for i in range(2):
                link(dve.tensor_copy(spanT[:, i, :], bank[i][0:NT, 0:NQUAD * SLOTS]))
            link(dve.tensor_scalar(inside[:], spanT[:, 1, :], const[0:NT, C_TLO:C_TLO + 1], None, ALU.is_ge))
            link(dve.scalar_tensor_tensor(spanT[:, 0, :], spanT[:, 0, :], const[0:NT, C_THI:C_THI + 1], inside[:],
                                          ALU.is_lt, ALU.mult))
            link(dve.scalar_tensor_tensor(spanT[:, 1, :], quad_no[:], 1.0, spanT[:, 0, :], ALU.add, ALU.mult))
            link(dve.tensor_scalar(inside[:], quad_no[:], 1000.0, None, ALU.add))
            link(dve.scalar_tensor_tensor(inside[:], spanT[:, 0, :], -1000.0, inside[:], ALU.mult, ALU.add))
            link(dve.tensor_reduce(lohi[:, 0:1], inside[:], AX.X, ALU.min))
            link(dve.tensor_reduce(lohi[:, 1:2], spanT[:, 1, :], AX.X, ALU.max))
            link(dve.tensor_scalar(lohi[:, 1:2], lohi[:, 1:2], float(NSEG), None, ALU.max))
            link(dve.tensor_scalar(lohi[:, 3:4], lohi[:, 1:2], -float(NSEG), None, ALU.add))
            link(dve.tensor_tensor(lohi[:, 0:1], lohi[:, 0:1], lohi[:, 3:4], ALU.min))
            link(dve.tensor_tensor(lohi[:, 2:3], lohi[:, 1:2], lohi[:, 0:1], ALU.subtract))
            link(dve.tensor_scalar(lohi[:, 3:4], lohi[:, 2:3], 1.0 / NSEG, 0.5 / NSEG - 0.5, ALU.mult, ALU.add))
            dve.tensor_scalar(lohi[:, 3:4], lohi[:, 3:4], MAGIC, MAGIC, ALU.add, ALU.subtract).then_inc(lohi_ready, 1)
            dve.wait_ge(lohi_T, 1)
            link(dve.tensor_copy(ranges_f[:, 0:4, :], bank[0][0:1, 0:4 * NT].rearrange("p (a t) -> p a t", a=4)))
            link(dve.tensor_tensor(ranges_f[:, 4, :], ranges_f[:, 2, :], ranges_f[:, 0, :], ALU.subtract))
            link(dve.tensor_tensor(ranges_f[:, 5, :], ranges_f[:, 4, :], ranges_f[:, 1, :], ALU.add))
            dve.tensor_copy(ranges[:], ranges_f[:]).then_inc(ranges_ready, 1)

            def segment(bounds, before, k):
                with dve.Fori(bounds[k], bounds[k + 1]) as i:
                    for slot in range(SLOTS):
                        dve.wait_ge(counted, (i + before) * SLOTS + (slot + 1))
                        dve.tensor_scalar(oh_src[:, slot, :], iota[:], ids[:, 0, bass.ds(i * SLOTS + slot, 1)], None,
                                          ALU.is_equal)
                        dve.tensor_scalar(oh_dst[:, slot, :], iota[:, 0:P], ids[:, 1, bass.ds(i * SLOTS + slot, 1)], None,
                                          ALU.is_equal).then_inc(onehots, 1)

            def next_ids(bounds, before):
                dve.wait_ge(onehots, (bounds[NSEG] + before) * SLOTS)
                dve.tensor_scalar(ids[:, 1, :], ids[:, 1, :], float(P), None, ALU.subtract).then_inc(ids_ready, 1)

            def counts_split(u):
                dve.wait_ge(rows_copied, u + 1)
                dve.tensor_scalar(degree[:, 1:2], degree[:, 0:1], 1.0, None, ALU.max).then_inc(deg_done, 1)
                dve.wait_ge(deg_done, u * 2 + 1)
                dve.reciprocal(degree[:, 1:2], degree[:, 1:2]).then_inc(deg_done, 1)
                dve.wait_ge(c_hi_done, u + 1)
                dve.tensor_tensor(c_lo[:], p_t[:, 0:NPAD].rearrange("p (s c) -> p s c", c=P), c_hi[:],
                                  ALU.subtract).then_inc(c_lo_done, 1)

            def edge_scores(u):
                w = TAIL if isinstance(u, int) and u == NT - 1 else P
                e = edges[:, :, bass.ds(u * P, w)]
                dve.wait_ge(logs_done, u + 1)
                dve.tensor_scalar(no_edge[:, :, 0:w], e, 0.0, -NOEDGE / 40, ALU.min, ALU.mult).then_inc(no_edge_done, 1)
                dve.wait_ge(no_edge_done, u + 1)
                dve.scalar_tensor_tensor(e, e, KAPPA, no_edge[:, :, 0:w], ALU.mult, ALU.add).then_inc(scores_set, 1)

            def mean_split(u):
                dve.wait_ge(mT_hi_done, u + 1)
                dve.tensor_tensor(mT_lo[:], p_t[:, 0:D].rearrange("p (k c) -> p k c", k=KD), mT_hi[:],
                                  ALU.subtract).then_inc(mT_lo_done, 1)

            def layer(u):
                dve.wait_ge(h_done, u + 1)
                dve.scalar_tensor_tensor(h[:], bank[1][:], 1.0 / WS, vecs[:, 0, :], ALU.mult, ALU.add).then_inc(h_free, 1)
                dve.wait_ge(h_free, u + 2)
                dve.bn_stats(bn[:, 0, :], h[:]).then_inc(bn0_done, 1)
                dve.wait_ge(ld_vec, 48)
                dve.wait_ge(bn0_done, u + 1)
                dve.bn_aggr(mv[:, 0, :], bn[:, 0, :]).then_inc(stat0, 1)

            def finish(u):
                dve.wait_ge(affine0, u + 1)
                dve.scalar_tensor_tensor(hn[:].unsqueeze(1), hn[:].unsqueeze(1), 0.0, x[:, bass.ds(u, 1), :], ALU.max,
                                         ALU.add).then_inc(sum_done, 1)
                dve.wait_ge(sum_done, u + 1)
                dve.bn_stats(bn[:, 1, :], hn[:]).then_inc(bn1_done, 1)
                dve.wait_ge(ld_vec, 48)
                dve.wait_ge(bn1_done, u + 1)
                dve.bn_aggr(mv[:, 1, :], bn[:, 1, :]).then_inc(stat1, 1)

            def silu_input():
                dve.wait_ge(ld_f, 160)
                dve.wait_ge(f1_done, 1)
                dve.tensor_scalar(noise[0:CE, :], p_t[0:CE, 0:NPAD], fb1[:, 0:1], None, ALU.add).then_inc(z_ready, 1)

            def silu():
                dve.wait_ge(e_ready, 3)
                dve.tensor_tensor(turns[0:CE, :], turns[0:CE, :], noise[0:CE, :], ALU.mult).then_inc(silu_ready, 1)

            def weights_low(i):
                dve.wait_ge(ac, 3 + i)
                dve.scalar_tensor_tensor(w_lo[:, i], stage[:, 0:KD * D].rearrange("p (k d) -> p k d", k=KD), WS,
                                         w_hi[:, i], ALU.mult, ALU.subtract).then_inc(stage_free, 1)

            def conditioning():
                link(dve.tensor_tensor(fb2[:], fb2[:], const[:, C_ONE:C_ONE + 1], ALU.add))
                dve.wait_ge(f2_done, 1)
                dve.tensor_scalar(cond_raw, p_t[:, 0:NPAD], fb2[:, 0:1], None, ALU.add).then_inc(cond_read, 1)
                dve.memset(c_rows[:, N:NPAD], 0.0).then_inc(pad_rows, 1)

            def conditioning_halves():
                dve.wait_ge(cond_read, 1)
                dve.tensor_copy(cond[:], cond_raw).then_inc(cond_read, 1)
                dve.wait_ge(cond_read, 2)
                for q in (1, 3):
                    r = slice(32 * q, 32 * q + 32)
                    dve.tensor_tensor(cond[r, :], cond_raw[r, :], cond[r, :], ALU.subtract).then_inc(cond_read, 1)

            def iteration(t, counts=True, mid=True, old=True):
                first = isinstance(t, int) and t == 0
                if counts:
                    first_quad = dve.value_load(ranges[0:1, 0, bass.ds(t, 1)], min_val=0, max_val=NQUAD - NSEG)
                    end = dve.value_load(ranges[0:1, 1, bass.ds(t, 1)], min_val=NSEG, max_val=NQUAD)
                    size = dve.value_load(ranges[0:1, 3, bass.ds(t, 1)], min_val=1, max_val=NQUAD // NSEG)
                    before = dve.value_load(ranges[0:1, 4, bass.ds(t, 1)], min_val=0, max_val=NQUAD * NT)
                    bounds = segments_of(nc, dve, first_quad, size, end, NQUAD)
                    count = in_register(dve, t + 2)
                    dve.wait_ge(ld_const, 64)
                    dve.wait_ge(ids_ready, count)
                    segment(bounds, before, 0)
                if first:
                    silu_input()
                if mid:
                    counts_split(t - 1)
                if counts:
                    segment(bounds, before, 1)
                if first:
                    silu()
                if isinstance(t, int) and t == 1:
                    weights_low(1)
                if old:
                    layer(t - 2)
                if counts:
                    segment(bounds, before, 2)
                if first:
                    weights_low(0)
                if counts:
                    segment(bounds, before, 3)
                    next_ids(bounds, before)
                if first:
                    conditioning()
                if isinstance(t, int) and t == 1:
                    conditioning_halves()
                if mid:
                    mean_split(t - 1)
                    edge_scores(t - 1)
                if old:
                    finish(t - 2)

            dve.wait_ge(ld_vec, 48)
            dve.wait_ge(padded, 10)
            dve.memset(degree[:], 0.0).then_inc(h_free, 1)
            dve.wait_ge(ranges_ready, 1)
            iteration(0, mid=False, old=False)
            iteration(1, old=False)
            with dve.Fori(2, NT) as t:
                iteration(t)
            iteration(NT, counts=False)
            iteration(NT + 1, counts=False, mid=False)

        @block.tensor
        def _(pe):
            pe.wait_ge(rows_ready, 1)
            pe.wait_ge(ld_const, 64)
            for i in range(2):
                for g in range(NG):
                    last = pe.transpose(bank[i][:, g * P:(g + 1) * P], ids_row[:, i, g, :], ident[:])
                last.then_inc(ids_T, 1)
            pe.wait_ge(span_ready, 1)
            pe.wait_ge(ids_ready, 2)
            for i in range(2):
                for g in range(NG):
                    last = pe.matmul(bank[i][0:NT, g * P:(g + 1) * P], span10[:, i, g, :], ident[:], start=True, stop=True)
                last.then_inc(span_T, 1)
            pe.wait_ge(lohi_ready, 1)
            for i in (0, 1, 3):
                pe.matmul(bank[0][0:1, i * NT:(i + 1) * NT], lohi[:, i:i + 1], ident[0:NT, 0:NT], start=True, stop=True)
            pe.matmul(bank[0][0:1, 2 * NT:3 * NT], lohi[:, 2:3], const[0:NT, C_LOWER:C_LOWER + NT], start=True,
                      stop=True).then_inc(lohi_T, 1)
            pe.wait_ge(ld_f, 160)
            pe.wait_ge(emb_ready, 1)
            for a, b in COLS_PAD:
                last = pe.matmul(p_t[0:CE, a:b], f1[:], noise[:, a:b], start=True, stop=True)
            last.then_inc(f1_done, 1)
            pe.wait_ge(ranges_ready, 1)
            pe.wait_ge(padded, 10)

            def clear_counts(last=False):
                for j, (a, b) in enumerate(COLS):
                    m = pe.matmul(p_cnt[:, a:b], zeros[:, 0:P], zeros[:, 0:b - a], start=not last, stop=last)
                return m

            def segment(bounds, k):
                with pe.Fori(bounds[k], bounds[k + 1]) as i:
                    for slot in range(SLOTS):
                        pe.wait_ge(onehots, i * SLOTS + (slot + 1))
                        for a, b in COLS:
                            last = pe.matmul(p_cnt[:, a:b], oh_dst[:, slot, :], oh_src[:, slot, a:b], start=False, stop=False)
                        last.then_inc(counted, 1)

            def neighbours(u):
                pe.wait_ge(c_lo_done, u + 1)
                split_matmuls(pe, bank[0][:], [(c_hi[0:rows(s), s, :], c_lo[0:rows(s), s, :]) for s in range(NT)],
                              [(x_hi[0:rows(s), s, :], x_lo[0:rows(s), s, :]) for s in range(NT)]).then_inc(agg_done, 1)

            def turn_mean(u):
                pe.wait_ge(logs_done, u + 1)
                pe.wait_ge(mean_done, u + 1)
                for k in range(KD):
                    last = pe.transpose(p_t[:, k * P:(k + 1) * P], mean[:, k * P:(k + 1) * P], ident[:])
                last.then_inc(m_T, 1)

            def layer(u):
                pe.wait_ge(h_free, u + 1)
                for k in range(KD):
                    for j, (a, b) in enumerate(((xT_hi, w_hi), (xT_hi, w_lo), (xT_lo, w_hi))):
                        pe.matmul(bank[1][:], a[:, k, bass.ds(u * P, P)], b[:, 0, k, :], start=k == 0 and j == 0, stop=False)
                pe.wait_ge(mT_lo_done, u + 1)
                split_matmuls(pe, bank[1][:], [(mT_hi[:, k, :], mT_lo[:, k, :]) for k in range(KD)],
                              [(w_hi[:, 1, k, :], w_lo[:, 1, k, :]) for k in range(KD)], start=False).then_inc(h_done, 1)

            def turn_counts(t):
                if isinstance(t, int) and t == 0:
                    pe.wait_ge(cond_read, 1)
                pe.wait_ge(rows_copied, t + 1)
                for s in range(NT):
                    last = pe.transpose(p_t[:, s * P:(s + 1) * P], c_rows[:, s * P:(s + 1) * P], ident[:])
                last.then_inc(c_T, 1)

            def iteration(t, counts=True, mid=True):
                first, second = (isinstance(t, int) and t == n for n in (0, 1))
                if counts:
                    start = pe.value_load(ranges[0:1, 2, bass.ds(t, 1)], min_val=0, max_val=NQUAD * NT)
                    size = pe.value_load(ranges[0:1, 3, bass.ds(t, 1)], min_val=1, max_val=NQUAD // NSEG)
                    end = pe.value_load(ranges[0:1, 5, bass.ds(t, 1)], min_val=NSEG, max_val=NQUAD * NT)
                    bounds = segments_of(nc, pe, start, size, end, NQUAD * NT)
                    clear_counts()
                    segment(bounds, 0)
                    segment(bounds, 1)
                if second:
                    pe.wait_ge(split_done, 1)
                if mid:
                    neighbours(t - 1)
                if counts:
                    segment(bounds, 2)
                if first:
                    pe.wait_ge(silu_ready, 1)
                    for a, b in COLS_PAD:
                        last = pe.matmul(p_t[:, a:b], f2[:], turns[0:CE, a:b], start=True, stop=True)
                    last.then_inc(f2_done, 1)
                if mid:
                    turn_mean(t - 1)
                if counts:
                    segment(bounds, 3)
                    clear_counts(last=True).then_inc(cnt_done, 1)
                if second:
                    pe.wait_ge(stage_free, 3)
                if mid:
                    layer(t - 1)
                if counts:
                    turn_counts(t)

            clear_counts()
            clear_counts(last=True).then_inc(counted, SLOTS)
            iteration(0, mid=False)
            iteration(1)
            with pe.Fori(2, NT) as t:
                iteration(t)
            iteration(NT, counts=False)


STEPS = H * NT
GROUPS = (NT + 1) // 2
JOBS = H * 6 + NT
WIDTH = 2 * P
OS = 4.0
LOADS_FIRST = ["cond1", "q0", "q1", "k0", "k1", "bv"]
LOADS_TICKS = [3, 4, 5, 6, 7]
LOADS_STEP = {2: "m20", 4: "m21", 6: "m10", 8: "m11", 10: "cond2"}
LOADS_NEXT = {12: "cond1", 14: "bv", 32: "q0", 34: "q1", 36: "k0", 38: "k1"}
LATE = ["v0", "v1", "o0", "o1"]
JOBS_HELD = 2
JOBS_FIRST = 6 + NT - JOBS_HELD
JOBS_EARLY = 4
TICKS_EARLY = 5


def block_loads(last):
    steps = dict(LOADS_STEP) if last else {**LOADS_STEP, **LOADS_NEXT}
    return [steps[n] for n in sorted(steps)]


LOADS = len(block_loads(False))


def tick(k, start, end):
    return [(stage, i) for stage, i in (("stats", k), ("norm", k - 1), ("turn", k - 2)) if start <= i < end]


def mlp_tick(k):
    return [(stage, i) for stage, i in (("norm", k), ("turn", k - 1)) if 0 <= i < NT]


def early_ticks():
    return [item for k in range(TICKS_EARLY) for item in mlp_tick(k)]


def first_sequence():
    seq = []
    for k in range(NT + 2):
        seq += tick(k, 0, NT)
        if k == 0:
            seq.append(("load", 0))
        if k in LOADS_TICKS:
            seq.append(("load", LOADS_TICKS.index(k) + 1))
        if k >= NT + 2 - JOBS_EARLY:
            seq.append(("job", k - (NT + 2 - JOBS_EARLY)))
        if k >= NT:
            seq.append(("late", k - NT))
    return seq


def mlp_sequence(last):
    def next_tick(k):
        return [] if last else tick(k, NT, 2 * NT)

    seq = mlp_tick(TICKS_EARLY)
    for j in range(KD):
        seq.append(("up", j))
        seq += mlp_tick(TICKS_EARLY + 1 + j)
    for c in range(3):
        if c < 2:
            seq.append(("up", (c + 1) * KD))
        for t in range(4 * c, min(4 * c + 4, NT)):
            seq.append(("down", t))
            if last:
                seq.append(("final", t))
            seq += mlp_tick(TICKS_EARLY + 1 + KD + t)
            seq += next_tick(NT + t)
            if not last and t >= NT - 2:
                seq.append(("job", t - (NT - 2)))
        if c < 2:
            seq += [("up", (c + 1) * KD + j) for j in range(1, KD)]
    if not last:
        seq += next_tick(2 * NT) + [("job", 2), ("late", 0)] + next_tick(2 * NT + 1) + [("job", 3), ("late", 1)]
    return seq


def values_at(n):
    if n < 3:
        return None
    h, r = divmod(n - 3, NT)
    g, part = divmod(r, 2)
    return (h * GROUPS + g, part) if h < H else None


def output_at(n):
    if n < 5 or n >= 5 + 2 * H * GROUPS:
        return None
    return divmod(n - 5, 2)


DRAIN = 5 + 2 * H * GROUPS


def job_list(h):
    jobs = [(kind, c) for c in range(3) for kind in "kq"]
    return jobs + ([("v", t) for t in range(NT)] if h == 0 else [])


def jobs_before(h):
    return len(job_list(h)) if h else JOBS_FIRST


def job_start(h):
    return 6 * h + (NT if h else 0)


def transformer(nc, io, keep):
    ctx = ExitStack()
    with ctx:
        def sb(name, shape, dt):
            return ctx.enter_context(nc.sbuf_tensor(name, shape, dt))

        def ps(name, n):
            return ctx.enter_context(nc.psum_tensor(name, [P, n], F32))

        def sem(name):
            return ctx.enter_context(nc.semaphore(name))

        x, edges, cond, ident, mhalf = keep.x, keep.edges, keep.cond, keep.ident, keep.mhalf

        w_q, w_k, w_v, w_o, w_2 = (sb(n, [P, 2, KD, D], F16) for n in ("w_q", "w_k", "w_v", "w_o", "w_2"))
        w_1 = w_v
        stage = sb("wstage", [P, 2 * D], F32)
        wc1 = sb("wc1", [P, 2, D], F16)
        wc2 = sb("wc2", [P, 2, D], F16)
        bv = sb("bv", [64, D], F16)
        ones = sb("ones", [64, P], F16)
        brow = sb("brow", [P, D], F32)
        bcols = sb("bcols", [P, B, 3 * KD], F32)
        bcol = sb("bcol", [P, 3 * KD], F32)
        yT = sb("yT", [P, 2, KD, N], F16)
        v = sb("v", [P, 2, NT, D], F16)
        qk = sb("qk", [P, 2, 2, N], F16)
        pr = sb("pr", [P, 2, NPAD], F32)
        pT = sb("pT", [P, 2, 2, NT * WIDTH], F16)
        oT = sb("oT", [P, 2, WIDTH], F16)
        small = sb("small", [P, 8, 4], F32)
        bn = sb("bn_b", [P, NT, 6], F32)
        mv = sb("mv_b", [P, NT, 2], F32)
        rstd = sb("rstd_b", [P, NT, 4], F32)
        xn = [pr[:, i, 0:D] for i in range(2)]
        yn = [pr[:, i, D:2 * D] for i in range(2)]
        pTv = [pT[:, :, i, :].rearrange("p a (t c) -> p a t c", t=NT) for i in range(2)]
        wide = pT[:].rearrange("p a b c -> p (a b c)").bitcast(F32)
        first_raw = [v[:].rearrange("p a b c -> p (a b c)").bitcast(F32)[:, j * 2 * D:(j + 1) * 2 * D] for j in range(4)]
        late_raw = [wide[:, j * 2 * D:(j + 1) * 2 * D] for j in range(len(LATE))]
        x_in = wide.rearrange("p (t d) -> p t d", t=NT)
        hid = qk[:].rearrange("p a b c -> p (a b c)").bitcast(F32)[:, 0:2 * 512].rearrange("p (a c) -> p a c", a=2)

        psA, psB, ps6, ps7 = ps("psA", 3 * 512), ps("psB", 3 * 512), ps("ps6", 512), ps("ps7", 512)
        norm_bank = [psA[:, 0:512], psA[:, 512:1024]]
        turn_bank = [psA[:, 1024:1536], psB[:, 0:512]]
        up_bank = [psB[:, 512:1024], psB[:, 1024:1536]]
        down_bank = [ps6[:], ps7[:]]

        setup = sem("setup")
        stage_in, stage_scaled, stage_hi, stage_lo = (sem(n) for n in ("stage_in", "stage_scaled", "stage_hi", "stage_lo"))
        late_in, late_hi, late_lo = (sem(n) for n in ("late_in", "late_hi", "late_lo"))
        brow_in, bcols_in, bcols_scaled, bcol_set = (sem(n) for n in ("brow_in", "bcols_in", "bcols_scaled", "bcol_set"))
        x_saved, x_back, stored = sem("x_saved"), sem("x_back"), sem("stored")
        bn_done, stats_done, rstd_done, xn_done, scale_done, yn_done, turned, yT_hi, yT_lo = (
            sem(n) for n in ("bn_done", "stats_done", "rstd_done", "xn_done", "scale_done", "yn_done", "turned",
                             "yT_hi", "yT_lo"))
        job_done, job_hi, job_lo = sem("job_done"), sem("job_hi"), sem("job_lo")
        scores_done, masked, exp_done, inv_done, out_scaled = (
            sem(n) for n in ("scores_done", "masked", "exp_done", "inv_done", "out_scaled"))
        pT_done, pT_hi, pT_lo = sem("pT_done"), sem("pT_hi"), sem("pT_lo")
        values_done, oT_hi, oT_lo, out_done, out_added, bo_added = (
            sem(n) for n in ("values_done", "oT_hi", "oT_lo", "out_done", "out_added", "bo_added"))
        up_done, relu_done, hid_hi, hid_lo, down_done, down_added, b2_added = (
            sem(n) for n in ("up_done", "relu_done", "hid_hi", "hid_lo", "down_done", "down_added", "b2_added"))
        final_sum, final_bn, final_stats, final_rstd, final_done = (
            sem(n) for n in ("final_sum", "final_bn", "final_stats", "final_rstd", "final_done"))
        pool_step = sem("pool_step")

        def halves_of(name):
            if name in ("cond1", "cond2"):
                w = (wc1 if name == "cond1" else wc2)[:].rearrange("p a d -> p (a d)")
                return stage[:], w, stage[64:P, :], w[64:P, :], w[64:P, :]
            if name == "bv":
                return stage[0:64, 0:D], bv[:], stage[32:64, 0:D], bv[32:64, :], bv[32:64, :]
            w = {"q": w_q, "k": w_k, "m1": w_1, "m2": w_2}[name[:-1]]
            c = 2 * int(name[-1])
            raw = stage[:].rearrange("p (k d) -> p k d", k=2)
            return raw, w[:, 0, c:c + 2, :], raw, w[:, 0, c:c + 2, :], w[:, 1, c:c + 2, :]

        def first_halves(i):
            raw, high, low_of, high_of, low = halves_of(LOADS_FIRST[i])
            if 1 <= i <= 4:
                raw = low_of = first_raw[i - 1].rearrange("p (k d) -> p k d", k=2)
            return raw, high, low_of, high_of, low

        def scale_of(name):
            return 1.0 if name[0:2] in ("co", "bv") else WS

        def late_halves(j):
            w = w_v if j < 2 else w_o
            c = 2 * (j % 2)
            return late_raw[j].rearrange("p (k d) -> p k d", k=2), w[:, 0, c:c + 2, :], w[:, 1, c:c + 2, :]

        def loads_before(b):
            return b * LOADS + len(LOADS_FIRST)

        def norms_before(b):
            return b * (2 * NT) + NT

        block = ctx.enter_context(nc.Block())

        @block.sync
        def _(sp):
            def load(name, b, seq):
                if not isinstance(seq, int) or seq > 0:
                    sp.wait_ge(stage_lo, seq)
                if name in ("cond1", "cond2"):
                    w = (io["w_cond1"] if name == "cond1" else io["w_cond2"])[bass.ds(b, 1)].rearrange("b r n -> (b r) n")
                    for q in range(4):
                        sp.dma_start(stage[32 * q:32 * q + CE + 1, :], w).then_inc(stage_in, 16)
                elif name == "bv":
                    for q in range(4):
                        r, c = 32 * (q % 2), (q // 2) * 256
                        sp.dma_start(stage[r:r + 1, c:c + 256], io["bv"][bass.ds(b, 1), c:c + 256]).then_inc(stage_in, 16)
                else:
                    w = {"q": io["wq"], "k": io["wk"], "m1": io["m_w1"], "m2": io["m_w2"]}[name[:-1]]
                    src = w[bass.ds(b, 1)].rearrange("b (k p) d -> p (b k) d", p=P)
                    for q in range(4):
                        k, c = 2 * int(name[-1]) + q // 2, (q % 2) * 256
                        sp.dma_start(stage[:, q * 256:(q + 1) * 256].unsqueeze(1), src[:, k:k + 1, c:c + 256]).then_inc(stage_in, 16)

            def load_late(b):
                for j in range(len(LATE)):
                    src = (io["wv"] if j < 2 else io["wo"])[bass.ds(b, 1)].rearrange("b (k p) d -> p (b k) d", p=P)
                    for q in range(4):
                        k, c = 2 * (j % 2) + q // 2, (q % 2) * 256
                        sp.dma_start(late_raw[j][:, q * 256:(q + 1) * 256].unsqueeze(1), src[:, k:k + 1, c:c + 256]).then_inc(late_in, 16)

            def load_row(w, b):
                sp.dma_start(brow[:], w[bass.ds(b, 1), :].rearrange("b d -> (b d)").partition_broadcast(P)).then_inc(brow_in, 16)

            sp.dma_start(bcols[:], io["bias_cols"].rearrange("b p j -> p b j")).then_inc(bcols_in, 16)
            sp.wait_ge(pool_step, 1)
            load(LOADS_FIRST[0], 0, 0)
            sp.wait_ge(stage_in, 64)
            for i, w in enumerate((io["wq"], io["wk"])):
                for q in range(8):
                    k, c = q // 2, (q % 2) * 256
                    sp.dma_start(first_raw[2 * i + k // 2][:, (q % 4) * 256:(q % 4 + 1) * 256],
                                 w[0, k * P:(k + 1) * P, c:c + 256]).then_inc(stage_in, 16)
            load_row(io["bo"], 0)
            load_late(0)
            sp.wait_ge(stage_in, 5 * 64)
            load(LOADS_FIRST[5], 0, 1)
            sp.dma_start(io["x_scratch"].rearrange("(t p) d -> p t d", p=P), x[:]).then_inc(x_saved, 16)

            def body(b, last):
                sp.wait_ge(bo_added, (b + 1) * NT)
                load_row(io["b2"], b)
                names = block_loads(last)
                for i, name in enumerate(names):
                    load(name, b if name in LOADS_STEP.values() else b + 1, loads_before(b) + i)
                if not last:
                    sp.wait_ge(values_done, (b + 1) * H * GROUPS)
                    load_late(b + 1)
                    sp.wait_ge(b2_added, (b + 1) * NT)
                    load_row(io["bo"], b + 1)

            with sp.Fori(0, B - 1) as b:
                body(b, False)
            body(B - 1, True)
            sp.wait_ge(values_done, B * H * GROUPS)
            sp.wait_ge(x_saved, 16)
            sp.dma_start(x_in, io["x_scratch"].rearrange("(t p) d -> p t d", p=P)).then_inc(x_back, 16)
            for t in range(NT):
                sp.wait_ge(final_done, t + 1)
                sp.dma_start(io["out"][t * P:t * P + rows(t), :], x_in[0:rows(t), t, :]).then_inc(stored, 16)
            sp.wait_ge(stored, 16 * NT)

        @block.gpsimd
        def _(pool):
            pool.memset(rstd[:], 0.0).then_inc(setup, 1)
            pool.memset(stage[:], 0.0).then_inc(pool_step, 1)
            pool.memset(ones[:], 0.0).then_inc(pool_step, 1)
            pool.memset(pr[:, :, N:NPAD], 0.0).then_inc(pool_step, 1)
            pool.memset(small[:], 0.0).then_inc(pool_step, 1)
            pool.wait_ge(pool_step, 4)
            pool.memset(ones[0:1, :], WS).then_inc(pool_step, 1)
            pool.memset(ones[32:33, :], WS).then_inc(pool_step, 1)
            pool.wait_ge(pool_step, 6)

            def split(name, seq):
                raw, _, low_of, high, low = halves_of(name)
                count = in_register(pool, seq * 64 + 64)
                pool.wait_ge(pool_step, 6)
                pool.wait_ge(stage_in, count)
                pool.tensor_scalar(raw, raw, scale_of(name), None, ALU.mult).then_inc(stage_scaled, 1)
                pool.wait_ge(stage_hi, seq + 1)
                pool.tensor_tensor(low, low_of, high, ALU.subtract).then_inc(stage_lo, 1)
                pool.wait_ge(stage_lo, seq + 1)

            def inverse(i, before, aggregated, count, done):
                count = in_register(pool, count)
                pool.wait_ge(pool_step, 6)
                pool.wait_ge(aggregated, count)
                pool.tensor_scalar(rstd[:, i, 0:1], mv[:, i, 1:2], EPS, None, ALU.add).then_inc(pool_step, 1)
                pool.wait_ge(pool_step, before * 2 + 7)
                pool.tensor_tensor(rstd[:, i, 1:2], rstd[:, i, 0:1], mhalf[:, 0:1], ALU.pow).then_inc(pool_step, 1)
                count = in_register(pool, before * 2 + 8)
                pool.wait_ge(pool_step, 6)
                pool.wait_ge(pool_step, count)
                pool.tensor_scalar(rstd[:, i, 2:3], mv[:, i, 0:1], rstd[:, i, 1:2], -1.0, ALU.mult, ALU.mult).then_inc(done, 1)

            for k in range(NT):
                inverse(k, k, stats_done, k + 1, rstd_done)
            pool.wait_ge(x_saved, 16)

            def body(b, last):
                pool.wait_ge(xn_done, norms_before(b))
                pool.wait_ge(brow_in, b * 32 + 16)
                for t in range(NT):
                    pool.tensor_tensor(x[:, t, :], x[:, t, :], brow[:], ALU.add).then_inc(bo_added, 1)
                names = block_loads(last)
                ready = 0 if last else 2
                for j in range(len(names)):
                    if j == len(names) - 1:
                        for k in range(ready):
                            inverse(k, norms_before(b) + k, stats_done, norms_before(b) + k + 1, rstd_done)
                    split(names[j], loads_before(b) + j)
                pool.wait_ge(brow_in, b * 32 + 32)
                for k in range(ready, NT):
                    inverse(k, norms_before(b) + k, stats_done, norms_before(b) + k + 1, rstd_done)
                for kind, k in early_ticks() + mlp_sequence(last):
                    if kind == "stats":
                        inverse(k % NT, norms_before(b) + k, stats_done, norms_before(b) + k + 1, rstd_done)
                    elif kind == "turn" and k < NT:
                        pool.wait_ge(xn_done, norms_before(b) + k + 1)
                        pool.tensor_tensor(x[:, k, :], x[:, k, :], brow[:], ALU.add).then_inc(b2_added, 1)
                    elif kind == "final":
                        inverse(k, norms_before(b) + NT + k, final_stats, k + 1, final_rstd)

            with pool.Fori(0, B - 1) as b:
                body(b, False)
            body(B - 1, True)

        @block.scalar
        def _(act):
            def split(name, seq):
                raw, high = halves_of(name)[0:2]
                act.wait_ge(stage_scaled, seq + 1 - len(LOADS_FIRST))
                act.activation(high, raw, ACT.Copy).then_inc(stage_hi, 1)

            def norm(i, before):
                t = i % NT
                act.wait_ge(rstd_done, before + i + 1)
                act.activation(xn[i % 2], x[:, t, :], ACT.Identity, bias=rstd[:, t, 2:3],
                               scale=rstd[:, t, 1:2]).then_inc(xn_done, 1)

            def turn(i, before):
                t = i % NT
                r = rows(t)
                act.wait_ge(turned, before + i + 1)
                act.activation(yT[:, 0, :, t * P:t * P + r],
                               turn_bank[i % 2].rearrange("p (k c) -> p k c", k=KD)[:, :, 0:r], ACT.Copy).then_inc(yT_hi, 1)

            def job(b, h, i, slot):
                kind, c = job_list(h)[i]
                act.wait_ge(bcol_set, b + 1)
                act.wait_ge(job_done, b * JOBS + job_start(h) + i + 1)
                if kind == "v":
                    r = rows(c)
                    act.activation(v[0:r, 0, c, :], slot[0:r, :], ACT.Copy).then_inc(job_hi, 1)
                else:
                    which = int(kind == "k")
                    lo, hi = COLS[c]
                    act.activation(qk[:, which, 0, lo:hi], slot[:, 0:hi - lo], ACT.Identity,
                                   bias=bcol[:, which * KD + h:which * KD + h + 1]).then_inc(job_hi, 1)

            def late_high(j, b):
                raw, high, _ = late_halves(j)
                act.wait_ge(late_in, (b + 1) * (len(LATE) * 64))
                act.activation(high, raw, ACT.Copy, scale=WS).then_inc(late_hi, 1)

            for kind, k in first_sequence():
                if kind == "load":
                    raw, high = first_halves(k)[0:2]
                    act.wait_ge(stage_in, 64 * (5 if 1 <= k <= 4 else k + 1))
                    act.activation(high, raw, ACT.Copy, scale=scale_of(LOADS_FIRST[k])).then_inc(stage_hi, 1)
                elif kind == "norm":
                    norm(k, 0)
                elif kind == "turn":
                    turn(k, 0)
                elif kind == "job":
                    job(0, 0, k, up_bank[k % 2])
                elif kind == "late":
                    late_high(k, 0)

            def project(b, h):
                for i in range(0 if h else JOBS_EARLY, jobs_before(h)):
                    job(b, h, i, psA[:, (i % 3) * 512:(i % 3 + 1) * 512])
                    if h == 0 and i < JOBS_EARLY + 2:
                        late_high(i - JOBS_EARLY + 2, b)

            def exponential(b, n):
                r = rows(n % NT)
                act.wait_ge(masked, b * STEPS + n + 1)
                act.activation(pr[0:r, n % 2, 0:N], pr[0:r, n % 2, 0:N], ACT.Exp, bias=small[0:r, n % 8, 0:1], scale=-1.0,
                               accum_out=small[0:r, n % 8, 1:2]).then_inc(exp_done, 1)

            def transposed(b, n):
                s = n % NT
                G, r = n // 2, rows(s)
                if G >= 2:
                    act.wait_ge(values_done, b * H * GROUPS + G - 1)
                act.wait_ge(pT_done, b * STEPS + n + 1)
                act.activation(pTv[G % 2][:, 0, :, (s % 2) * P:(s % 2) * P + r],
                               psB[:, 0:NPAD].rearrange("p (t c) -> p t c", c=P)[:, :, 0:r], ACT.Copy).then_inc(pT_hi, 1)

            def values(b, n):
                G, part = values_at(n) or (0, 0)
                if part:
                    w = sum(rows(2 * (G % GROUPS) + i) for i in range(2))
                    if G:
                        act.wait_ge(out_done, b * STEPS + 2 * G)
                    act.wait_ge(values_done, b * H * GROUPS + G + 1)
                    act.activation(oT[:, 0, 0:w], ps6[:, 0:w], ACT.Copy, scale=1.0 / (WS * OS)).then_inc(oT_hi, 1)

            def body(b, last):
                names = block_loads(last)
                steps = LOADS_STEP if last else {**LOADS_STEP, **LOADS_NEXT}
                i = 0
                for n in range(DRAIN):
                    boundary = n % NT == 0 and n < STEPS
                    if boundary:
                        project(b, n // NT)
                    if 1 <= n <= STEPS:
                        transposed(b, n - 1)
                    if n < STEPS:
                        exponential(b, n)
                    if n < JOBS_HELD:
                        job(b, 0, JOBS_FIRST + n, down_bank[n])
                    values(b, n)
                    if n in steps:
                        split(names[i], loads_before(b) + i)
                        i += 1
                    if n >= DRAIN - TICKS_EARLY:
                        second_half(b, mlp_tick(n - (DRAIN - TICKS_EARLY)))
                second_half(b, mlp_sequence(last))

            def second_half(b, items):
                for kind, k in items:
                    if kind == "norm":
                        norm(k, norms_before(b))
                    elif kind == "turn":
                        turn(k, norms_before(b))
                    elif kind == "up":
                        c, j = divmod(k, KD)
                        w = COLS[c][1] - COLS[c][0]
                        if c == 2:
                            act.wait_ge(down_done, b * NT + 4)
                        if k >= 2:
                            act.wait_ge(hid_lo, b * 3 * KD + k - 1)
                        act.wait_ge(up_done, b * 3 * KD + k + 1)
                        act.activation(hid[:, k % 2, 0:w], up_bank[k % 2][:, 0:w], ACT.Relu,
                                       bias=bcol[:, 2 * KD + j:2 * KD + j + 1]).then_inc(relu_done, 1)
                        act.wait_ge(relu_done, b * 3 * KD + k + 1)
                        act.activation(v[:, 0, (c % 2) * KD + j, 0:w], hid[:, k % 2, 0:w], ACT.Copy).then_inc(hid_hi, 1)
                    elif kind == "job":
                        act.wait_ge(hid_lo, (b + 1) * (3 * KD))
                        job(b + 1, 0, k, up_bank[k % 2])
                    elif kind == "late":
                        late_high(k, b + 1)
                    elif kind == "final":
                        act.wait_ge(final_rstd, k + 1)
                        act.activation(x_in[:, k, :], x[:, k, :], ACT.Identity, bias=rstd[:, k, 2:3],
                                       scale=rstd[:, k, 1:2]).then_inc(final_done, 1)

            with act.Fori(0, B - 1) as b:
                body(b, False)
            body(B - 1, True)

        @block.vector
        def _(dve):
            def stats(i, before):
                dve.bn_stats(bn[:, i % NT, :], x[:, i % NT, :]).then_inc(bn_done, 1)
                count = in_register(dve, before + i + 1)
                dve.wait_ge(setup, 1)
                dve.wait_ge(bn_done, count)
                dve.bn_aggr(mv[:, i % NT, :], bn[:, i % NT, :]).then_inc(stats_done, 1)

            def norm(i, before):
                dve.wait_ge(xn_done, before + i + 1)
                dve.wait_ge(scale_done, before + i + 1)
                dve.scalar_tensor_tensor(yn[i % 2], norm_bank[i % 2], 1.0, xn[i % 2], ALU.add, ALU.mult).then_inc(yn_done, 1)

            def turn(i, before):
                t = i % NT
                r = rows(t)
                dve.wait_ge(yT_hi, before + i + 1)
                dve.tensor_tensor(yT[:, 1, :, t * P:t * P + r], turn_bank[i % 2].rearrange("p (k c) -> p k c", k=KD)[:, :, 0:r],
                                  yT[:, 0, :, t * P:t * P + r], ALU.subtract).then_inc(yT_lo, 1)

            dve.wait_ge(setup, 1)
            def job(b, h, i, slot):
                kind, c = job_list(h)[i]
                dve.wait_ge(job_hi, b * JOBS + job_start(h) + i + 1)
                if kind == "v":
                    r = rows(c)
                    dve.tensor_tensor(v[0:r, 1, c, :], slot[0:r, :], v[0:r, 0, c, :], ALU.subtract).then_inc(job_lo, 1)
                else:
                    which = int(kind == "k")
                    lo, hi = COLS[c]
                    dve.scalar_tensor_tensor(qk[:, which, 1, lo:hi], slot[:, 0:hi - lo],
                                             bcol[:, which * KD + h:which * KD + h + 1], qk[:, which, 0, lo:hi],
                                             ALU.add, ALU.subtract).then_inc(job_lo, 1)

            def late_low(j, b):
                raw, high, low = late_halves(j)
                dve.wait_ge(late_hi, b * len(LATE) + (j + 1))
                dve.scalar_tensor_tensor(low, raw, WS, high, ALU.mult, ALU.subtract).then_inc(late_lo, 1)

            for kind, k in first_sequence():
                if kind == "load":
                    _, _, raw, high, low = first_halves(k)
                    dve.wait_ge(stage_hi, k + 1)
                    dve.scalar_tensor_tensor(low, raw, scale_of(LOADS_FIRST[k]), high, ALU.mult,
                                             ALU.subtract).then_inc(stage_lo, 1)
                elif kind == "stats":
                    stats(k, 0)
                elif kind == "norm":
                    norm(k, 0)
                elif kind == "turn":
                    turn(k, 0)
                elif kind == "job":
                    if k == 0:
                        dve.wait_ge(bcols_in, 16)
                        dve.tensor_scalar(bcols[:], bcols[:], WS, None, ALU.mult).then_inc(bcols_scaled, 1)
                        dve.wait_ge(bcols_scaled, 1)
                        dve.tensor_copy(bcol[:], bcols[:, 0, :]).then_inc(bcol_set, 1)
                    job(0, 0, k, up_bank[k % 2])
                elif kind == "late":
                    late_low(k, 0)

            def project(b, h):
                for i in range(0 if h else JOBS_EARLY, jobs_before(h)):
                    job(b, h, i, psA[:, (i % 3) * 512:(i % 3 + 1) * 512])
                    if h == 0 and i < JOBS_EARLY + 2:
                        late_low(i - JOBS_EARLY + 2, b)

            def mask(b, n):
                s = n % NT
                r = rows(s)
                count = in_register(dve, b * STEPS + n + 1)
                dve.wait_ge(setup, 1)
                dve.wait_ge(scores_done, count)
                dve.tensor_tensor_reduce(out=pr[0:r, n % 2, 0:N], in0=psA[0:r, 0:N], in1=edges[0:r, s, :],
                                         scale=-1.0 / KAPPA, scalar=3e38, op0=ALU.add, op1=ALU.min,
                                         accum_out=small[0:r, n % 8, 0:1]).then_inc(masked, 1)

            def inverse(b, n):
                m = small[0:rows(n % NT), n % 8, :]
                dve.wait_ge(exp_done, b * STEPS + n + 1)
                dve.reciprocal(m[:, 2:3], m[:, 1:2])
                dve.tensor_scalar(m[:, 3:4], m[:, 0:1], -NOEDGE / KAPPA / 8, OS / WS, ALU.is_lt, ALU.mult).then_inc(inv_done, 1)

            def scale(b, n):
                m = small[0:rows(n % NT), n % 8, :]
                dve.wait_ge(inv_done, b * STEPS + n + 1)
                dve.tensor_tensor(m[:, 3:4], m[:, 3:4], m[:, 2:3], ALU.mult).then_inc(out_scaled, 1)

            def transposed(b, n):
                s = n % NT
                G, r = n // 2, rows(s)
                out = pTv[G % 2][:, :, :, (s % 2) * P:(s % 2) * P + r]
                dve.wait_ge(pT_hi, b * STEPS + n + 1)
                dve.tensor_tensor(out[:, 1], psB[:, 0:NPAD].rearrange("p (t c) -> p t c", c=P)[:, :, 0:r], out[:, 0],
                                  ALU.subtract).then_inc(pT_lo, 1)

            def values(b, n):
                G, part = values_at(n) or (0, 0)
                if part:
                    w = sum(rows(2 * (G % GROUPS) + i) for i in range(2))
                    dve.wait_ge(oT_hi, b * H * GROUPS + G + 1)
                    dve.scalar_tensor_tensor(oT[:, 1, 0:w], ps6[:, 0:w], 1.0 / (WS * OS), oT[:, 0, 0:w], ALU.mult, ALU.subtract).then_inc(oT_lo, 1)

            def output(b, n):
                if output_at(n) is None:
                    return
                G, i = output_at(n)
                t = 2 * (G % GROUPS) + i
                r = rows(t)
                if G < GROUPS:
                    dve.wait_ge(bo_added, b * NT + t + 1)
                dve.wait_ge(out_scaled, b * STEPS + 2 * G + i + 1)
                dve.wait_ge(out_done, b * STEPS + 2 * G + i + 1)
                dve.scalar_tensor_tensor(x[0:r, t, :], ps7[0:r, :], small[0:r, (2 * G + i) % 8, 3:4], x[0:r, t, :], ALU.mult,
                                         ALU.add).then_inc(out_added, 1)

            def body(b, last):
                for n in range(DRAIN):
                    boundary = n % NT == 0 and n < STEPS
                    if boundary:
                        project(b, n // NT)
                    elif n < STEPS:
                        mask(b, n)
                    if 2 <= n < STEPS + 2:
                        scale(b, n - 2)
                    if 1 <= n <= STEPS:
                        transposed(b, n - 1)
                        inverse(b, n - 1)
                    if boundary:
                        mask(b, n)
                    if n < JOBS_HELD:
                        job(b, 0, JOBS_FIRST + n, down_bank[n])
                    values(b, n)
                    output(b, n)
                    if n >= DRAIN - NT:
                        dve.wait_ge(out_added, b * STEPS + n - (DRAIN - STEPS) + 1)
                        stats(n - (DRAIN - NT), norms_before(b))
                    if n >= DRAIN - TICKS_EARLY:
                        second_half(b, mlp_tick(n - (DRAIN - TICKS_EARLY)))
                second_half(b, mlp_sequence(last))

            def second_half(b, items):
                for kind, k in items:
                    t = k % NT
                    if kind == "stats":
                        dve.wait_ge(down_added, b * NT + t + 1)
                        stats(k, norms_before(b))
                    elif kind == "norm":
                        norm(k, norms_before(b))
                    elif kind == "turn":
                        turn(k, norms_before(b))
                    elif kind == "up":
                        c, j = divmod(k, KD)
                        w = COLS[c][1] - COLS[c][0]
                        dve.wait_ge(hid_hi, b * 3 * KD + k + 1)
                        slot = (c % 2) * KD + j
                        dve.tensor_tensor(v[:, 1, slot, 0:w], hid[:, k % 2, 0:w], v[:, 0, slot, 0:w],
                                          ALU.subtract).then_inc(hid_lo, 1)
                    elif kind == "job":
                        if k == 0:
                            count = in_register(dve, (b + 1) * (3 * KD))
                            dve.wait_ge(bcols_scaled, 1)
                            dve.wait_ge(relu_done, count)
                            dve.tensor_copy(bcol[:].unsqueeze(1), bcols[:, bass.ds(b + 1, 1), :]).then_inc(bcol_set, 1)
                        job(b + 1, 0, k, up_bank[k % 2])
                    elif kind == "late":
                        late_low(k, b + 1)
                    elif kind == "down":
                        r = rows(t)
                        dve.wait_ge(b2_added, b * NT + t + 1)
                        dve.wait_ge(down_done, b * NT + t + 1)
                        dve.scalar_tensor_tensor(x[0:r, t, :], down_bank[t % 2][0:r, :], 1.0 / (WS * WS), x[0:r, t, :],
                                                 ALU.mult, ALU.add).then_inc(down_added, 1)
                    elif kind == "final":
                        if t == 0:
                            dve.wait_ge(x_back, 16)
                        dve.wait_ge(down_added, b * NT + t + 1)
                        dve.tensor_tensor(x[:, t, :], x[:, t, :], x_in[:, t, :], ALU.add).then_inc(final_sum, 1)
                        dve.wait_ge(final_sum, t + 1)
                        dve.bn_stats(bn[:, t, :], x[:, t, :]).then_inc(final_bn, 1)
                        dve.wait_ge(final_bn, t + 1)
                        dve.bn_aggr(mv[:, t, :], bn[:, t, :]).then_inc(final_stats, 1)

            with dve.Fori(0, B - 1) as b:
                body(b, False)
            body(B - 1, True)

        @block.tensor
        def _(pe):
            def norm(i, before, wc, wait=None):
                t = i % NT
                pe.matmul(norm_bank[i % 2], cond[:, t * P:(t + 1) * P], wc[:, 0, :], start=True, stop=True).then_inc(scale_done, 1)

            def turn(i, before, wc):
                t = i % NT
                r = rows(t)
                if not isinstance(before, int) or before + i >= 2:
                    pe.wait_ge(yT_lo, before + i - 1)
                pe.wait_ge(yn_done, before + i + 1)
                for k in range(KD):
                    out = turn_bank[i % 2][:, k * P:k * P + r]
                    pe.matmul(out, wc[:, 1, k * P:(k + 1) * P], cond[:, t * P:t * P + r], start=True, stop=False)
                    last = pe.matmul(out, yn[i % 2][0:r, k * P:(k + 1) * P], ident[0:r, 0:r], start=False, stop=True,
                                     is_transpose=True)
                last.then_inc(turned, 1)

            pe.wait_ge(stage_lo, 1)
            def job(b, h, i, slot):
                kind, c = job_list(h)[i]
                if kind == "v":
                    if c == 0:
                        pe.wait_ge(late_lo, b * len(LATE) + 2)
                    r = rows(c)
                    pe.matmul(slot[0:r, :], ones[:, 0:r], bv[:], start=True, stop=False)
                    last = split_matmuls(pe, slot[0:r, :],
                                         [(yT[:, 0, k, c * P:c * P + r], yT[:, 1, k, c * P:c * P + r]) for k in range(KD)],
                                         [(w_v[:, 0, k, :], w_v[:, 1, k, :]) for k in range(KD)], start=False)
                else:
                    w = w_k if kind == "k" else w_q
                    lo, hi = COLS[c]
                    last = split_matmuls(pe, slot[:, 0:hi - lo],
                                         [(w[:, 0, k, h * P:(h + 1) * P], w[:, 1, k, h * P:(h + 1) * P]) for k in range(KD)],
                                         [(yT[:, 0, k, lo:hi], yT[:, 1, k, lo:hi]) for k in range(KD)])
                last.then_inc(job_done, 1)

            def early_job(b, k):
                if k == 0:
                    pe.wait_ge(stage_lo, loads_before(b))
                if k >= 2:
                    pe.wait_ge(job_lo, b * JOBS + k - 1)
                c = job_list(0)[k][1]
                pe.wait_ge(yT_lo, norms_before(b) - NT + 4 * (c + 1))
                job(b, 0, k, up_bank[k % 2])

            for kind, k in first_sequence():
                if kind == "norm":
                    norm(k, 0, wc1)
                elif kind == "turn":
                    turn(k, 0, wc1)
                elif kind == "job":
                    early_job(0, k)

            def project(b, h):
                if h:
                    pe.wait_ge(masked, b * STEPS + h * NT)
                else:
                    pe.wait_ge(yT_lo, norms_before(b))
                start = 0 if h else JOBS_EARLY
                for i in range(start, jobs_before(h)):
                    if i >= start + 3:
                        pe.wait_ge(job_lo, b * JOBS + job_start(h) + i - 2)
                    job(b, h, i, psA[:, (i % 3) * 512:(i % 3 + 1) * 512])

            def scores(b, n):
                s = n % NT
                r = rows(s)
                if s == 0:
                    pe.wait_ge(job_lo, b * JOBS + job_start(n // NT) + jobs_before(n // NT))
                else:
                    pe.wait_ge(masked, b * STEPS + n)
                for part, (i, j) in enumerate(((0, 0), (0, 1), (1, 0))):
                    for lo, hi in COLS:
                        last = pe.matmul(psA[0:r, lo:hi], qk[:, 0, i, s * P:s * P + r], qk[:, 1, j, lo:hi],
                                         start=part == 0, stop=part == 2)
                last.then_inc(scores_done, 1)

            def values(b, n):
                if values_at(n) is None:
                    return
                G, part = values_at(n)
                h, g = divmod(G, GROUPS)
                w = sum(rows(2 * g + i) for i in range(2))
                if part == 0:
                    if G:
                        pe.wait_ge(oT_lo, b * H * GROUPS + G)
                    else:
                        pe.wait_ge(job_lo, b * JOBS + job_start(1))
                    pe.wait_ge(pT_lo, b * STEPS + 2 * G + 2)
                half = NT // 2
                tiles = range(part * half, part * half + half)
                last = split_matmuls(pe, ps6[:, 0:w],
                                     [(v[0:rows(d), 0, d, h * P:(h + 1) * P], v[0:rows(d), 1, d, h * P:(h + 1) * P]) for d in tiles],
                                     [(pTv[G % 2][0:rows(d), 0, d, 0:w], pTv[G % 2][0:rows(d), 1, d, 0:w]) for d in tiles],
                                     start=part == 0, stop=part == 1)
                if part:
                    last.then_inc(values_done, 1)

            def transpose(b, n):
                r = rows(n % NT)
                if n:
                    pe.wait_ge(pT_lo, b * STEPS + n)
                pe.wait_ge(exp_done, b * STEPS + n + 1)
                for d in range(NT):
                    last = pe.transpose(psB[:, d * P:d * P + r], pr[0:r, n % 2, d * P:(d + 1) * P], ident[0:r, 0:r])
                last.then_inc(pT_done, 1)

            def output(b, n):
                if output_at(n) is None:
                    return
                G, i = output_at(n)
                h, g = divmod(G, GROUPS)
                r = rows(2 * g + i)
                if n > 5:
                    pe.wait_ge(out_added, b * STEPS + 2 * G + i)
                if n == 5:
                    pe.wait_ge(late_lo, (b + 1) * len(LATE))
                if i == 0:
                    pe.wait_ge(oT_lo, b * H * GROUPS + G + 1)
                split_matmuls(pe, ps7[0:r, :], [(oT[:, 0, i * P:i * P + r], oT[:, 1, i * P:i * P + r])],
                              [(w_o[:, 0, h, :], w_o[:, 1, h, :])]).then_inc(out_done, 1)

            def body(b, last):
                names = block_loads(last)
                for n in range(DRAIN):
                    boundary = n % NT == 0 and n < STEPS
                    if boundary:
                        project(b, n // NT)
                    elif n < STEPS:
                        scores(b, n)
                    if n == STEPS:
                        values(b, n)
                    if 1 <= n <= STEPS:
                        transpose(b, n - 1)
                    if boundary:
                        scores(b, n)
                    if n < JOBS_HELD:
                        job(b, 0, JOBS_FIRST + n, down_bank[n])
                    if n != STEPS:
                        values(b, n)
                    output(b, n)
                    if n >= DRAIN - TICKS_EARLY:
                        if n == DRAIN - TICKS_EARLY:
                            pe.wait_ge(stage_lo, loads_before(b) + names.index("cond2") + 1)
                        second_half(b, mlp_tick(n - (DRAIN - TICKS_EARLY)), last)
                second_half(b, mlp_sequence(last), last)

            def second_half(b, items, last):
                names = block_loads(last)
                for kind, k in items:
                    wc = wc2 if k < NT else wc1
                    if kind == "norm":
                        if k == NT:
                            pe.wait_ge(stage_lo, loads_before(b) + names.index("cond1") + 1)
                        norm(k, norms_before(b), wc)
                    elif kind == "turn":
                        turn(k, norms_before(b), wc)
                    elif kind == "job":
                        early_job(b + 1, k)
                    elif kind == "up":
                        c, j = divmod(k, KD)
                        lo, hi = COLS[c]
                        if j == 0:
                            pe.wait_ge(yT_lo, norms_before(b) + min(4 * c + 4, NT))
                        if k >= 2:
                            pe.wait_ge(relu_done, b * 3 * KD + k - 1)
                        split_matmuls(pe, up_bank[k % 2][:, 0:hi - lo],
                                      [(w_1[:, 0, i, j * P:(j + 1) * P], w_1[:, 1, i, j * P:(j + 1) * P]) for i in range(KD)],
                                      [(yT[:, 0, i, lo:hi], yT[:, 1, i, lo:hi]) for i in range(KD)]).then_inc(up_done, 1)
                    elif kind == "down":
                        c, r = k // KD, rows(k)
                        if k >= 2:
                            pe.wait_ge(down_added, b * NT + k - 1)
                        if k % KD == 0:
                            pe.wait_ge(hid_lo, b * 3 * KD + (c + 1) * KD)
                        at = (k % KD) * P
                        split_matmuls(pe, down_bank[k % 2][0:r, :],
                                      [(v[:, 0, (c % 2) * KD + i, at:at + r], v[:, 1, (c % 2) * KD + i, at:at + r]) for i in range(KD)],
                                      [(w_2[:, 0, i, :], w_2[:, 1, i, :]) for i in range(KD)]).then_inc(down_done, 1)

            with pe.Fori(0, B - 1) as b:
                body(b, False)
            body(B - 1, True)


class Kept:
    pass


def kept(nc, ctx):
    k = Kept()

    def sb(name, shape, dt):
        return ctx.enter_context(nc.sbuf_tensor(name, shape, dt))

    k.x = sb("x", [P, NT, D], F32)
    k.edges = sb("edges", [P, NT, N], F32)
    k.cond = sb("cond", [P, NPAD], F16)
    k.ident = sb("ident", [P, P], F32)
    k.const = sb("const", [P, N_CONST], F32)
    k.mhalf = sb("mhalf", [P, 1], F32)
    return k


def build(nc, io):
    io["x_scratch"] = nc.dram_tensor("x_scratch", (NPAD, D), F32).ap()
    ctx = ExitStack()
    with ctx:
        keep = kept(nc, ctx)
        graph_layer(nc, io, keep)
        transformer(nc, io, keep)


def arrays(inputs):
    import numpy as np
    a = {k: np.ascontiguousarray(v) for k, v in inputs.items()}
    g, b = "L0_gnn_", "L1_gnn_"
    const = np.zeros((P, N_CONST), np.float32)
    const[0:2 * FREQ, C_FREQ] = np.tile(np.arange(1, FREQ + 1) / 16.0, 2)
    const[FREQ:2 * FREQ, C_PHASE] = 0.25
    const[CE::32, C_ONE] = 1.0
    const[:, C_TLO] = P * np.arange(P)
    const[:, C_THI] = P * np.arange(1, P + 1)
    const[0:NT, C_LOWER:C_LOWER + NT] = np.triu(np.ones((NT, NT)), 1)
    t = lambda v: np.ascontiguousarray(v.T)
    cols = lambda v: v.reshape(B, KD, P).transpose(0, 2, 1)

    def norm_weights(n):
        parts = [np.concatenate([a[b + f"{m}{n}_w"], a[b + f"{m}{n}_b"][:, None, :]], axis=1) for m in "sb"]
        return np.ascontiguousarray(np.concatenate(parts, axis=2))

    return {
        "x": a["x"], "xT": t(a["x"]), "src": a["src"], "dst": a["dst"], "noise": a["node_vec1"].reshape(N),
        "w_self_T": t(a[g + "w_self"]), "w_neigh_T": t(a[g + "w_neigh"]),
        "bias": a[g + "bias"], "gamma": a[g + "gamma"], "beta": a[g + "beta"],
        "f_w1": a[b + "f_w1"], "f_b1": a[b + "f_b1"], "f_w2": a[b + "f_w2"], "f_b2": a[b + "f_b2"],
        "const": const, "ident": np.eye(P, dtype=np.float32), "iota": np.arange(N).astype(np.float16),
        "quad_no": (np.arange(NQUAD * SLOTS) // SLOTS).astype(np.float32),
        "w_cond1": norm_weights("1"), "w_cond2": norm_weights("2"),
        "wq": a[b + "wq"], "wk": a[b + "wk"], "wv": a[b + "wv"], "wo": a[b + "wo"],
        "m_w1": a[b + "m_w1"], "m_w2": a[b + "m_w2"],
        "bias_cols": np.ascontiguousarray(np.concatenate([cols(a[b + n]) for n in ("bq", "bk", "m_b1")], axis=2)),
        "bv": a[b + "bv"], "bo": a[b + "bo"], "b2": a[b + "m_b2"],
    }


def kernel(**inputs):
    import numpy as np
    import concourse.bacc as bacc
    from concourse.bass_utils import run_bass_kernel_spmd

    nc = bacc.Bacc("TRN2", target_bir_lowering=False, num_devices=1)
    given = arrays({k: np.asarray(v) for k, v in inputs.items()})
    io = {
        k: nc.dram_tensor(f"in_{k}", v.shape, mybir.dt.from_np(v.dtype), kind="ExternalInput").ap()
        for k, v in given.items()}
    io["out"] = nc.dram_tensor("out", (N, D), F32, kind="ExternalOutput").ap()
    build(nc, io)
    r = run_bass_kernel_spmd(nc, [{f"in_{k}": v for k, v in given.items()}], core_ids=[0])
    return r.results[0]["out"]
```
